# Optimizing a Trainium2 kernel written in Bass

```python
import numpy as np
import jax
import jax.numpy as jnp

def _softmax(x, axis=-1):
    return jax.nn.softmax(x, axis=axis)

def _gelu(x):
    return jax.nn.gelu(x, approximate=True)

def _silu(x):
    return jax.nn.silu(x)

def _sigmoid(x):
    return jax.nn.sigmoid(x)

def _layernorm(x, axis=-1, eps=1e-05):
    m = jnp.mean(x, axis=axis, keepdims=True)
    v = jnp.var(x, axis=axis, keepdims=True)
    return (x - m) / jnp.sqrt(v + eps)

def _scatter_add(tgt, idx, src, axis=0):
    return tgt.at[idx].add(src)

def _segment_sum(src, seg, n):
    return jax.ops.segment_sum(src, seg, n)
kernel_name = 'mk_flamingo_gated_d2_seqx_r4_4570f1'

def setup_inputs(seed: int=0):
    np.random.seed(seed)
    _w = jnp.asarray

    def _rec_inputs():
        import jax
        import jax.numpy as jnp
        _rk = jax.random.key(seed)
        x = -0.0002928 + 1 * jax.random.normal(jax.random.fold_in(_rk, 1), (4, 512, 256), jnp.float32)
        _lenS = 512 - jax.random.randint(jax.random.fold_in(_rk, 7), (4,), 0, max(1, 512 // 4) + 1, jnp.int32)
        _lenS2 = 1024 - jax.random.randint(jax.random.fold_in(_rk, 8), (4,), 0, max(1, 1024 // 4) + 1, jnp.int32)
        _ctx_1024P = jax.random.normal(jax.random.fold_in(_rk, 11), (4, 16, 256), jnp.float32)
        _ctx_1024c = jax.random.dirichlet(jax.random.fold_in(_rk, 511), 0.3 * jnp.ones((16,), jnp.float32), (4, 1024))
        _ctx_1024t = jnp.einsum('bsk,bkd->bsd', _ctx_1024c, _ctx_1024P)
        _ctx_1024t = _ctx_1024t * jax.lax.rsqrt(jnp.mean(jnp.square(_ctx_1024t)) + 1e-12) * 0.953939
        ctx_1024 = -1.39393e-06 + 0.999914 * (_ctx_1024t + 0.3 * jax.random.normal(jax.random.fold_in(_rk, 611), (4, 1024, 256), jnp.float32))
        _validS = jnp.arange(512)[None, :] < _lenS[:, None]
        _validS2 = jnp.arange(1024)[None, :] < _lenS2[:, None]
        _causal = jnp.tril(jnp.ones((512, 512), dtype=bool))
        mask_Bx1xSxS2_ik1 = jnp.where(jnp.broadcast_to(_validS2[:, None, None, :], (4, 1, 512, 1024)), 1, 0).astype(jnp.int32)
        mask_BxS2_bf1 = jnp.ones((4, 1024), dtype=bool)
        _g = jax.random.normal(jax.random.fold_in(_rk, 9001), (2, 2), jnp.float32)
        _g = jnp.sign(_g) * jnp.maximum(jnp.abs(_g), 1.0) + (_g == 0) * 1.0
        g_xattn = _g[0]
        g_ffn = _g[1]
        return (x, ctx_1024, mask_Bx1xSxS2_ik1, mask_BxS2_bf1, g_xattn, g_ffn)
    x, ctx_1024, mask_Bx1xSxS2_ik1, mask_BxS2_bf1, g_xattn, g_ffn = _rec_inputs()

    def _L0_xattn_setup():
        import jax, jax.numpy as jnp
        import numpy as np
        D_MODEL = 256
        NUM_HEAD = 16
        D_K = D_MODEL // NUM_HEAD

        def _split_heads(x):
            b, s, _ = x.shape
            return x.reshape(b, s, NUM_HEAD, D_K).transpose(0, 2, 1, 3)
        key = jax.random.key(seed)
        ks = jax.random.split(key, 13)
        B, S = (2, 512)
        s = 1.0 / np.sqrt(D_MODEL)
        return {'q': jax.random.normal(ks[0], (B, S, D_MODEL), jnp.float32), 'k': jax.random.normal(ks[1], (B, S, D_MODEL), jnp.float32), 'v': jax.random.normal(ks[2], (B, S, D_MODEL), jnp.float32), 'mask': jax.random.randint(ks[3], (B, 1, S, S), 0, 2, jnp.int32), 'wq': jax.random.normal(ks[4], (D_MODEL, D_MODEL), jnp.float32) * s, 'bq': jax.random.normal(ks[5], (D_MODEL,), jnp.float32) * 0.02, 'wk': jax.random.normal(ks[6], (D_MODEL, D_MODEL), jnp.float32) * s, 'bk': jax.random.normal(ks[7], (D_MODEL,), jnp.float32) * 0.02, 'wv': jax.random.normal(ks[8], (D_MODEL, D_MODEL), jnp.float32) * s, 'bv': jax.random.normal(ks[9], (D_MODEL,), jnp.float32) * 0.02, 'wo': jax.random.normal(ks[10], (D_MODEL, D_MODEL), jnp.float32) * s, 'bo': jax.random.normal(ks[11], (D_MODEL,), jnp.float32) * 0.02}
    _L0_xattn_all = _L0_xattn_setup()
    _L0_xattn_in = {k: v for k, v in _L0_xattn_all.items() if k in ('wq', 'bq', 'wk', 'bk', 'wv', 'bv', 'wo', 'bo')}
    del _L0_xattn_all

    def _L0_ffn_setup():
        import jax, jax.numpy as jnp
        import numpy as np
        D_MODEL = 256
        D_HIDDEN = 1024
        NUM_EXPERT = 8
        TOP_K = 2
        B, N = (1, 2048)

        def _expert_mlp(x, W1, b1, W2, b2, W3, b3):
            h = jax.nn.gelu(jnp.einsum('bnd,dh->bnh', x, W1) + b1, approximate=False)
            h = jax.nn.gelu(jnp.einsum('bnh,hk->bnk', h, W2) + b2, approximate=False)
            return jnp.einsum('bnh,hd->bnd', h, W3) + b3
        key = jax.random.key(seed)
        ks = jax.random.split(key, 8)
        s1 = 1.0 / np.sqrt(D_MODEL)
        s2 = 1.0 / np.sqrt(D_HIDDEN)
        return {'x': jax.random.normal(ks[0], (B, N, D_MODEL), jnp.float32), 'expert_tokens': jax.random.normal(ks[1], (NUM_EXPERT, D_MODEL), jnp.float32), 'W1': jax.random.normal(ks[2], (NUM_EXPERT, D_MODEL, D_HIDDEN), jnp.float32) * s1, 'b1': jnp.zeros((NUM_EXPERT, D_HIDDEN), jnp.float32), 'W2': jax.random.normal(ks[3], (NUM_EXPERT, D_HIDDEN, D_HIDDEN), jnp.float32) * s2, 'b2': jnp.zeros((NUM_EXPERT, D_HIDDEN), jnp.float32), 'W3': jax.random.normal(ks[4], (NUM_EXPERT, D_HIDDEN, D_MODEL), jnp.float32) * s2, 'b3': jnp.zeros((NUM_EXPERT, D_MODEL), jnp.float32)}
    _L0_ffn_all = _L0_ffn_setup()
    _L0_ffn_in = {k: v for k, v in _L0_ffn_all.items() if k in ('expert_tokens', 'W1', 'b1', 'W2', 'b2', 'W3', 'b3')}
    del _L0_ffn_all

    def _L1_xattn_setup():
        import jax, jax.numpy as jnp
        import numpy as np
        EPS = 1e-05

        def layer_norm(x, gamma):
            mu = jnp.mean(x, axis=-1, keepdims=True)
            var = jnp.var(x, axis=-1, keepdims=True)
            return (x - mu) / jnp.sqrt(var + EPS) * gamma
        key = jax.random.key(seed)
        ks = jax.random.split(key, 8)
        b, n, m = (4, 512, 512)
        dim, ctx_dim, heads, dim_head = (256, 256, 8, 64)
        inner = heads * dim_head
        x = jax.random.normal(ks[0], (b, n, dim), dtype=jnp.float32)
        context = jax.random.normal(ks[1], (b, m, ctx_dim), dtype=jnp.float32)
        mask = jnp.ones((b, m), dtype=bool)
        gamma = jnp.ones((dim,), dtype=jnp.float32)
        w_q = jax.random.normal(ks[2], (dim, inner), dtype=jnp.float32) * dim ** (-0.5)
        w_kv = jax.random.normal(ks[3], (ctx_dim, 2 * inner), dtype=jnp.float32) * ctx_dim ** (-0.5)
        null_kv = jax.random.normal(ks[4], (2, dim_head), dtype=jnp.float32)
        w_out = jax.random.normal(ks[5], (inner, dim), dtype=jnp.float32) * inner ** (-0.5)
        out_gamma = jnp.ones((dim,), dtype=jnp.float32)
        return {'x': x, 'context': context, 'mask': mask, 'gamma': gamma, 'w_q': w_q, 'w_kv': w_kv, 'null_kv': null_kv, 'w_out': w_out, 'out_gamma': out_gamma}
    _L1_xattn_all = _L1_xattn_setup()
    _L1_xattn_in = {k: v for k, v in _L1_xattn_all.items() if k in ('gamma', 'w_q', 'w_kv', 'null_kv', 'w_out', 'out_gamma')}
    del _L1_xattn_all

    def _L1_ffn_setup():
        import jax, jax.numpy as jnp
        import numpy as np
        B, S, D, E = (4, 1024, 256, 8)
        key = jax.random.key(seed)
        k1, k2, k3, k4, k5 = jax.random.split(key, 5)
        scale = 1.0 / np.sqrt(D)
        return {'x': jax.random.normal(k1, (B, S, D), dtype=jnp.float32), 'Wg': jax.random.normal(k2, (D, D), dtype=jnp.float32) * scale, 'bg': jnp.zeros((D,), dtype=jnp.float32), 'We': jax.random.normal(k3, (E, D, D), dtype=jnp.float32) * scale, 'be': jnp.zeros((E, D), dtype=jnp.float32)}
    _L1_ffn_all = _L1_ffn_setup()
    _L1_ffn_in = {k: v for k, v in _L1_ffn_all.items() if k in ('Wg', 'bg', 'We', 'be')}
    del _L1_ffn_all
    return {'x': x, 'ctx_1024': ctx_1024, 'mask_Bx1xSxS2_ik1': mask_Bx1xSxS2_ik1, 'mask_BxS2_bf1': mask_BxS2_bf1, 'g_xattn': g_xattn, 'g_ffn': g_ffn, 'L0_xattn_wq': _L0_xattn_in['wq'], 'L0_xattn_bq': _L0_xattn_in['bq'], 'L0_xattn_wk': _L0_xattn_in['wk'], 'L0_xattn_bk': _L0_xattn_in['bk'], 'L0_xattn_wv': _L0_xattn_in['wv'], 'L0_xattn_bv': _L0_xattn_in['bv'], 'L0_xattn_wo': _L0_xattn_in['wo'], 'L0_xattn_bo': _L0_xattn_in['bo'], 'L0_ffn_expert_tokens': _L0_ffn_in['expert_tokens'], 'L0_ffn_W1': _L0_ffn_in['W1'], 'L0_ffn_b1': _L0_ffn_in['b1'], 'L0_ffn_W2': _L0_ffn_in['W2'], 'L0_ffn_b2': _L0_ffn_in['b2'], 'L0_ffn_W3': _L0_ffn_in['W3'], 'L0_ffn_b3': _L0_ffn_in['b3'], 'L1_xattn_gamma': _L1_xattn_in['gamma'], 'L1_xattn_w_q': _L1_xattn_in['w_q'], 'L1_xattn_w_kv': _L1_xattn_in['w_kv'], 'L1_xattn_null_kv': _L1_xattn_in['null_kv'], 'L1_xattn_w_out': _L1_xattn_in['w_out'], 'L1_xattn_out_gamma': _L1_xattn_in['out_gamma'], 'L1_ffn_Wg': _L1_ffn_in['Wg'], 'L1_ffn_bg': _L1_ffn_in['bg'], 'L1_ffn_We': _L1_ffn_in['We'], 'L1_ffn_be': _L1_ffn_in['be']}

def reference(x, ctx_1024, mask_Bx1xSxS2_ik1, mask_BxS2_bf1, g_xattn, g_ffn, L0_xattn_wq, L0_xattn_bq, L0_xattn_wk, L0_xattn_bk, L0_xattn_wv, L0_xattn_bv, L0_xattn_wo, L0_xattn_bo, L0_ffn_expert_tokens, L0_ffn_W1, L0_ffn_b1, L0_ffn_W2, L0_ffn_b2, L0_ffn_W3, L0_ffn_b3, L1_xattn_gamma, L1_xattn_w_q, L1_xattn_w_kv, L1_xattn_null_kv, L1_xattn_w_out, L1_xattn_out_gamma, L1_ffn_Wg, L1_ffn_bg, L1_ffn_We, L1_ffn_be):
    import jax
    import jax.numpy as jnp

    def _L0_xattn_ref(q, k, v, mask, wq, bq, wk, bk, wv, bv, wo, bo):
        import jax, jax.numpy as jnp
        import numpy as np
        D_MODEL = 256
        NUM_HEAD = 16
        D_K = D_MODEL // NUM_HEAD

        def _split_heads(x):
            b, s, _ = x.shape
            return x.reshape(b, s, NUM_HEAD, D_K).transpose(0, 2, 1, 3)
        query = _split_heads(q @ wq + bq)
        key = _split_heads(k @ wk + bk)
        value = _split_heads(v @ wv + bv)
        scale = 1.0 / np.sqrt(D_K).astype(np.float32)
        scores = jnp.einsum('bhqd,bhkd->bhqk', query, key) * scale
        scores = jnp.where(mask == 0, -jnp.inf, scores)
        attn = jax.nn.softmax(scores, axis=-1)
        out = jnp.einsum('bhqk,bhkd->bhqd', attn, value)
        b, h, s, d = out.shape
        out = out.transpose(0, 2, 1, 3).reshape(b, s, h * d)
        return out @ wo + bo

    def _L0_ffn_ref(x, expert_tokens, W1, b1, W2, b2, W3, b3):
        import jax, jax.numpy as jnp
        import numpy as np
        D_MODEL = 256
        D_HIDDEN = 1024
        NUM_EXPERT = 8
        TOP_K = 2
        B, N = (1, 2048)

        def _expert_mlp(x, W1, b1, W2, b2, W3, b3):
            h = jax.nn.gelu(jnp.einsum('bnd,dh->bnh', x, W1) + b1, approximate=False)
            h = jax.nn.gelu(jnp.einsum('bnh,hk->bnk', h, W2) + b2, approximate=False)
            return jnp.einsum('bnh,hd->bnd', h, W3) + b3
        scores = jnp.einsum('bnd,ed->bne', x, expert_tokens)
        _, topk_idx = jax.lax.top_k(scores, TOP_K)
        outputs = jnp.zeros_like(x)
        num_expert = W1.shape[0]
        for i in range(num_expert):
            w = jnp.mean((topk_idx == i).astype(x.dtype), axis=-1, keepdims=True)
            y = _expert_mlp(x, W1[i], b1[i], W2[i], b2[i], W3[i], b3[i])
            outputs = outputs + y * w
        return outputs

    def _L1_xattn_ref(x, context, mask, gamma, w_q, w_kv, null_kv, w_out, out_gamma):
        import jax, jax.numpy as jnp
        import numpy as np
        EPS = 1e-05

        def layer_norm(x, gamma):
            mu = jnp.mean(x, axis=-1, keepdims=True)
            var = jnp.var(x, axis=-1, keepdims=True)
            return (x - mu) / jnp.sqrt(var + EPS) * gamma
        heads = 8
        dim_head = w_q.shape[1] // heads
        scale = dim_head ** (-0.5)
        b, n, _ = x.shape
        xn = layer_norm(x, gamma)
        ctx = context
        q = xn @ w_q
        kv = ctx @ w_kv
        k, v = jnp.split(kv, 2, axis=-1)

        def split_heads(t):
            return t.reshape(t.shape[0], t.shape[1], heads, dim_head).transpose(0, 2, 1, 3)
        q, k, v = (split_heads(q), split_heads(k), split_heads(v))
        nk = jnp.broadcast_to(null_kv[0], (b, heads, 1, dim_head))
        nv = jnp.broadcast_to(null_kv[1], (b, heads, 1, dim_head))
        k = jnp.concatenate([nk, k], axis=2)
        v = jnp.concatenate([nv, v], axis=2)
        q = q * scale
        sim = jnp.einsum('bhid,bhjd->bhij', q, k)
        full_mask = jnp.pad(mask, ((0, 0), (1, 0)), constant_values=True)
        sim = jnp.where(full_mask[:, None, None, :], sim, jnp.finfo(sim.dtype).min)
        attn = jax.nn.softmax(sim.astype(jnp.float32), axis=-1).astype(sim.dtype)
        out = jnp.einsum('bhij,bhjd->bhid', attn, v)
        out = out.transpose(0, 2, 1, 3).reshape(b, n, heads * dim_head)
        out = out @ w_out
        return layer_norm(out, out_gamma)

    def _L1_ffn_ref(x, Wg, bg, We, be):
        import jax, jax.numpy as jnp
        import numpy as np
        B, S, D, E = (4, 1024, 256, 8)
        probs = jax.nn.softmax(x @ Wg + bg, axis=-1)
        idx = jnp.argmax(probs, axis=-1)
        p = jnp.take_along_axis(probs, idx[..., None], axis=-1)[..., 0]
        e_idx = idx % We.shape[0]
        h = jax.nn.relu(jnp.einsum('bsd,edf->besf', x, We) + be[None, :, None, :])
        onehot = jax.nn.one_hot(e_idx, We.shape[0], dtype=x.dtype)
        out = jnp.einsum('besf,bse->bsf', h, onehot) * p[..., None]
        return out
    x = x + jnp.tanh(g_xattn[0]) * _L0_xattn_ref(_layernorm(x, axis=-1), ctx_1024, ctx_1024, mask_Bx1xSxS2_ik1, L0_xattn_wq, L0_xattn_bq, L0_xattn_wk, L0_xattn_bk, L0_xattn_wv, L0_xattn_bv, L0_xattn_wo, L0_xattn_bo)
    x = x + jnp.tanh(g_ffn[0]) * _L0_ffn_ref(_layernorm(x, axis=-1), L0_ffn_expert_tokens, L0_ffn_W1, L0_ffn_b1, L0_ffn_W2, L0_ffn_b2, L0_ffn_W3, L0_ffn_b3)
    x = x + jnp.tanh(g_xattn[1]) * _L1_xattn_ref(_layernorm(x, axis=-1), ctx_1024, mask_BxS2_bf1, L1_xattn_gamma, L1_xattn_w_q, L1_xattn_w_kv, L1_xattn_null_kv, L1_xattn_w_out, L1_xattn_out_gamma)
    x = x + jnp.tanh(g_ffn[1]) * _L1_ffn_ref(_layernorm(x, axis=-1), L1_ffn_Wg, L1_ffn_bg, L1_ffn_We, L1_ffn_be)
    return x

_drawn_inputs = setup_inputs


def setup_inputs(seed=0):
    import zlib

    import numpy as np

    out = dict(_drawn_inputs(seed))
    spreads = {'g_ffn': (-1.0, 0.6),
     'L0_ffn_b1': (0.0, 0.476),
     'L0_ffn_b2': (0.0, 0.333),
     'L0_ffn_b3': (0.0, 0.1),
     'L1_xattn_gamma': (1.0, 0.2),
     'L1_xattn_out_gamma': (1.0, 0.2),
     'L1_ffn_bg': (0.0, 0.8),
     'L1_ffn_be': (0.0, 0.8)}
    factors = {'L0_xattn_bq': 8.0,
     'L0_xattn_bk': 8.0,
     'L1_xattn_null_kv': 8.0,
     'L1_ffn_Wg': 3.537,
     'L1_ffn_We': 3.488}
    for name, (base, spread) in spreads.items():
        noise = np.random.default_rng([zlib.crc32(name.encode()), seed]).standard_normal(out[name].shape)
        drawn = base * np.exp(spread * noise) if base else spread * noise
        out[name] = jnp.asarray(drawn.astype(out[name].dtype))
    for name, factor in factors.items():
        out[name] = (out[name] * factor).astype(out[name].dtype)
    return out
```

```python
from contextlib import ExitStack

import numpy as np

import concourse.bass as bass
import concourse.mybir as mybir
from concourse.alu_op_type import AluOpType as ALU

F32 = mybir.dt.float32
F32R = mybir.dt.float32r
BF16 = mybir.dt.bfloat16
I32 = mybir.dt.int32
U32 = mybir.dt.uint32
U8 = mybir.dt.uint8
ACT = mybir.ActivationFunctionType
AX = mybir.AxisListType

P = 128
B, S, D, CTX = 4, 512, 256, 1024
N = B * S
KC = D // P
NT = 512
QT = S // P
KT = CTX // P
H0, D0 = 16, 16
H1, D1 = 8, 64
I1 = H1 * D1
E, HID = 8, 1024
EPS = 1e-5
BIG = 3e38


class Steps:

    def __init__(self, eng, sem, per=0, rnd=0):
        self.eng, self.sem, self.per, self.rnd, self.n = eng, sem, per, rnd, 0

    def did(self, ins):
        self.n += 1
        ins.then_inc(self.sem, 1)

    def wait(self):
        self.eng.wait_ge(self.sem, self.rnd * self.per + self.n)

    def link(self, ins):
        self.did(ins)
        self.wait()

    def close(self):
        assert self.n == self.per, (self.n, self.per)


class Space:

    def __init__(self, nc, tag):
        self.nc, self.tag, self.ctx, self.sems = nc, tag, ExitStack(), []

    def __enter__(self):
        return self

    def __exit__(self, *a):
        self.ctx.__exit__(*a)
        if a[0] is None:
            self.nc.clear_and_free_semaphores(self.sems)
            self.nc.all_engine_barrier()

    def sb(self, name, shape, dt=F32):
        return self.ctx.enter_context(self.nc.sbuf_tensor(f"{self.tag}_{name}", shape, dt))

    def ps(self, name, shape, dt=F32):
        return self.ctx.enter_context(self.nc.psum_tensor(f"{self.tag}_{name}", shape, dt))

    def sem(self, name):
        self.sems.append(self.nc.alloc_semaphore(f"{self.tag}_{name}"))
        return self.sems[-1]

    def block(self):
        return self.ctx.enter_context(self.nc.Block())


def apart(eng, spare):
    eng.sem_inc(spare, 1)


def product3(pe, out, pairs, start=True, stop=True):
    n = 3 * len(pairs)
    k = 0
    for (s_hi, s_lo), (m_hi, m_lo) in pairs:
        for s, m in ((s_hi, m_hi), (s_hi, m_lo), (s_lo, m_hi)):
            ins = pe.matmul(out, s, m, start=start and k == 0, stop=stop and k == n - 1)
            k += 1
    return ins


def row_of(vec, n):
    return vec.rearrange("(a n) -> a n", a=1).broadcast_to([P, n])


def make_identity(pool, sp, ident, made):
    pool.memset(ident[:], 0.0).then_inc(made, 1)
    pool.wait_ge(made, 1)
    pool.affine_select(out=ident[:], in_=ident[:], compare_op=ALU.not_equal, fill=1.0, base=0,
                       pattern=[[-1, P]], channel_multiplier=1).then_inc(made, 1)


def stage_context(nc, ctx, wk, bk, wv, bv, wkv, mask0, mask1, k0s, v0s, k1s, v1s, bias0, bias1):
    with Space(nc, "c") as sp:
        W = D + D + 2 * I1
        w_raw = sp.sb("w_raw", [P, KC, W])
        w_hi = sp.sb("w_hi", [P, KC, W], F32R)
        w_lo = sp.sb("w_lo", [P, KC, W], F32R)
        bk_col = sp.sb("bk_col", [P, KC])
        bv_row = sp.sb("bv_row", [P, D])
        ident = sp.sb("ident", [P, P])
        rows = [sp.sb(f"rows{i}", [P, QT, D]) for i in range(2)]
        t_hi = [sp.sb(f"t_hi{i}", [P, KC, NT], F32R) for i in range(2)]
        t_lo = [sp.sb(f"t_lo{i}", [P, KC, NT], F32R) for i in range(2)]
        k_hi = [sp.sb(f"k_hi{i}", [P, 6, NT], F32R) for i in range(2)]
        k_lo = [sp.sb(f"k_lo{i}", [P, 6, NT], F32R) for i in range(2)]
        v1_st = [sp.sb(f"v1_st{i}", [P, QT, I1]) for i in range(2)]
        v0_st = [sp.sb(f"v0_st{i}", [P, QT, D]) for i in range(2)]
        m_raw = [sp.sb(f"m_raw{i}", [P, CTX], I32) for i in range(2)]
        m_bias = [sp.sb(f"m_bias{i}", [P, CTX], BF16) for i in range(2)]
        m1_raw, m1_bias = sp.sb("m1_raw", [B, CTX], U8), sp.sb("m1_bias", [B, CTX], BF16)
        tp = [sp.ps(f"tp{i}", [P, NT]) for i in range(KC)]
        bank = [sp.ps(f"bank{i}", [P, NT]) for i in range(6)]

        w_loaded, made = sp.sem("w_loaded"), sp.sem("made")
        w_hi_ready, w_ready = sp.sem("w_hi_ready"), sp.sem("w_ready")
        rows_loaded = [sp.sem(f"rows_loaded{i}") for i in range(2)]
        rows_free = sp.sem("rows_free")
        turned, t_hi_ready, t_ready = sp.sem("turned"), sp.sem("t_hi_ready"), sp.sem("t_ready")
        bank_full, act_free, dve_free = sp.sem("bank_full"), sp.sem("act_free"), sp.sem("dve_free")
        k_hi_ready = sp.sem("k_hi_ready")
        stored = [sp.sem(f"stored{i}") for i in range(2)]
        m_loaded = [sp.sem(f"m_loaded{i}") for i in range(2)]
        m_made, m_stored = sp.sem("m_made"), sp.sem("m_stored")
        m1_loaded, spare = sp.sem("m1_loaded"), sp.sem("spare")
        STORES = 6
        block = sp.block()

        @block.gpsimd
        def _(pool):
            make_identity(pool, sp, ident, made)
            pool.sem_inc(rows_free, 2)
            pool.wait_ge(m1_loaded, 16)
            pool.tensor_scalar(m1_bias[:], m1_raw[:], 0.0, BIG, ALU.is_equal, ALU.mult).then_inc(m_made, 1)
            with pool.Fori(0, B) as b:
                for half in range(2):
                    pool.wait_ge(rows_free, b * 2 + half + 1)
                    pool.dma_start(rows[half][:], ctx[b, half * NT:(half + 1) * NT, :].rearrange(
                        "(s p) d -> p s d", p=P)).then_inc(rows_loaded[half], 16)
                    for i in range(2):
                        n = (b * 2 + half) * 2 + i
                        pool.wait_ge(m_loaded[i], (b * 2 + half) * 16 + 16)
                        pool.wait_ge(m_stored, n * 16 + 16)
                        apart(pool, spare)
                        pool.tensor_scalar(m_bias[i][:], m_raw[i][:], 0.0, BIG, ALU.is_equal, ALU.mult
                                           ).then_inc(m_made, 1)

        @block.sync
        def _(sync):
            sync.dma_start(w_raw[:, :, 0:D], wk.rearrange("(c p) n -> p c n", p=P)).then_inc(w_loaded, 16)
            sync.dma_start(w_raw[:, :, D:2 * D], wv.rearrange("(c p) n -> p c n", p=P)).then_inc(w_loaded, 16)
            sync.dma_start(w_raw[:, :, 2 * D:], wkv.rearrange("(c p) n -> p c n", p=P)).then_inc(w_loaded, 16)
            sync.dma_start(bk_col[:], bk.rearrange("(c p) -> p c", p=P),
                           allow_slow_non_contiguous=True).then_inc(w_loaded, 16)
            sync.dma_start(bv_row[:], row_of(bv, D)).then_inc(w_loaded, 16)
            sync.dma_start(m1_raw[:], mask1).then_inc(m1_loaded, 16)
            sync.wait_ge(m_made, 1)
            sync.dma_start(bias1, m1_bias[:]).then_inc(m_stored, 16)
            with sync.Fori(0, B) as b:
                for half in range(2):
                    n = b * 2 + half
                    cols = slice(half * NT, (half + 1) * NT)
                    for i in range(2):
                        rows_m = slice((half * 2 + i) * P, (half * 2 + i + 1) * P)
                        sync.dma_start(m_raw[i][:], mask0[b, rows_m, :]).then_inc(m_loaded[i], 16)
                        sync.wait_ge(m_made, n * 2 + i + 2)
                        apart(sync, spare)
                        sync.dma_start(bias0[b, rows_m, :], m_bias[i][:]).then_inc(m_stored, 16)
                    sync.wait_ge(dve_free, n * 8 + 2 + 6)
                    for part, src in ((0, k_hi[half]), (1, k_lo[half])):
                        sync.dma_start(k0s[part, b, :, cols].rearrange("(c p) t -> p c t", p=P),
                                       src[:, 0:2, :].bitcast(F32)).then_inc(stored[half], 16)
                        sync.dma_start(k1s[part, b, :, cols].rearrange("(c p) t -> p c t", p=P),
                                       src[:, 2:6, :].bitcast(F32)).then_inc(stored[half], 16)
                    sync.wait_ge(act_free, n * 4 + 4 + 4)
                    sync.dma_start(v1s[b, cols, :].rearrange("(s p) n -> p s n", p=P),
                                   v1_st[half][:]).then_inc(stored[half], 16)
                    sync.wait_ge(dve_free, n * 8 + 2 + 8)
                    sync.dma_start(v0s[b, cols, :].rearrange("(s p) n -> p s n", p=P),
                                   v0_st[half][:]).then_inc(stored[half], 16)
            for half in range(2):
                sync.wait_ge(stored[half], 16 * STORES * B + 1)
            sync.wait_ge(m_stored, 16 * (1 + 2 * 2 * B))

        @block.tensor
        def _(pe):
            pe.wait_ge(made, 2)
            pe.wait_ge(w_ready, KC)
            with pe.Fori(0, B) as b:
                for half in range(2):
                    n = b * 2 + half
                    pe.wait_ge(rows_loaded[half], b * 16 + 16)
                    for c in range(KC):
                        for s in range(QT):
                            ins = pe.transpose(tp[c][:, s * P:(s + 1) * P], rows[half][:, s, c * P:(c + 1) * P],
                                               ident[:])
                        ins.then_inc(turned, 1)
                    pe.wait_ge(t_ready, n * KC + KC)
                    hi, lo = t_hi[half], t_lo[half]
                    for j in range(6):
                        col = j * P if j < 2 else 2 * D + (j - 2) * P
                        if j < 4:
                            pe.wait_ge(act_free, n * 4 + j + 1)
                        else:
                            pe.wait_ge(dve_free, n * 8 + (j - 4) + 1)
                        product3(pe, bank[j][:], [((w_hi[:, c, col:col + P], w_lo[:, c, col:col + P]),
                                                   (hi[:, c, :], lo[:, c, :])) for c in range(KC)]
                                 ).then_inc(bank_full, 1)
                    for s in range(QT):
                        pe.wait_ge(dve_free, n * 8 + 2 + s + 1)
                        product3(pe, bank[s][:], [((hi[:, c, s * P:(s + 1) * P], lo[:, c, s * P:(s + 1) * P]),
                                                   (w_hi[:, c, 2 * D + I1:], w_lo[:, c, 2 * D + I1:]))
                                                  for c in range(KC)]).then_inc(bank_full, 1)
                    for j in range(2):
                        pe.wait_ge(dve_free, n * 8 + 2 + 4 + j + 1)
                        for s in (2 * j, 2 * j + 1):
                            ins = product3(pe, bank[4 + j][:, (s % 2) * D:(s % 2 + 1) * D],
                                           [((hi[:, c, s * P:(s + 1) * P], lo[:, c, s * P:(s + 1) * P]),
                                             (w_hi[:, c, D:2 * D], w_lo[:, c, D:2 * D])) for c in range(KC)])
                        ins.then_inc(bank_full, 1)

        @block.scalar
        def _(act):
            act.wait_ge(w_loaded, 80)
            for c in range(KC):
                act.activation(w_hi[:, c, :], w_raw[:, c, :], ACT.Copy).then_inc(w_hi_ready, 1)
            act.sem_inc(act_free, 4)
            act.sem_inc(stored[0], 1)
            act.sem_inc(stored[1], 1)
            with act.Fori(0, B) as b:
                for half in range(2):
                    n = b * 2 + half
                    for c in range(KC):
                        act.wait_ge(turned, n * KC + c + 1)
                        act.activation(t_hi[half][:, c, :], tp[c][:], ACT.Copy).then_inc(t_hi_ready, 1)
                    act.wait_ge(stored[half], b * (16 * STORES) + 1)
                    for j in range(6):
                        act.wait_ge(bank_full, n * 12 + j + 1)
                        if j < 2:
                            ins = act.activation(k_hi[half][:, j, :], bank[j][:], ACT.Identity, bias=bk_col[:, j:j + 1])
                        else:
                            ins = act.activation(k_hi[half][:, j, :], bank[j][:], ACT.Copy)
                        ins.then_inc(k_hi_ready, 1)
                    for s in range(QT):
                        act.wait_ge(bank_full, n * 12 + 6 + s + 1)
                        act.activation(v1_st[half][:, s, :], bank[s][:], ACT.Copy).then_inc(act_free, 1)

        @block.vector
        def _(dve):
            dve.sem_inc(dve_free, 2)
            for c in range(KC):
                dve.wait_ge(w_hi_ready, c + 1)
                dve.tensor_tensor(w_lo[:, c, :], w_raw[:, c, :], w_hi[:, c, :].bitcast(F32),
                                  ALU.subtract).then_inc(w_ready, 1)
            with dve.Fori(0, B) as b:
                for half in range(2):
                    n = b * 2 + half
                    for c in range(KC):
                        dve.wait_ge(t_hi_ready, n * KC + c + 1)
                        dve.tensor_tensor(t_lo[half][:, c, :], tp[c][:], t_hi[half][:, c, :].bitcast(F32),
                                          ALU.subtract).then_inc(t_ready, 1)
                    dve.sem_inc(rows_free, 1)
                    dve.wait_ge(stored[half], b * (16 * STORES) + 1)
                    for j in range(6):
                        dve.wait_ge(k_hi_ready, n * 6 + j + 1)
                        if j < 2:
                            ins = dve.scalar_tensor_tensor(k_lo[half][:, j, :], bank[j][:], bk_col[:, j:j + 1],
                                                           k_hi[half][:, j, :].bitcast(F32), ALU.add, ALU.subtract)
                        else:
                            ins = dve.tensor_tensor(k_lo[half][:, j, :], bank[j][:],
                                                    k_hi[half][:, j, :].bitcast(F32), ALU.subtract)
                        ins.then_inc(dve_free, 1)
                    for j in range(2):
                        dve.wait_ge(bank_full, n * 12 + 10 + j + 1)
                        for s in range(2):
                            ins = dve.tensor_tensor(v0_st[half][:, 2 * j + s, :], bank[4 + j][:, s * D:(s + 1) * D],
                                                    bv_row[:], ALU.add)
                        ins.then_inc(dve_free, 1)


class Norm:

    def __init__(self, sp, tag):
        self.stats = sp.sb(f"{tag}_stats", [P, QT, 6])
        self.mv = sp.sb(f"{tag}_mv", [P, QT, 2])
        self.dev = sp.sb(f"{tag}_dev", [P, QT])
        self.rstd = sp.sb(f"{tag}_rstd", [P, QT])
        self.sums_ready, self.roots_ready = sp.sem(f"{tag}_sums_ready"), sp.sem(f"{tag}_roots_ready")

    def vector(self, dve, steps, rnd, src, dst, gamma=None):
        for s in range(QT):
            ins = dve.bn_stats(self.stats[:, s, :], src[s])
        steps.link(ins)
        for s in range(QT):
            ins = dve.bn_aggr(self.mv[:, s, :], self.stats[:, s, :])
        ins.then_inc(self.sums_ready, 1)
        dve.wait_ge(self.roots_ready, rnd + 1)
        steps.link(dve.reciprocal(self.rstd[:], self.dev[:]))
        for s in range(QT):
            ins = dve.tensor_scalar(dst[s], src[s], self.mv[:, s, 0:1], self.rstd[:, s:s + 1],
                                    ALU.subtract, ALU.mult)
        if gamma is not None:
            steps.link(ins)
            for s in range(QT):
                ins = dve.tensor_tensor(dst[s], dst[s], gamma, ALU.mult)
        steps.link(ins)

    def scalar(self, act, rnd, eps):
        act.wait_ge(self.sums_ready, rnd + 1)
        act.activation(self.dev[:], self.mv[:, :, 1], ACT.Sqrt, bias=eps).then_inc(self.roots_ready, 1)


def stage_queries(nc, x, wq, bq, q0s):
    with Space(nc, "q") as sp:
        neg_scale = -float(D0) ** -0.5
        w_raw = sp.sb("w_raw", [P, KC, D])
        w_hi, w_lo = sp.sb("w_hi", [P, KC, D], F32R), sp.sb("w_lo", [P, KC, D], F32R)
        bq_raw, bq_col = sp.sb("bq_raw", [P, KC]), sp.sb("bq_col", [P, KC])
        eps, ident = sp.sb("eps", [P, 1]), sp.sb("ident", [P, P])
        xin = sp.sb("xin", [P, B, QT, D])
        xn = sp.sb("xn", [P, QT, D])
        t_hi, t_lo = sp.sb("t_hi", [P, KC, NT], F32R), sp.sb("t_lo", [P, KC, NT], F32R)
        q_hi, q_lo = sp.sb("q_hi", [P, KC, NT], F32R), sp.sb("q_lo", [P, KC, NT], F32R)
        tp = [sp.ps(f"tp{i}", [P, NT]) for i in range(KC)]
        bank = [sp.ps(f"bank{i}", [P, NT]) for i in range(KC)]
        norm = Norm(sp, "norm")
        loaded, x_loaded, made = sp.sem("loaded"), sp.sem("x_loaded"), sp.sem("made")
        w_hi_ready, w_ready = sp.sem("w_hi_ready"), sp.sem("w_ready")
        xn_ready, turned, t_hi_ready, t_ready = (sp.sem(n) for n in ("xn_ready", "turned", "t_hi_ready", "t_ready"))
        full, q_hi_ready, q_ready, stored = (sp.sem(n) for n in ("full", "q_hi_ready", "q_ready", "stored"))
        own = sp.sem("own")
        block = sp.block()

        @block.gpsimd
        def _(pool):
            pool.memset(eps[:], EPS).then_inc(made, 1)
            pool.memset(ident[:], 0.0).then_inc(made, 1)
            pool.wait_ge(made, 2)
            pool.affine_select(out=ident[:], in_=ident[:], compare_op=ALU.not_equal, fill=1.0, base=0,
                               pattern=[[-1, P]], channel_multiplier=1).then_inc(made, 1)

        @block.sync
        def _(sync):
            sync.dma_start(xin[:], x.rearrange("b (s p) d -> p b s d", p=P)).then_inc(x_loaded, 16)
            sync.dma_start(w_raw[:], wq.rearrange("(c p) n -> p c n", p=P)).then_inc(loaded, 16)
            sync.dma_start(bq_raw[:], bq.rearrange("(c p) -> p c", p=P),
                           allow_slow_non_contiguous=True).then_inc(loaded, 16)
            for b in range(B):
                sync.wait_ge(q_ready, KC * (b + 1))
                for part, src in ((0, q_hi), (1, q_lo)):
                    sync.dma_start(q0s[part, b].rearrange("(c p) t -> p c t", p=P),
                                   src[:].bitcast(F32)).then_inc(stored, 16)
            sync.wait_ge(stored, 32 * B)

        @block.tensor
        def _(pe):
            pe.wait_ge(made, 3)
            pe.wait_ge(w_ready, KC)
            for b in range(B):
                pe.wait_ge(xn_ready, b + 1)
                for c in range(KC):
                    for s in range(QT):
                        ins = pe.transpose(tp[c][:, s * P:(s + 1) * P], xn[:, s, c * P:(c + 1) * P], ident[:])
                    ins.then_inc(turned, 1)
                pe.wait_ge(t_ready, KC * (b + 1))
                for j in range(KC):
                    if b:
                        pe.wait_ge(q_ready, KC * (b - 1) + j + 1)
                    product3(pe, bank[j][:], [((w_hi[:, c, j * P:(j + 1) * P], w_lo[:, c, j * P:(j + 1) * P]),
                                               (t_hi[:, c, :], t_lo[:, c, :])) for c in range(KC)]).then_inc(full, 1)

        @block.scalar
        def _(act):
            act.wait_ge(loaded, 32)
            for c in range(KC):
                act.activation(w_hi[:, c, :], w_raw[:, c, :], ACT.Copy, scale=neg_scale).then_inc(w_hi_ready, 1)
            act.activation(bq_col[:], bq_raw[:], ACT.Copy, scale=neg_scale).then_inc(w_hi_ready, 1)
            act.wait_ge(w_hi_ready, KC + 1)
            act.wait_ge(made, 3)
            for b in range(B):
                norm.scalar(act, b, eps[:])
                for c in range(KC):
                    act.wait_ge(turned, KC * b + c + 1)
                    act.activation(t_hi[:, c, :], tp[c][:], ACT.Copy).then_inc(t_hi_ready, 1)
                if b:
                    act.wait_ge(stored, 32 * b)
                for j in range(KC):
                    act.wait_ge(full, KC * b + j + 1)
                    act.activation(q_hi[:, j, :], bank[j][:], ACT.Identity, bias=bq_col[:, j:j + 1]
                                   ).then_inc(q_hi_ready, 1)

        @block.vector
        def _(dve):
            steps = Steps(dve, own)
            for c in range(KC):
                dve.wait_ge(w_hi_ready, c + 1)
                dve.scalar_tensor_tensor(w_lo[:, c, :], w_raw[:, c, :], neg_scale, w_hi[:, c, :].bitcast(F32),
                                         ALU.mult, ALU.subtract).then_inc(w_ready, 1)
            dve.wait_ge(x_loaded, 16)
            for b in range(B):
                if b:
                    dve.wait_ge(turned, KC * b)
                norm.vector(dve, steps, b, [xin[:, b, s, :] for s in range(QT)], [xn[:, s, :] for s in range(QT)])
                dve.sem_inc(xn_ready, 1)
                for c in range(KC):
                    dve.wait_ge(t_hi_ready, KC * b + c + 1)
                    dve.tensor_tensor(t_lo[:, c, :], tp[c][:], t_hi[:, c, :].bitcast(F32),
                                      ALU.subtract).then_inc(t_ready, 1)
                for j in range(KC):
                    dve.wait_ge(q_hi_ready, KC * b + j + 1)
                    dve.scalar_tensor_tensor(q_lo[:, j, :], bank[j][:], bq_col[:, j:j + 1],
                                             q_hi[:, j, :].bitcast(F32), ALU.add, ALU.subtract).then_inc(q_ready, 1)


class Count:

    def __init__(self, sem, prime):
        self.sem, self.prime = sem, prime

    def start(self, eng):
        eng.sem_inc(self.sem, self.prime)

    def wait(self, eng, n):
        eng.wait_ge(self.sem, n + self.prime)


def stage_attention(nc, tag, heads, dh, group, q_s, k_s, v_s, o_s, bias_s, null_s=None, null_kv=None):
    with Space(nc, tag) as sp:
        null = null_kv is not None
        groups = heads // group
        stacked = 3 * dh <= P
        per_query = len(bias_s.shape) == 3
        R = 2 * group if null else group
        rows_q = 3 * dh if stacked else 2 * dh
        qs = [sp.sb(f"qs{i}", [rows_q, S], F32R) for i in range(2)]
        ks = [sp.sb(f"ks{i}", [rows_q, CTX], F32R) for i in range(2)]
        kl = None if stacked else [sp.sb(f"kl{i}", [dh, CTX], F32R) for i in range(2)]
        vz = [sp.sb(f"vz{i}", [P, KT, group, P]) for i in range(2)]
        bias = sp.sb("bias", [P, QT if per_query else 1, CTX], BF16)
        p = [sp.sb(f"p{i}", [P, QT, CTX]) for i in range(2)]
        pt = [sp.sb(f"pt{i}", [P, NT]) for i in range(4)]
        nmax, sums = sp.sb("nmax", [P, heads, QT]), sp.sb("sums", [P, heads, QT])
        rcols, rrows = sp.sb("rcols", [P, QT, R]), sp.sb("rrows", [R, S])
        ident = sp.sb("ident", [P, P])
        sel = sp.sb("sel", [R, P])
        o_raw, o_out = sp.sb("o_raw", [P, S]), sp.sb("o_out", [P, S])
        s_ps = [sp.ps(f"s{i}", [P, CTX]) for i in range(2)]
        t_ps = [sp.ps(f"t{i}", [P, NT]) for i in range(2)]
        o_ps, f_ps = sp.ps("o", [P, NT]), sp.ps("f", [P, NT])
        dn, tot = sp.sb("dn", [P, group, QT]), sp.sb("tot", [P, group, QT])
        if null:
            nv_row = sp.sb("nv_row", [R, P])
            sn = sp.sb("sn", [P, heads, QT])
            pn = sp.sb("pn", [P, group, QT])

        PV = KT * group
        END_COPY, END_DIFF = 1, 2
        END_COLS, END_ROWS, END_MUL, END_ALL = (5, 6, 7, 8) if null else (6, 7, 8, 8)
        PE_END = 3 if null else 2
        QK = 6 if stacked else 5

        made, nv_loaded = sp.sem("made"), sp.sem("nv_loaded")
        qk_loaded = [sp.sem(f"qk_loaded{i}") for i in range(2)]
        v_loaded = [sp.sem(f"v_loaded{i}") for i in range(2)]
        bias_loaded = sp.sem("bias_loaded")
        scored = Count(sp.sem("scored"), 2 * QT)
        maxed = Count(sp.sem("maxed"), 1)
        exped = Count(sp.sem("exped"), 2)
        turned = Count(sp.sem("turned"), 2 * KT)
        act_moved = Count(sp.sem("act_moved"), 1)
        dve_moved = Count(sp.sem("dve_moved"), 1)
        weighed = Count(sp.sem("weighed"), PV + 4)
        ended = Count(sp.sem("ended"), END_ALL)
        pe_ended = sp.sem("pe_ended")
        null_exped = sp.sem("null_exped")
        stored = Count(sp.sem("stored"), 1)
        spare = sp.sem("spare")
        MADE = 9 if null else 7
        block = sp.block()

        @block.gpsimd
        def _(pool):
            pool.memset(ident[:], 0.0).then_inc(made, 1)
            pool.memset(sel[:], 1.0).then_inc(made, 1)
            pool.wait_ge(made, 2)
            pool.affine_select(out=ident[:], in_=ident[:], compare_op=ALU.not_equal, fill=1.0, base=0,
                               pattern=[[-1, P]], channel_multiplier=1).then_inc(made, 1)
            pool.affine_select(out=sel[:], in_=sel[:], compare_op=ALU.is_ge, fill=0.0, base=0,
                               pattern=[[1, P]], channel_multiplier=-dh).then_inc(made, 1)
            pool.wait_ge(made, 4)
            pool.affine_select(out=sel[:], in_=sel[:], compare_op=ALU.is_ge, fill=0.0, base=dh - 1,
                               pattern=[[-1, P]], channel_multiplier=dh).then_inc(made, 1)
            for i in range(2):
                pool.memset(vz[i][:], 0.0).then_inc(made, 1)
            if null:
                pool.wait_ge(nv_loaded, 32)
                pool.affine_select(out=nv_row[:], in_=nv_row[:], compare_op=ALU.is_ge, fill=0.0,
                                   base=dh * group, pattern=[[1, P]], channel_multiplier=-dh).then_inc(made, 1)
                pool.wait_ge(made, 8)
                pool.affine_select(out=nv_row[:], in_=nv_row[:], compare_op=ALU.is_ge, fill=0.0,
                                   base=dh - 1 - dh * group, pattern=[[-1, P]], channel_multiplier=dh
                                   ).then_inc(made, 1)

        @block.sync
        def _(sync):
            if null:
                for e in range(2):
                    sync.dma_start(nv_row[:, e * dh:(e + 1) * dh], null_kv[1:2, :].broadcast_to([R, dh])
                                   ).then_inc(nv_loaded, 16)
            sync.wait_ge(made, MADE)

            def load_qk(b, j):
                i, rows = j % 2, slice(j * dh, (j + 1) * dh)
                scored.wait(sync, (b * heads + j - 1) * QT)
                apart(sync, spare)
                for n, part in enumerate((0, 1, 0) if stacked else (0, 1)):
                    sync.dma_start(qs[i][n * dh:(n + 1) * dh, :].bitcast(F32), q_s[part, b, rows, :]
                                   ).then_inc(qk_loaded[i], 16)
                for n, part in enumerate((0, 0, 1) if stacked else (0, 0)):
                    sync.dma_start(ks[i][n * dh:(n + 1) * dh, :].bitcast(F32), k_s[part, b, rows, :]
                                   ).then_inc(qk_loaded[i], 16)
                if not stacked:
                    sync.dma_start(kl[i][:].bitcast(F32), k_s[1, b, rows, :]).then_inc(qk_loaded[i], 16)

            def load_v(b, g):
                weighed.wait(sync, (b * groups + g - 1) * PV)
                for e in range(group):
                    h = g * group + e
                    sync.dma_start(vz[g % 2][:, :, e, e * dh:(e + 1) * dh],
                                   v_s[b, :, h * dh:(h + 1) * dh].rearrange("(t p) d -> p t d", p=P)
                                   ).then_inc(v_loaded[g % 2], 16)

            with sync.Fori(0, B) as b:
                for j in range(heads):
                    load_qk(b, j)
                    if j == 1:
                        maxed.wait(sync, b * heads * QT)
                        if per_query:
                            sync.dma_start(bias[:], bias_s[b].rearrange("(t p) k -> p t k", p=P)
                                           ).then_inc(bias_loaded, 16)
                        else:
                            sync.dma_start(bias[:, 0, :], bias_s[bass.ds(b, 1), :].broadcast_to([P, CTX])
                                           ).then_inc(bias_loaded, 16)
                        if null:
                            ended.wait(sync, b * groups * END_ALL)
                            sync.dma_start(sn[:], null_s[b]).then_inc(bias_loaded, 16)
                    if j % group == 0:
                        load_v(b, j // group)

        @block.tensor
        def _(pe):
            scored.start(pe)
            turned.start(pe)
            weighed.start(pe)
            pe.wait_ge(made, MADE)

            def scores(b, j, t):
                i = j % 2
                if t == 0:
                    pe.wait_ge(qk_loaded[i], (b * (heads // 2) + j // 2 + 1) * 16 * QK)
                exped.wait(pe, (b * heads + j) * QT + t - 1)
                for half in range(2):
                    cols = slice(half * NT, (half + 1) * NT)
                    out = s_ps[t % 2][:, cols]
                    ins = pe.matmul(out, qs[i][:, t * P:(t + 1) * P], ks[i][:, cols], start=True, stop=stacked)
                    if not stacked:
                        ins = pe.matmul(out, qs[i][0:dh, t * P:(t + 1) * P], kl[i][:, cols], start=False, stop=True)
                ins.then_inc(scored.sem, 1)

            def turn(b, j, t):
                h = b * heads + j
                if t == 0:
                    exped.wait(pe, h * QT + QT)
                (act_moved, dve_moved)[t % 2].wait(pe, h * (KT // 2) + t // 2)
                for u in range(QT):
                    ins = pe.transpose(t_ps[t % 2][:, u * P:(u + 1) * P], p[j % 2][:, u, t * P:(t + 1) * P], ident[:])
                ins.then_inc(turned.sem, 1)

            def weigh(b, j, t):
                h, g, e = b * heads + j, j // group, j % group
                if t == 0 and e == 0:
                    pe.wait_ge(v_loaded[g % 2], (b * (groups // 2) + g // 2 + 1) * 16 * group)
                    ended.wait(pe, (b * groups + g - 1) * END_ALL + END_COPY)
                (act_moved, dve_moved)[t % 2].wait(pe, h * (KT // 2) + t // 2 + 1)
                pe.matmul(o_ps[:], vz[g % 2][:, t, e, :], pt[t % 4][:], start=(t == 0 and e == 0),
                          stop=(t == KT - 1 and e == group - 1)).then_inc(weighed.sem, 1)

            def end_group(b, g, step):
                k = b * groups + g
                if step == 0:
                    ended.wait(pe, k * END_ALL + END_COLS)
                    for u in range(QT):
                        ins = pe.transpose(f_ps[0:R, u * P:(u + 1) * P], rcols[:, u, :], ident[:])
                elif step == 1:
                    ended.wait(pe, k * END_ALL + END_ROWS)
                    ins = pe.matmul(f_ps[:], sel[:], rrows[:], start=True, stop=True)
                else:
                    ended.wait(pe, k * END_ALL + END_MUL)
                    ins = pe.matmul(f_ps[:], nv_row[:], rrows[:], start=True, stop=True)
                ins.then_inc(pe_ended, 1)

            with pe.Fori(0, B) as b:
                for t in range(QT):
                    scores(b, 0, t)
                for j in range(heads):
                    for t in range(KT):
                        turn(b, j, t)
                        if t % 2 and j + 1 < heads:
                            scores(b, j + 1, t // 2)
                        if t:
                            weigh(b, j, t - 1)
                        if j and j % group == 0 and t in (2, 4, 6)[:PE_END]:
                            end_group(b, j // group - 1, t // 2 - 1)
                    weigh(b, j, KT - 1)
                for step in range(PE_END):
                    end_group(b, groups - 1, step)

        @block.scalar
        def _(act):
            exped.start(act)
            act_moved.start(act)
            stored.start(act)

            def exps(b, j, t):
                h = b * heads + j
                maxed.wait(act, h * QT + t + 1)
                if t == 0:
                    turned.wait(act, (h - 1) * KT)
                act.activation(p[j % 2][:, t, :], s_ps[t % 2][:], ACT.Exp, bias=nmax[:, j, t:t + 1], scale=-1.0,
                               accum_out=sums[:, j, t:t + 1]).then_inc(exped.sem, 1)

            def move(b, j, t):
                h = b * heads + j
                turned.wait(act, h * KT + t + 1)
                weighed.wait(act, h * KT + t - 3)
                act.activation(pt[t % 4][:], t_ps[t % 2][:], ACT.Copy).then_inc(act_moved.sem, 1)

            def null_exps(b, g):
                k = b * groups + g
                ended.wait(act, k * END_ALL + END_DIFF)
                act.activation(pn[:], dn[:], ACT.Exp).then_inc(null_exped, 1)

            def store(b, g):
                ended.wait(act, (b * groups + g) * END_ALL + END_ALL)
                act.dma_start(o_s[b, g * P:(g + 1) * P, :], o_out[:]).then_inc(stored.sem, 16)

            with act.Fori(0, B) as b:
                for t in range(QT):
                    exps(b, 0, t)
                for j in range(heads):
                    more = j + 1 < heads
                    move(b, j, 0)
                    if null and j and j % group == 0:
                        null_exps(b, j // group - 1)
                    move(b, j, 2)
                    if more:
                        exps(b, j + 1, 0)
                    move(b, j, 4)
                    if more:
                        exps(b, j + 1, 1)
                    move(b, j, 6)
                    if more:
                        exps(b, j + 1, 2)
                        exps(b, j + 1, 3)
                    if j and j % group == 0:
                        store(b, j // group - 1)
                if null:
                    null_exps(b, groups - 1)
                store(b, groups - 1)
            stored.wait(act, 16 * B * groups)

        @block.vector
        def _(dve):
            maxed.start(dve)
            dve_moved.start(dve)
            ended.start(dve)

            def biased_max(b, j, t):
                h = b * heads + j
                if j == 0 and t == 0:
                    dve.wait_ge(bias_loaded, b * (32 if null else 16) + (32 if null else 16))
                scored.wait(dve, h * QT + t + 1)
                apart(dve, spare)
                dve.tensor_tensor_reduce(s_ps[t % 2][:], s_ps[t % 2][:], bias[:, t if per_query else 0, :],
                                         1.0, sn[:, j, t:t + 1] if null else BIG, ALU.add, ALU.min,
                                         nmax[:, j, t:t + 1]).then_inc(maxed.sem, 1)

            def move(b, j, t):
                h = b * heads + j
                turned.wait(dve, h * KT + t + 1)
                weighed.wait(dve, h * KT + t - 3)
                dve.tensor_copy(pt[t % 4][:], t_ps[t % 2][:]).then_inc(dve_moved.sem, 1)

            def end_group(b, g, step):
                k = b * groups + g
                hs = slice(g * group, (g + 1) * group)
                cols = rcols[:, :, 0:group].rearrange("p t e -> p e t")

                def did(ins, n):
                    ins.then_inc(ended.sem, 1)
                    ended.wait(dve, k * END_ALL + n)
                if step == 0:
                    weighed.wait(dve, (k + 1) * PV)
                    did(dve.tensor_copy(o_raw[:], o_ps[:]), END_COPY)
                    exped.wait(dve, (b * heads + (g + 1) * group) * QT)
                    if null:
                        did(dve.tensor_tensor(dn[:], nmax[:, hs, :], sn[:, hs, :], ALU.subtract), END_DIFF)
                        dve.wait_ge(null_exped, k + 1)
                        did(dve.tensor_tensor(tot[:], sums[:, hs, :], pn[:], ALU.add), 3)
                        did(dve.reciprocal(cols, tot[:]), 4)
                        did(dve.tensor_tensor(rcols[:, :, group:R].rearrange("p t e -> p e t"), cols, pn[:],
                                              ALU.mult), END_COLS)
                    else:
                        did(dve.tensor_scalar(dn[:], nmax[:, hs, :], BIG / 2, BIG, ALU.is_ge, ALU.mult), 2)
                        did(dve.tensor_scalar(dn[:], dn[:], 4.0, None, ALU.mult), 3)
                        did(dve.tensor_tensor(dn[:], dn[:], dn[:], ALU.subtract), 4)
                        did(dve.tensor_tensor(tot[:], sums[:, hs, :], dn[:], ALU.add), 5)
                        did(dve.reciprocal(cols, tot[:]), END_COLS)
                elif step == 1:
                    dve.wait_ge(pe_ended, k * PE_END + 1)
                    did(dve.tensor_copy(rrows[:], f_ps[0:R, :]), END_ROWS)
                elif step == 2:
                    dve.wait_ge(pe_ended, k * PE_END + 2)
                    stored.wait(dve, 16 * k)
                    did(dve.tensor_tensor(o_out[:], o_raw[:], f_ps[:], ALU.mult), END_MUL)
                else:
                    dve.wait_ge(pe_ended, k * PE_END + 3)
                    did(dve.tensor_tensor(o_out[:], o_out[:], f_ps[:], ALU.add), END_ALL)

            with dve.Fori(0, B) as b:
                for t in range(QT):
                    biased_max(b, 0, t)
                for j in range(heads):
                    ending = j and j % group == 0
                    if ending:
                        end_group(b, j // group - 1, 0)
                    for t in range(QT):
                        move(b, j, 2 * t + 1)
                        if ending and 1 <= t < PE_END + 1:
                            end_group(b, j // group - 1, t)
                        if j + 1 < heads:
                            biased_max(b, j + 1, t)
                for step in range(PE_END + 1):
                    end_group(b, groups - 1, step)


T = 384
TS = T // P
TOP = 2
J = (TOP * N - E) // T + E
SLOTS = J * T
NB = N // P
HC = HID // P
BW = 2 * HC + KC


def stage_route(nc, x, o0s, wo, bo, gate, tokens, b1, b2, b3, x1s, xgs, pos_s, tile_s, bias_s):
    with Space(nc, "r") as sp:
        w_raw = sp.sb("w_raw", [P, KC, D])
        w_hi, w_lo = sp.sb("w_hi", [P, KC, D], F32R), sp.sb("w_lo", [P, KC, D], F32R)
        bo_row, tanh_g, g_raw = sp.sb("bo_row", [P, D]), sp.sb("tanh_g", [P, 1]), sp.sb("g_raw", [P, 1])
        eps, ident, ones, tri = (sp.sb("eps", [P, 1]), sp.sb("ident", [P, P]), sp.sb("ones", [P, P]),
                                 sp.sb("tri", [P, P]))
        zeros = sp.sb("zeros", [P, 8, D])
        tok_t = sp.sb("tok_t", [P, KC, E])
        tok_raw = sp.sb("tok_raw", [E, D])
        brows = [sp.sb("b1rows", [E * HC, P]), sp.sb("b2rows", [E * HC, P]), sp.sb("b3rows", [E * KC, P])]
        bcols = sp.sb("bcols", [P, E, BW])
        iota_e = sp.sb("iota_e", [P, NB, E])
        iota_j = sp.sb("iota_j", [P, J + 2])
        xin = sp.sb("xin", [P, B, QT, D])
        xn = sp.sb("xn", [P, NB, D])
        ot = [sp.sb(f"ot{i}", [P, KC, NT]) for i in range(2)]
        ot_hi, ot_lo = sp.sb("ot_hi", [P, KC, NT], F32R), sp.sb("ot_lo", [P, KC, NT], F32R)
        tmp = sp.sb("tmp", [P, QT, D])
        xt = sp.sb("xt", [P, KC, NT])
        scores = sp.sb("scores", [P, NB, E])
        best, best_i = sp.sb("best", [P, NB, 8]), sp.sb("best_i", [P, NB, 8], U32)
        pick = sp.sb("pick", [P, TOP, NB])
        hot = sp.sb("hot", [P, TOP, NB, E])
        both, before = sp.sb("both", [P, NB, E]), sp.sb("before", [P, NB + 1, E])
        tiles, cum = sp.sb("tiles", [P, E]), sp.sb("cum", [P, E + 1])
        slot, mine = sp.sb("slot", [P, NB, E]), sp.sb("mine", [P, TOP, NB, E])
        pos_f, pos = sp.sb("pos_f", [P, TOP, NB]), sp.sb("pos", [P, TOP, NB], I32)
        tile_f, tile_i = sp.sb("tile_f", [P, J + 2]), sp.sb("tile_i", [P, J + 2], I32)
        bank = [sp.ps(f"bank{i}", [P, 2, D]) for i in range(2)]
        tp = [sp.ps(f"tp{i}", [P, NT]) for i in range(KC)]
        sc_ps, rank_ps, tot_ps = sp.ps("sc", [P, QT, E]), sp.ps("rank", [P, NB, E]), sp.ps("tot", [P, NB, E])
        b_ps = sp.ps("b_ps", [P, 2 * E * HC + E * KC + KC * E])
        norm = Norm(sp, "norm")

        loaded, x_loaded, made = sp.sem("loaded"), sp.sem("x_loaded"), sp.sem("made")
        o_loaded = [sp.sem(f"o_loaded{i}") for i in range(2)]
        w_hi_ready, w_ready = sp.sem("w_hi_ready"), sp.sem("w_ready")
        o_hi_ready, o_ready, full = sp.sem("o_hi_ready"), sp.sem("o_ready"), sp.sem("full")
        xn_ready, turned, xt_ready = sp.sem("xn_ready"), sp.sem("turned"), sp.sem("xt_ready")
        scored, sc_moved, zeroed = sp.sem("scored"), sp.sem("sc_moved"), sp.sem("zeroed")
        b_turned, b_moved, counted, both_ready = (sp.sem("b_turned"), sp.sem("b_moved"), sp.sem("counted"),
                                                  sp.sem("both_ready"))
        placed, scattered, stored, own = sp.sem("placed"), sp.sem("scattered"), sp.sem("stored"), sp.sem("own")
        x1_ready = sp.sem("x1_ready")
        MADE = 8
        ZR = 8 * P
        NZ = (SLOTS + T) // ZR
        ZREST = (SLOTS + T - NZ * ZR) // P
        block = sp.block()
        BC = [0, E * HC, 2 * E * HC, 2 * E * HC + E * KC]

        @block.gpsimd
        def _(pool):
            pool.memset(zeros[:], 0.0).then_inc(made, 1)
            pool.memset(eps[:], EPS).then_inc(made, 1)
            pool.memset(ident[:], 0.0).then_inc(made, 1)
            pool.memset(ones[:], 1.0).then_inc(made, 1)
            pool.wait_ge(made, 4)
            pool.affine_select(out=ident[:], in_=ident[:], compare_op=ALU.not_equal, fill=1.0, base=0,
                               pattern=[[-1, P]], channel_multiplier=1).then_inc(made, 1)
            pool.affine_select(out=tri[:], in_=ones[:], compare_op=ALU.is_ge, fill=0.0, base=-1,
                               pattern=[[1, P]], channel_multiplier=-1).then_inc(made, 1)
            pool.iota(iota_e[:], [[0, NB], [1, E]], base=0, channel_multiplier=0,
                      allow_small_or_imprecise_dtypes=True).then_inc(made, 1)
            pool.iota(iota_j[:], [[1, J + 2]], base=0, channel_multiplier=0,
                      allow_small_or_imprecise_dtypes=True).then_inc(made, 1)
            pool.wait_ge(placed, 1)
            pool.wait_ge(zeroed, 16 * (NZ + 1))
            for t in range(NB):
                for k in range(TOP):
                    pool.indirect_dma_start(xgs, bass.IndirectOffsetOnAxis(ap=pos[:, k, t:t + 1], axis=0),
                                            xn[:, t, :], None).then_inc(scattered, 16)
            pool.wait_ge(scattered, 16 * NB * TOP)

        @block.sync
        def _(sync):
            sync.dma_start(w_raw[:], wo.rearrange("(c p) n -> p c n", p=P)).then_inc(loaded, 16)
            sync.dma_start(bo_row[:], row_of(bo, D)).then_inc(loaded, 16)
            sync.dma_start(g_raw[:], row_of(gate, 2)[:, 0:1]).then_inc(loaded, 16)
            sync.dma_start(tok_raw[:], tokens).then_inc(loaded, 16)
            sync.dma_start(brows[0][:], b1.rearrange("e (c p) -> (e c) p", p=P)).then_inc(loaded, 16)
            sync.dma_start(brows[1][:], b2.rearrange("e (c p) -> (e c) p", p=P)).then_inc(loaded, 16)
            sync.dma_start(brows[2][:], b3.rearrange("e (c p) -> (e c) p", p=P)).then_inc(loaded, 16)
            sync.dma_start(xin[:], x.rearrange("b (s p) d -> p b s d", p=P)).then_inc(x_loaded, 16)
            for b in range(2):
                sync.dma_start(ot[b][:], o0s[b].rearrange("(c p) t -> p c t", p=P)).then_inc(o_loaded[b], 16)
            sync.wait_ge(made, MADE)
            for z in range(NZ):
                sync.dma_start(xgs[z * ZR:(z + 1) * ZR, :].rearrange("(s p) d -> p s d", p=P),
                               zeros[:]).then_inc(zeroed, 16)
            sync.dma_start(xgs[NZ * ZR:SLOTS + T, :].rearrange("(s p) d -> p s d", p=P),
                           zeros[:, 0:ZREST, :]).then_inc(zeroed, 16)
            for b in range(2, B):
                sync.wait_ge(o_ready, KC * (b - 1))
                sync.dma_start(ot[b % 2][:], o0s[b].rearrange("(c p) t -> p c t", p=P)).then_inc(o_loaded[b % 2], 16)
            sync.wait_ge(x1_ready, B)
            sync.dma_start(x1s.rearrange("b (s p) d -> p b s d", p=P), xin[:]).then_inc(stored, 16)
            sync.wait_ge(b_moved, 2)
            sync.dma_start(bias_s.rearrange("e p c -> p e c"), bcols[:]).then_inc(stored, 16)
            sync.wait_ge(placed, 1)
            sync.dma_start(pos_s, pos[:]).then_inc(stored, 16)
            sync.dma_start(tile_s, tile_i[0:1, :]).then_inc(stored, 16)
            sync.wait_ge(stored, 64)

        @block.tensor
        def _(pe):
            pe.wait_ge(made, MADE)
            pe.wait_ge(loaded, 16 * 7)
            for i in range(3):
                n = brows[i].shape[0]
                pe.transpose(b_ps[:, BC[i]:BC[i] + n], brows[i][:], ident[0:n, 0:n])
            for c in range(KC):
                ins = pe.transpose(b_ps[:, BC[3] + c * E:BC[3] + (c + 1) * E], tok_raw[:, c * P:(c + 1) * P],
                                   ident[0:E, 0:E])
            ins.then_inc(b_turned, 1)
            pe.wait_ge(w_ready, KC)
            pe.wait_ge(b_moved, 2)
            for b in range(B):
                pe.wait_ge(o_ready, KC * (b + 1))
                if b:
                    pe.wait_ge(x1_ready, b)
                for s in range(QT):
                    ins = product3(pe, bank[s // 2][:, s % 2, :],
                                   [((ot_hi[:, c, s * P:(s + 1) * P], ot_lo[:, c, s * P:(s + 1) * P]),
                                     (w_hi[:, c, :], w_lo[:, c, :])) for c in range(KC)])
                ins.then_inc(full, 1)
                pe.wait_ge(xn_ready, b + 1)
                for c in range(KC):
                    for s in range(QT):
                        ins = pe.transpose(tp[c][:, s * P:(s + 1) * P], xn[:, b * QT + s, c * P:(c + 1) * P], ident[:])
                    ins.then_inc(turned, 1)
                pe.wait_ge(xt_ready, KC * (b + 1))
                if b:
                    pe.wait_ge(sc_moved, b)
                for s in range(QT):
                    for c in range(KC):
                        ins = pe.matmul(sc_ps[:, s, :], xt[:, c, s * P:(s + 1) * P], tok_t[:, c, :],
                                        start=(c == 0), stop=(c == KC - 1))
                ins.then_inc(scored, 1)
            pe.wait_ge(both_ready, 1)
            flat = both[:].rearrange("p t e -> p (t e)")
            pe.matmul(rank_ps[:].rearrange("p t e -> p (t e)"), tri[:], flat, start=True, stop=True)
            pe.matmul(tot_ps[:].rearrange("p t e -> p (t e)"), ones[:], flat, start=True, stop=True).then_inc(counted, 1)

        @block.scalar
        def _(act):
            act.wait_ge(loaded, 16 * 7)
            for c in range(KC):
                act.activation(w_hi[:, c, :], w_raw[:, c, :], ACT.Copy).then_inc(w_hi_ready, 1)
            act.activation(tanh_g[:], g_raw[:], ACT.Tanh).then_inc(w_hi_ready, 1)
            act.wait_ge(made, MADE)
            for b in range(B):
                act.wait_ge(o_loaded[b % 2], 16 * (b // 2 + 1))
                if b:
                    act.wait_ge(full, b)
                for c in range(KC):
                    act.activation(ot_hi[:, c, :], ot[b % 2][:, c, :], ACT.Copy).then_inc(o_hi_ready, 1)
                norm.scalar(act, b, eps[:])
                if b:
                    act.wait_ge(scored, b)
                for c in range(KC):
                    act.wait_ge(turned, KC * b + c + 1)
                    act.activation(xt[:, c, :], tp[c][:], ACT.Copy).then_inc(xt_ready, 1)

        @block.vector
        def _(dve):
            steps = Steps(dve, own)
            for c in range(KC):
                dve.wait_ge(w_hi_ready, c + 1)
                dve.tensor_tensor(w_lo[:, c, :], w_raw[:, c, :], w_hi[:, c, :].bitcast(F32),
                                  ALU.subtract).then_inc(w_ready, 1)
            dve.wait_ge(b_turned, 1)
            for i, (at, n) in enumerate(((0, HC), (HC, HC), (2 * HC, KC))):
                ins = dve.tensor_copy(bcols[:, :, at:at + n],
                                      b_ps[:, BC[i]:BC[i] + E * n].rearrange("p (e c) -> p e c", e=E))
            ins.then_inc(b_moved, 1)
            dve.tensor_copy(tok_t[:], b_ps[:, BC[3]:BC[3] + KC * E].rearrange("p (c e) -> p c e", c=KC)
                            ).then_inc(b_moved, 1)
            dve.wait_ge(x_loaded, 16)
            dve.wait_ge(w_hi_ready, KC + 1)
            for b in range(B):
                if b:
                    dve.wait_ge(full, b)
                for c in range(KC):
                    dve.wait_ge(o_hi_ready, KC * b + c + 1)
                    dve.tensor_tensor(ot_lo[:, c, :], ot[b % 2][:, c, :], ot_hi[:, c, :].bitcast(F32),
                                      ALU.subtract).then_inc(o_ready, 1)
                dve.wait_ge(full, b + 1)
                for i in range(2):
                    ins = dve.tensor_tensor(tmp[:, 2 * i:2 * i + 2, :], bank[i][:],
                                            bo_row[:].unsqueeze(1).broadcast_to([P, 2, D]), ALU.add)
                steps.link(ins)
                ins = dve.scalar_tensor_tensor(xin[:, b], tmp[:], tanh_g[:, 0:1], xin[:, b], ALU.mult, ALU.add)
                ins.then_inc(x1_ready, 1)
                dve.wait_ge(x1_ready, b + 1)
                norm.vector(dve, steps, b, [xin[:, b, s, :] for s in range(QT)],
                            [xn[:, b * QT + s, :] for s in range(QT)])
                dve.sem_inc(xn_ready, 1)
                dve.wait_ge(scored, b + 1)
                dve.tensor_copy(scores[:, b * QT:(b + 1) * QT, :], sc_ps[:]).then_inc(sc_moved, 1)
            dve.wait_ge(sc_moved, B)
            for t in range(NB):
                ins = dve.max(best[:, t, :], scores[:, t, :])
            steps.link(ins)
            for t in range(NB):
                ins = dve.max_index(best_i[:, t, :], best[:, t, :], scores[:, t, :])
            steps.link(ins)
            steps.link(dve.tensor_copy(pick[:].rearrange("p k t -> p t k"), best_i[:, :, 0:TOP]))
            for k in range(TOP):
                ins = dve.tensor_tensor(hot[:, k], iota_e[:], pick[:, k, :].unsqueeze(2).broadcast_to([P, NB, E]),
                                        ALU.is_equal)
            steps.link(ins)
            dve.tensor_tensor(both[:], hot[:, 0], hot[:, 1], ALU.add).then_inc(both_ready, 1)
            steps.link(dve.memset(before[:, 0, :], 0.0))
            dve.wait_ge(counted, 1)
            for t in range(NB):
                steps.link(dve.tensor_tensor(before[:, t + 1, :], before[:, t, :], tot_ps[:, t, :], ALU.add))
            steps.link(dve.tensor_scalar(tiles[:], before[:, NB, :], 0.0, None, ALU.is_gt))
            for i in range(1, -(-N // T)):
                steps.link(dve.scalar_tensor_tensor(tiles[:], before[:, NB, :], float(i * T), tiles[:],
                                                    ALU.is_gt, ALU.add))
            steps.link(dve.memset(cum[:, 0:1], 0.0))
            for e in range(E):
                steps.link(dve.tensor_tensor(cum[:, e + 1:e + 2], cum[:, e:e + 1], tiles[:, e:e + 1], ALU.add))
            steps.link(dve.tensor_tensor(slot[:], rank_ps[:], before[:, 0:NB, :], ALU.add))
            steps.link(dve.scalar_tensor_tensor(slot[:], cum[:, 0:E].unsqueeze(1).broadcast_to([P, NB, E]), float(T),
                                                slot[:], ALU.mult, ALU.add))
            for k in range(TOP):
                ins = dve.tensor_tensor(mine[:, k], hot[:, k], slot[:], ALU.mult)
            steps.link(ins)
            steps.link(dve.tensor_reduce(pos_f[:], mine[:], AX.X, ALU.add))
            dve.tensor_copy(pos[:], pos_f[:])
            steps.link(dve.tensor_scalar(tile_f[:], iota_j[:], cum[:, 1:2], None, ALU.is_ge))
            for e in range(1, E):
                steps.link(dve.scalar_tensor_tensor(tile_f[:], iota_j[:], cum[:, e + 1:e + 2], tile_f[:],
                                                    ALU.is_ge, ALU.add))
            steps.link(dve.tensor_scalar(tile_f[:], tile_f[:], float(E - 1), None, ALU.min))
            dve.tensor_copy(tile_i[:], tile_f[:]).then_inc(placed, 1)


def stage_experts(nc, xgs, tile_s, bias_s, w1, w2, w3, ys):
    with Space(nc, "e") as sp:
        RING = 6
        CH = 2 + HC + 2
        W2C, W3C = 2, 2 + HC
        raw = [sp.sb(f"raw{i}", [P, HID]) for i in range(RING)]
        w_hi, w_lo = sp.sb("w_hi", [P, CH, HID], F32R), sp.sb("w_lo", [P, CH, HID], F32R)
        b1_t, b2_t, b3_t = sp.sb("b1_t", [P, HC]), sp.sb("b2_t", [P, HC]), sp.sb("b3_t", [P, KC])
        rows = sp.sb("rows", [P, TS, D])
        x_hi, x_lo = sp.sb("x_hi", [P, KC, T], F32R), sp.sb("x_lo", [P, KC, T], F32R)
        h_hi = [sp.sb(f"h{i}_hi", [P, HC, T], F32R) for i in range(2)]
        h_lo = [sp.sb(f"h{i}_lo", [P, HC, T], F32R) for i in range(2)]
        g = [sp.sb(f"g{i}", [P, T]) for i in range(2)]
        y_t, y_rows = sp.sb("y_t", [P, KC, T]), sp.sb("y_rows", [P, TS, D])
        ident = sp.sb("ident", [P, P])
        tile_e = sp.sb("tile_e", [1, J + 2], I32)
        RB = 3
        bank = [sp.ps(f"bank{i}", [P, NT]) for i in range(RB)]
        tp = [sp.ps(f"tp{i}", [P, NT]) for i in range(KC)]
        yp = [sp.ps(f"yp{i}", [P, 2, D]) for i in range(2)]

        made, te_loaded = sp.sem("made"), sp.sem("te_loaded")
        raw_loaded = [sp.sem(f"raw_loaded{i}") for i in range(RING)]
        split_hi = sp.sem("split_hi")
        split = Count(sp.sem("split"), RING)
        b1_loaded, b2_loaded, b3_loaded, rows_loaded = (sp.sem(n) for n in ("b1_loaded", "b2_loaded", "b3_loaded",
                                                                            "rows_loaded"))
        x_turned, x_hi_ready, x_ready = sp.sem("x_turned"), sp.sem("x_hi_ready"), sp.sem("x_ready")
        full = Count(sp.sem("full"), 2 * HC + KC)
        read = Count(sp.sem("read"), 2 * HC + KC)
        h_ready = Count(sp.sem("h_ready"), 2)
        y_turned, y_moved = sp.sem("y_turned"), Count(sp.sem("y_moved"), 1)
        y_stored, y_free = sp.sem("y_stored"), Count(sp.sem("y_free"), 1)
        spare = sp.sem("spare")
        NBK = 2 * HC + KC
        assert NBK % RB == 0
        block = sp.block()
        ORDER = list(range(W2C, CH)) + [0, 1]

        @block.gpsimd
        def _(pool):
            make_identity(pool, sp, ident, made)
            y_free.start(pool)
            with pool.Fori(0, J) as t:
                y_moved.wait(pool, t + 1)
                pool.dma_start(ys[bass.ds(t * T, T), :].rearrange("(s p) d -> p s d", p=P), y_rows[:]
                               ).then_inc(y_stored, 16)
                pool.wait_ge(y_stored, t * 16 + 16)
                pool.sem_inc(y_free.sem, 1)

        @block.sync
        def _(sync):
            sync.dma_start(tile_e[:], tile_s).then_inc(te_loaded, 16)
            sync.wait_ge(te_loaded, 16)

            def load_chunk(q, e, n, slot):
                split.wait(sync, n - RING + 1)
                apart(sync, spare)
                if q < W2C:
                    src, dst = w1[e, q * P:(q + 1) * P, :], raw[slot][:]
                elif q < W3C:
                    src, dst = w2[e, (q - W2C) * P:(q - W2C + 1) * P, :], raw[slot][:]
                else:
                    r = (q - W3C) * 4 * P
                    src = w3[e, r:r + 4 * P, :].rearrange("(c p) n -> p c n", p=P)
                    dst = raw[slot][:].rearrange("p (c n) -> p c n", c=4)
                sync.dma_start(dst, src).then_inc(raw_loaded[slot], 16)

            e0 = sync.value_load(tile_e[0:1, 0:1], min_val=0, max_val=E - 1)
            sync.dma_start(rows[:], xgs[0:T, :].rearrange("(s p) d -> p s d", p=P)).then_inc(rows_loaded, 16)
            sync.dma_start(b1_t[:], bias_s[e0, :, 0:HC]).then_inc(b1_loaded, 16)
            for q in (0, 1):
                split.wait(sync, q - RING + 1)
                sync.dma_start(raw[q][:], w1[e0, q * P:(q + 1) * P, :]).then_inc(raw_loaded[q], 16)
            with sync.Fori(0, J) as t:
                e = sync.value_load(tile_e[0:1, bass.ds(t, 1)], min_val=0, max_val=E - 1)
                en = sync.value_load(tile_e[0:1, bass.ds(t + 1, 1)], min_val=0, max_val=E - 1)
                read.wait(sync, t * NBK - KC)
                apart(sync, spare)
                sync.dma_start(b2_t[:], bias_s[e, :, HC:2 * HC]).then_inc(b2_loaded, 16)
                for i, q in enumerate(ORDER):
                    if i == HC:
                        read.wait(sync, t * NBK)
                        apart(sync, spare)
                        sync.dma_start(b3_t[:], bias_s[e, :, 2 * HC:BW]).then_inc(b3_loaded, 16)
                    if i == HC + 2:
                        sync.wait_ge(x_turned, t * KC + KC)
                        apart(sync, spare)
                        sync.dma_start(rows[:], xgs[bass.ds((t + 1) * T, T), :].rearrange("(s p) d -> p s d", p=P)
                                       ).then_inc(rows_loaded, 16)
                        read.wait(sync, t * NBK + HC)
                        apart(sync, spare)
                        sync.dma_start(b1_t[:], bias_s[en, :, 0:HC]).then_inc(b1_loaded, 16)
                    load_chunk(q, en if q < W2C else e, t * CH + 2 + i, (2 + i) % RING)

        @block.tensor
        def _(pe):
            full.start(pe)
            pe.wait_ge(made, 2)

            def turn_rows(t):
                pe.wait_ge(rows_loaded, t * 16 + 16)
                for c in range(KC):
                    for s in range(TS):
                        ins = pe.transpose(tp[c][:, s * P:(s + 1) * P], rows[:, s, c * P:(c + 1) * P], ident[:])
                    ins.then_inc(x_turned, 1)

            def block_of(t, m, pairs, waits):
                read.wait(pe, t * NBK + m - RB + 1)
                for i, (stat, mov) in enumerate(pairs):
                    if waits[i]:
                        waits[i]()
                    ins = product3(pe, bank[m % RB][:, 0:T], [(stat, mov)], start=(i == 0), stop=(i == len(pairs) - 1))
                ins.then_inc(full.sem, 1)

            def weights(q, col):
                return w_hi[:, q, col:col + P], w_lo[:, q, col:col + P]

            turn_rows(0)
            with pe.Fori(0, J) as t:
                for m in range(HC):
                    def first(c):
                        if m == 0:
                            pe.wait_ge(x_ready, t * KC + c + 1)
                            split.wait(pe, t * CH + c + 1)
                    block_of(t, m, [(weights(c, m * P), (x_hi[:, c, :], x_lo[:, c, :])) for c in range(KC)],
                             [(lambda c=c: first(c)) for c in range(KC)])
                for m in range(HC):
                    def second(c):
                        if m == 0:
                            h_ready.wait(pe, t * 2 * HC + c + 1)
                            split.wait(pe, t * CH + 2 + c + 1)
                    block_of(t, HC + m, [(weights(W2C + c, m * P), (h_hi[0][:, c, :], h_lo[0][:, c, :]))
                                         for c in range(HC)], [(lambda c=c: second(c)) for c in range(HC)])
                    if m == 3:
                        turn_rows(t + 1)
                for m in range(KC):
                    def third(c):
                        if m == 0:
                            h_ready.wait(pe, t * 2 * HC + HC + c + 1)
                            split.wait(pe, t * CH + 2 + HC + c // 4 + 1)
                    block_of(t, 2 * HC + m, [(weights(W3C + c // 4, (c % 4) * D + m * P),
                                              (h_hi[1][:, c, :], h_lo[1][:, c, :])) for c in range(HC)],
                             [(lambda c=c: third(c)) for c in range(HC)])
                y_moved.wait(pe, t)
                for m in range(KC):
                    read.wait(pe, t * NBK + 2 * HC + m + 1)
                    for s in range(TS):
                        ins = pe.transpose(yp[s // 2][:, s % 2, m * P:(m + 1) * P], y_t[:, m, s * P:(s + 1) * P],
                                           ident[:])
                ins.then_inc(y_turned, 1)

        @block.scalar
        def _(act):
            read.start(act)

            def high(n, q, slot, t):
                act.wait_ge(raw_loaded[slot], (n // RING + 1) * 16 if isinstance(n, int) else t)
                act.activation(w_hi[:, q, :], raw[slot][:], ACT.Copy).then_inc(split_hi, 1)

            def chunk(t, i):
                q, slot = ORDER[i], (2 + i) % RING
                last = HC if q < W2C else 2 * HC - NBK if q < W3C else 2 * HC + KC - NBK
                full.wait(act, t * NBK + last)
                high(None, q, slot, (t * (CH // RING) + (2 + i) // RING + 1) * 16)

            def gelu(t, m):
                layer, c = m // HC, m % HC
                bias = (b1_t, b2_t)[layer]
                if c == 0:
                    act.wait_ge((b1_loaded, b2_loaded)[layer], t * 16 + 16)
                    full.wait(act, (t - 1) * NBK + (2 * HC + KC if layer else 2 * HC))
                full.wait(act, t * NBK + m + 1)
                h_ready.wait(act, t * 2 * HC + m - 1)
                act.activation(g[m % 2][:], bank[m % RB][:, 0:T], ACT.Gelu, bias=bias[:, c:c + 1])
                act.activation(h_hi[layer][:, c, :], bank[m % RB][:, 0:T], ACT.Gelu, bias=bias[:, c:c + 1]
                               ).then_inc(read.sem, 1)

            def rows_high(t):
                for c in range(KC):
                    act.wait_ge(x_turned, t * KC + c + 1)
                    act.activation(x_hi[:, c, :], tp[c][:, 0:T], ACT.Copy).then_inc(x_hi_ready, 1)

            for c in range(KC):
                act.wait_ge(raw_loaded[c], 16)
                act.activation(w_hi[:, c, :], raw[c][:], ACT.Copy).then_inc(split_hi, 1)
            rows_high(0)
            with act.Fori(0, J) as t:
                for i in range(4):
                    chunk(t, i)
                for m in range(HC):
                    gelu(t, m)
                    if m % 2 == 0:
                        chunk(t, 4 + m // 2)
                for i in range(HC, CH):
                    chunk(t, i)
                for m in range(HC, HC + 4):
                    gelu(t, m)
                rows_high(t + 1)
                for m in range(HC + 4, 2 * HC):
                    gelu(t, m)
                act.wait_ge(b3_loaded, t * 16 + 16)
                for m in range(KC):
                    full.wait(act, t * NBK + 2 * HC + m + 1)
                    act.activation(y_t[:, m, :], bank[(2 * HC + m) % RB][:, 0:T], ACT.Identity, bias=b3_t[:, m:m + 1]
                                   ).then_inc(read.sem, 1)

        @block.vector
        def _(dve):
            split.start(dve)
            h_ready.start(dve)
            y_moved.start(dve)

            def low(n, q, slot):
                dve.wait_ge(split_hi, n + 1)
                dve.tensor_tensor(w_lo[:, q, :], raw[slot][:], w_hi[:, q, :].bitcast(F32), ALU.subtract
                                  ).then_inc(split.sem, 1)

            def chunk(t, i):
                low(t * CH + 2 + i, ORDER[i], (2 + i) % RING)

            def rest(t, m):
                layer, c = m // HC, m % HC
                read.wait(dve, t * NBK + m + 1)
                dve.tensor_tensor(h_lo[layer][:, c, :], g[m % 2][:], h_hi[layer][:, c, :].bitcast(F32), ALU.subtract
                                  ).then_inc(h_ready.sem, 1)

            def rows_low(t):
                for c in range(KC):
                    dve.wait_ge(x_hi_ready, t * KC + c + 1)
                    dve.tensor_tensor(x_lo[:, c, :], tp[c][:, 0:T], x_hi[:, c, :].bitcast(F32), ALU.subtract
                                      ).then_inc(x_ready, 1)

            for c in range(KC):
                low(c, c, c)
            rows_low(0)
            with dve.Fori(0, J) as t:
                for i in range(4):
                    chunk(t, i)
                for m in range(HC):
                    rest(t, m)
                    if m % 2 == 0:
                        chunk(t, 4 + m // 2)
                for i in range(HC, CH):
                    chunk(t, i)
                for m in range(HC, HC + 4):
                    rest(t, m)
                rows_low(t + 1)
                for m in range(HC + 4, 2 * HC):
                    rest(t, m)
                dve.wait_ge(y_turned, t + 1)
                y_free.wait(dve, t)
                for s in range(TS):
                    ins = dve.tensor_copy(y_rows[:, s, :], yp[s // 2][:, s % 2, :])
                ins.then_inc(y_moved.sem, 1)


def stage_gather(nc, x1s, ys, pos_s, gate, gamma, wq, null_kv, x2s, q1s, null_s):
    with Space(nc, "g") as sp:
        neg_scale = -float(D1) ** -0.5
        QC = I1 // P
        w_raw = sp.sb("w_raw", [P, KC, I1])
        w_hi, w_lo = sp.sb("w_hi", [P, KC, I1], F32R), sp.sb("w_lo", [P, KC, I1], F32R)
        half_g, g_raw, gamma_row = sp.sb("half_g", [P, 1]), sp.sb("g_raw", [P, 1]), sp.sb("gamma_row", [P, D])
        tanh_g = sp.sb("tanh_g", [P, 1])
        eps, ident = sp.sb("eps", [P, 1]), sp.sb("ident", [P, P])
        nk_col = sp.sb("nk_col", [P, 1])
        nk, nk_hi, nk_lo = sp.sb("nk", [P, QC, H1]), sp.sb("nk_hi", [P, QC, H1], F32R), sp.sb("nk_lo", [P, QC, H1], F32R)
        pos = sp.sb("pos", [P, TOP, NB], I32)
        xin = sp.sb("xin", [P, B, QT, D])
        yg = [sp.sb(f"yg{i}", [P, TOP, QT, D]) for i in range(B)]
        tmp, xn = sp.sb("tmp", [P, QT, D]), sp.sb("xn", [P, QT, D])
        t_hi, t_lo = sp.sb("t_hi", [P, KC, NT], F32R), sp.sb("t_lo", [P, KC, NT], F32R)
        q_hi, q_lo = sp.sb("q_hi", [P, QC, NT], F32R), sp.sb("q_lo", [P, QC, NT], F32R)
        sn = sp.sb("sn", [P, H1, QT])
        tp = [sp.ps(f"tp{i}", [P, NT]) for i in range(KC)]
        bank = [sp.ps(f"bank{i}", [P, NT]) for i in range(QC)]
        sn_ps = sp.ps("sn_ps", [P, QT, H1])
        norm_a, norm_b = Norm(sp, "norm_a"), Norm(sp, "norm_b")
        loaded, x_loaded, pos_loaded, made = sp.sem("loaded"), sp.sem("x_loaded"), sp.sem("pos_loaded"), sp.sem("made")
        gathered = [sp.sem(f"gathered{i}") for i in range(B)]
        w_hi_ready, w_ready, nk_ready = sp.sem("w_hi_ready"), sp.sem("w_ready"), sp.sem("nk_ready")
        xn_ready, turned, t_hi_ready, t_ready = (sp.sem(n) for n in ("xn_ready", "turned", "t_hi_ready", "t_ready"))
        full, q_hi_ready, q_ready, n_scored = (sp.sem(n) for n in ("full", "q_hi_ready", "q_ready", "n_scored"))
        x2_ready, sn_ready, stored, own = sp.sem("x2_ready"), sp.sem("sn_ready"), sp.sem("stored"), sp.sem("own")
        block = sp.block()

        @block.gpsimd
        def _(pool):
            pool.memset(eps[:], EPS).then_inc(made, 1)
            pool.memset(ident[:], 0.0).then_inc(made, 1)
            pool.wait_ge(made, 2)
            pool.affine_select(out=ident[:], in_=ident[:], compare_op=ALU.not_equal, fill=1.0, base=0,
                               pattern=[[-1, P]], channel_multiplier=1).then_inc(made, 1)
            pool.wait_ge(pos_loaded, 16)
            for b in range(B):
                for s in range(QT):
                    for k in range(TOP):
                        t = b * QT + s
                        pool.indirect_dma_start(yg[b][:, k, s, :], None, ys,
                                                bass.IndirectOffsetOnAxis(ap=pos[:, k, t:t + 1], axis=0)
                                                ).then_inc(gathered[b], 16)

        @block.sync
        def _(sync):
            sync.dma_start(pos[:], pos_s).then_inc(pos_loaded, 16)
            sync.dma_start(w_raw[:], wq.rearrange("(c p) n -> p c n", p=P)).then_inc(loaded, 16)
            sync.dma_start(g_raw[:], row_of(gate, 2)[:, 0:1]).then_inc(loaded, 16)
            sync.dma_start(gamma_row[:], row_of(gamma, D)).then_inc(loaded, 16)
            for e in range(2):
                sync.dma_start(nk_col[e * D1:(e + 1) * D1, :], null_kv[0, :].rearrange("(d a) -> d a", a=1),
                               allow_slow_non_contiguous=True).then_inc(loaded, 16)
            sync.dma_start(xin[:], x1s.rearrange("b (s p) d -> p b s d", p=P)).then_inc(x_loaded, 16)
            for b in range(B):
                sync.wait_ge(q_ready, QC * (b + 1))
                for part, src in ((0, q_hi), (1, q_lo)):
                    sync.dma_start(q1s[part, b].rearrange("(c p) t -> p c t", p=P),
                                   src[:].bitcast(F32)).then_inc(stored, 16)
                sync.wait_ge(sn_ready, b + 1)
                sync.dma_start(null_s[b], sn[:]).then_inc(stored, 16)
                if b == B - 1:
                    sync.wait_ge(x2_ready, B)
                    sync.dma_start(x2s.rearrange("b (s p) d -> p b s d", p=P), xin[:]).then_inc(stored, 16)
            sync.wait_ge(stored, 48 * B + 16)

        @block.tensor
        def _(pe):
            pe.wait_ge(made, 3)
            pe.wait_ge(w_ready, KC)
            pe.wait_ge(nk_ready, 4)
            for b in range(B):
                pe.wait_ge(xn_ready, b + 1)
                for c in range(KC):
                    for s in range(QT):
                        ins = pe.transpose(tp[c][:, s * P:(s + 1) * P], xn[:, s, c * P:(c + 1) * P], ident[:])
                    ins.then_inc(turned, 1)
                pe.wait_ge(t_ready, KC * (b + 1))
                for j in range(QC):
                    if b:
                        pe.wait_ge(q_ready, QC * (b - 1) + j + 1)
                    product3(pe, bank[j][:], [((w_hi[:, c, j * P:(j + 1) * P], w_lo[:, c, j * P:(j + 1) * P]),
                                               (t_hi[:, c, :], t_lo[:, c, :])) for c in range(KC)]).then_inc(full, 1)
                pe.wait_ge(q_ready, QC * (b + 1))
                if b:
                    pe.wait_ge(sn_ready, b)
                for s in range(QT):
                    ins = product3(pe, sn_ps[:, s, :], [((q_hi[:, c, s * P:(s + 1) * P], q_lo[:, c, s * P:(s + 1) * P]),
                                                         (nk_hi[:, c, :], nk_lo[:, c, :])) for c in range(QC)])
                ins.then_inc(n_scored, 1)

        @block.scalar
        def _(act):
            act.wait_ge(loaded, 80)
            for c in range(KC):
                act.activation(w_hi[:, c, :], w_raw[:, c, :], ACT.Copy, scale=neg_scale).then_inc(w_hi_ready, 1)
            act.activation(tanh_g[:], g_raw[:], ACT.Tanh).then_inc(w_hi_ready, 1)
            act.wait_ge(w_hi_ready, KC + 1)
            act.activation(half_g[:], tanh_g[:], ACT.Copy, scale=1.0 / TOP).then_inc(w_hi_ready, 1)
            act.wait_ge(made, 3)
            for b in range(B):
                norm_a.scalar(act, b, eps[:])
                norm_b.scalar(act, b, eps[:])
                for c in range(KC):
                    act.wait_ge(turned, KC * b + c + 1)
                    act.activation(t_hi[:, c, :], tp[c][:], ACT.Copy).then_inc(t_hi_ready, 1)
                if b:
                    act.wait_ge(stored, 48 * b)
                    act.wait_ge(n_scored, b)
                for j in range(QC):
                    act.wait_ge(full, QC * b + j + 1)
                    act.activation(q_hi[:, j, :], bank[j][:], ACT.Copy).then_inc(q_hi_ready, 1)

        @block.vector
        def _(dve):
            steps = Steps(dve, own)
            dve.memset(nk[:], 0.0).then_inc(nk_ready, 1)
            dve.wait_ge(nk_ready, 1)
            dve.wait_ge(loaded, 80)
            for h in range(H1):
                rows = slice((h % 2) * D1, (h % 2 + 1) * D1)
                ins = dve.tensor_copy(nk[rows, h // 2, h:h + 1], nk_col[rows, :])
                steps.did(ins)
            steps.wait()
            dve.tensor_copy(nk_hi[:], nk[:]).then_inc(nk_ready, 1)
            dve.wait_ge(nk_ready, 2)
            dve.tensor_tensor(nk_lo[:], nk[:], nk_hi[:].bitcast(F32), ALU.subtract).then_inc(nk_ready, 2)
            for c in range(KC):
                dve.wait_ge(w_hi_ready, c + 1)
                dve.scalar_tensor_tensor(w_lo[:, c, :], w_raw[:, c, :], neg_scale, w_hi[:, c, :].bitcast(F32),
                                         ALU.mult, ALU.subtract).then_inc(w_ready, 1)
            dve.wait_ge(w_hi_ready, KC + 2)
            dve.wait_ge(x_loaded, 16)
            for b in range(B):
                dve.wait_ge(gathered[b], 16 * TOP * QT)
                steps.link(dve.tensor_tensor(tmp[:], yg[b][:, 0], yg[b][:, 1], ALU.add))
                dve.scalar_tensor_tensor(xin[:, b], tmp[:], half_g[:, 0:1], xin[:, b], ALU.mult, ALU.add
                                         ).then_inc(x2_ready, 1)
                dve.wait_ge(x2_ready, b + 1)
                if b:
                    dve.wait_ge(turned, KC * b)
                norm_a.vector(dve, steps, b, [xin[:, b, s, :] for s in range(QT)], [xn[:, s, :] for s in range(QT)])
                steps.wait()
                norm_b.vector(dve, steps, b, [xn[:, s, :] for s in range(QT)], [xn[:, s, :] for s in range(QT)],
                              gamma_row[:])
                dve.sem_inc(xn_ready, 1)
                for c in range(KC):
                    dve.wait_ge(t_hi_ready, KC * b + c + 1)
                    dve.tensor_tensor(t_lo[:, c, :], tp[c][:], t_hi[:, c, :].bitcast(F32),
                                      ALU.subtract).then_inc(t_ready, 1)
                for j in range(QC):
                    dve.wait_ge(q_hi_ready, QC * b + j + 1)
                    dve.tensor_tensor(q_lo[:, j, :], bank[j][:], q_hi[:, j, :].bitcast(F32), ALU.subtract
                                      ).then_inc(q_ready, 1)
                dve.wait_ge(n_scored, b + 1)
                if b:
                    dve.wait_ge(stored, 48 * b)
                dve.tensor_copy(sn[:].rearrange("p h t -> p t h"), sn_ps[:]).then_inc(sn_ready, 1)


def stage_final(nc, x2s, o1s, wo, out_gamma, gates, gate2, wg, bg, we, be, out):
    with Space(nc, "f") as sp:
        OC = I1 // P
        EW = E * D
        WN = OC * D + KC * D + KC * EW
        w_raw = [sp.sb(f"w_raw{i}", [P, EW]) for i in range(2)]
        w_hi, w_lo = sp.sb("w_hi", [P, WN], F32R), sp.sb("w_lo", [P, WN], F32R)
        g_raw, tanh_g = sp.sb("g_raw", [P, 2]), sp.sb("tanh_g", [P, 2])
        gamma_row, bg_row, be_sb = sp.sb("gamma_row", [P, D]), sp.sb("bg_row", [P, D]), sp.sb("be_sb", [E, D])
        eps, ident, iota_e = sp.sb("eps", [P, 1]), sp.sb("ident", [P, P]), sp.sb("iota_e", [P, E])
        xin = sp.sb("xin", [P, B, QT, D])
        ot = [sp.sb(f"ot{i}", [P, OC, NT]) for i in range(2)]
        ot_hi, ot_lo = sp.sb("ot_hi", [P, OC, NT], F32R), sp.sb("ot_lo", [P, OC, NT], F32R)
        att, xn = sp.sb("att", [P, QT, D]), sp.sb("xn", [P, QT, D])
        t_hi, t_lo = sp.sb("t_hi", [P, KC, NT], F32R), sp.sb("t_lo", [P, KC, NT], F32R)
        logits, probs = sp.sb("logits", [P, QT, D]), sp.sb("probs", [P, QT, D])
        top, top_i = sp.sb("top", [P, QT, 8]), sp.sb("top_i", [P, QT, 8], U32)
        neg_max, total, weight = sp.sb("neg_max", [P, QT]), sp.sb("total", [P, QT]), sp.sb("weight", [P, QT])
        e_i, e_f, hot = sp.sb("e_i", [P, QT], U32), sp.sb("e_f", [P, QT]), sp.sb("hot", [P, QT, E])
        hot_t = sp.sb("hot_t", [E, QT, P])
        acc, res = sp.sb("acc", [P, QT, D]), sp.sb("res", [P, QT, D])
        ex = [sp.ps(f"ex{i}", [P, 2, D]) for i in range(4)]
        tp = [sp.ps(f"tp{i}", [P, NT]) for i in range(KC)]
        lg = [sp.ps(f"lg{i}", [P, 2, D]) for i in range(2)]
        norms = [Norm(sp, f"norm{i}") for i in range(3)]
        loaded, x_loaded, made = sp.sem("loaded"), sp.sem("x_loaded"), sp.sem("made")
        w_loaded = [sp.sem(f"w_loaded{i}") for i in range(2)]
        o_loaded = [sp.sem(f"o_loaded{i}") for i in range(2)]
        w_hi_ready, w_ready, tanh_ready = sp.sem("w_hi_ready"), sp.sem("w_ready"), sp.sem("tanh_ready")
        o_hi_ready, o_ready, projected, att_ready = (sp.sem(n) for n in ("o_hi_ready", "o_ready", "projected", "att_ready"))
        xn_ready, turned, t_hi_ready, t_ready = (sp.sem(n) for n in ("xn_ready", "turned", "t_hi_ready", "t_ready"))
        gated, max_ready, exped, hot_ready = (sp.sem(n) for n in ("gated", "max_ready", "exped", "hot_ready"))
        hot_turned, hot_moved, be_ready, acc_ready = (sp.sem(n) for n in ("hot_turned", "hot_moved", "be_ready", "acc_ready"))
        ex_full, ex_read, res_ready, stored, own = (sp.sem(n) for n in ("ex_full", "ex_read", "res_ready", "stored", "own"))
        WO, WG, WE = 0, OC * D, OC * D + KC * D
        pieces = [(WO, OC * D, wo.rearrange("(c p) n -> p c n", p=P), OC),
                  (WG, KC * D, wg.rearrange("(c p) n -> p c n", p=P), KC)]
        for c in range(KC):
            pieces.append((WE + c * EW, EW, we[:, c * P:(c + 1) * P, :].rearrange("e p n -> p e n"), E))
        block = sp.block()

        @block.gpsimd
        def _(pool):
            pool.memset(eps[:], EPS).then_inc(made, 1)
            pool.memset(ident[:], 0.0).then_inc(made, 1)
            pool.wait_ge(made, 2)
            pool.affine_select(out=ident[:], in_=ident[:], compare_op=ALU.not_equal, fill=1.0, base=0,
                               pattern=[[-1, P]], channel_multiplier=1).then_inc(made, 1)
            pool.iota(iota_e[:], [[1, E]], base=0, channel_multiplier=0,
                      allow_small_or_imprecise_dtypes=True).then_inc(made, 1)

        @block.sync
        def _(sync):
            for i, (at, n, src, c) in enumerate(pieces):
                if i >= 2:
                    sync.wait_ge(w_ready, i - 1)
                sync.dma_start(w_raw[i % 2][:, 0:n].rearrange("p (c n) -> p c n", c=c), src).then_inc(w_loaded[i % 2], 16)
                if i == 0:
                    sync.dma_start(ot[0][:], o1s[0].rearrange("(c p) t -> p c t", p=P)).then_inc(o_loaded[0], 16)
                    sync.dma_start(g_raw[:, 0:1], row_of(gates, 2)[:, 1:2]).then_inc(loaded, 16)
                    sync.dma_start(g_raw[:, 1:2], row_of(gate2, 2)[:, 1:2]).then_inc(loaded, 16)
                    sync.dma_start(gamma_row[:], row_of(out_gamma, D)).then_inc(loaded, 16)
                    sync.dma_start(bg_row[:], row_of(bg, D)).then_inc(loaded, 16)
                    sync.dma_start(be_sb[:], be).then_inc(loaded, 16)
                    sync.dma_start(xin[:], x2s.rearrange("b (s p) d -> p b s d", p=P)).then_inc(x_loaded, 16)
            for b in range(1, B):
                if b >= 2:
                    sync.wait_ge(o_ready, b - 1)
                sync.dma_start(ot[b % 2][:], o1s[b].rearrange("(c p) t -> p c t", p=P)).then_inc(o_loaded[b % 2], 16)
            for b in range(B):
                sync.wait_ge(res_ready, b + 1)
                sync.dma_start(out[b].rearrange("(s p) d -> p s d", p=P), res[:]).then_inc(stored, 16)
            sync.wait_ge(stored, 16 * B)

        @block.tensor
        def _(pe):
            pe.wait_ge(made, 4)
            for b in range(B):
                if b == 0:
                    pe.wait_ge(w_ready, 1)
                pe.wait_ge(o_ready, b + 1)
                if b:
                    pe.wait_ge(ex_read, 4 * E * b)
                for s in range(QT):
                    ins = product3(pe, ex[s // 2][:, s % 2, :],
                                   [((ot_hi[:, c, s * P:(s + 1) * P], ot_lo[:, c, s * P:(s + 1) * P]),
                                     (w_hi[:, WO + c * D:WO + (c + 1) * D], w_lo[:, WO + c * D:WO + (c + 1) * D]))
                                    for c in range(OC)])
                ins.then_inc(projected, 1)
                pe.wait_ge(xn_ready, b + 1)
                for c in range(KC):
                    for s in range(QT):
                        ins = pe.transpose(tp[c][:, s * P:(s + 1) * P], xn[:, s, c * P:(c + 1) * P], ident[:])
                    ins.then_inc(turned, 1)
                pe.wait_ge(t_ready, KC * (b + 1))
                if b == 0:
                    pe.wait_ge(w_ready, len(pieces))

                def stat(s):
                    return [(t_hi[:, c, s * P:(s + 1) * P], t_lo[:, c, s * P:(s + 1) * P]) for c in range(KC)]
                for s in range(QT):
                    ins = product3(pe, lg[s // 2][:, s % 2, :],
                                   [(stat(s)[c], (w_hi[:, WG + c * D:WG + (c + 1) * D],
                                                  w_lo[:, WG + c * D:WG + (c + 1) * D])) for c in range(KC)])
                ins.then_inc(gated, 1)

                def experts(s):
                    for i in range(4):
                        if s:
                            pe.wait_ge(ex_read, 4 * E * b + E * (s - 1) + 2 * (i + 1))
                        cols = [slice(WE + c * EW + i * NT, WE + c * EW + (i + 1) * NT) for c in range(KC)]
                        product3(pe, ex[i][:].rearrange("p a n -> p (a n)"),
                                 [(stat(s)[c], (w_hi[:, cols[c]], w_lo[:, cols[c]])) for c in range(KC)]
                                 ).then_inc(ex_full, 1)
                pe.wait_ge(att_ready, b + 1)
                experts(0)
                pe.wait_ge(hot_ready, b + 1)
                for s in range(QT):
                    ins = pe.transpose(tp[0][0:E, s * P:(s + 1) * P], hot[:, s, :], ident[:])
                ins.then_inc(hot_turned, 1)
                pe.wait_ge(hot_moved, b + 1)
                for s in range(QT):
                    ins = pe.matmul(lg[s // 2][:, s % 2, :], hot_t[:, s, :], be_sb[:], start=True, stop=True)
                ins.then_inc(be_ready, 1)
                for s in range(1, QT):
                    experts(s)

        @block.scalar
        def _(act):
            act.wait_ge(made, 4)
            for i, (at, n, src, c) in enumerate(pieces):
                act.wait_ge(w_loaded[i % 2], 16 * (i // 2 + 1))
                act.activation(w_hi[:, at:at + n], w_raw[i % 2][:, 0:n], ACT.Copy).then_inc(w_hi_ready, 1)
                if i == 0:
                    act.wait_ge(o_loaded[0], 16)
                    act.activation(ot_hi[:], ot[0][:], ACT.Copy).then_inc(o_hi_ready, 1)
            act.wait_ge(loaded, 80)
            act.activation(tanh_g[:], g_raw[:], ACT.Tanh).then_inc(tanh_ready, 1)
            for b in range(B):
                if b:
                    act.wait_ge(o_loaded[b % 2], 16 * (b // 2 + 1))
                    act.wait_ge(projected, b)
                    act.activation(ot_hi[:], ot[b % 2][:], ACT.Copy).then_inc(o_hi_ready, 1)
                for norm in norms[:2]:
                    norm.scalar(act, b, eps[:])
                for c in range(KC):
                    act.wait_ge(turned, KC * b + c + 1)
                    act.activation(t_hi[:, c, :], tp[c][:], ACT.Copy).then_inc(t_hi_ready, 1)
                act.wait_ge(max_ready, b + 1)
                for s in range(QT):
                    act.activation(probs[:, s, :], logits[:, s, :], ACT.Exp, bias=neg_max[:, s:s + 1],
                                   accum_out=total[:, s:s + 1]).then_inc(exped, 1)
                act.wait_ge(hot_turned, b + 1)
                act.activation(hot_t[:].rearrange("e s p -> e (s p)"), tp[0][0:E, :], ACT.Copy).then_inc(hot_moved, 1)
                act.wait_ge(be_ready, b + 1)
                for i in range(2):
                    act.activation(acc[:, 2 * i:2 * i + 2, :], lg[i][:], ACT.Copy).then_inc(acc_ready, 1)

        @block.vector
        def _(dve):
            steps = Steps(dve, own)

            def split_o(b):
                dve.wait_ge(o_hi_ready, b + 1)
                dve.tensor_tensor(ot_lo[:], ot[b % 2][:], ot_hi[:].bitcast(F32), ALU.subtract).then_inc(o_ready, 1)
            for i, (at, n, src, c) in enumerate(pieces):
                dve.wait_ge(w_hi_ready, i + 1)
                dve.tensor_tensor(w_lo[:, at:at + n], w_raw[i % 2][:, 0:n], w_hi[:, at:at + n].bitcast(F32),
                                  ALU.subtract).then_inc(w_ready, 1)
                if i == 0:
                    split_o(0)
            dve.wait_ge(x_loaded, 16)
            dve.wait_ge(tanh_ready, 1)
            tiles = range(QT)
            for b in range(B):
                if b:
                    split_o(b)
                dve.wait_ge(projected, b + 1)
                norms[0].vector(dve, steps, b, [ex[s // 2][:, s % 2, :] for s in tiles], [att[:, s, :] for s in tiles],
                                gamma_row[:])
                steps.link(dve.scalar_tensor_tensor(xin[:, b], att[:], tanh_g[:, 0:1], xin[:, b], ALU.mult, ALU.add))
                dve.sem_inc(att_ready, 1)
                norms[1].vector(dve, steps, b, [xin[:, b, s, :] for s in tiles], [xn[:, s, :] for s in tiles])
                dve.sem_inc(xn_ready, 1)
                for c in range(KC):
                    dve.wait_ge(t_hi_ready, KC * b + c + 1)
                    dve.tensor_tensor(t_lo[:, c, :], tp[c][:], t_hi[:, c, :].bitcast(F32),
                                      ALU.subtract).then_inc(t_ready, 1)
                dve.wait_ge(gated, b + 1)
                for i in range(2):
                    ins = dve.tensor_tensor(logits[:, 2 * i:2 * i + 2, :], lg[i][:],
                                            bg_row[:].unsqueeze(1).broadcast_to([P, 2, D]), ALU.add)
                steps.link(ins)
                steps.link(dve.tensor_reduce(neg_max[:], logits[:], AX.X, ALU.max))
                dve.tensor_scalar(neg_max[:], neg_max[:], -1.0, None, ALU.mult).then_inc(max_ready, 1)
                for s in tiles:
                    dve.wait_ge(exped, QT * b + s + 1)
                    ins = dve.max(top[:, s, :], probs[:, s, :])
                steps.link(ins)
                for s in tiles:
                    ins = dve.max_index(top_i[:, s, :], top[:, s, :], probs[:, s, :])
                steps.link(ins)
                steps.link(dve.tensor_scalar(e_i[:], top_i[:, :, 0], E - 1, None, ALU.bitwise_and))
                steps.link(dve.tensor_copy(e_f[:], e_i[:]))
                dve.tensor_tensor(hot[:], iota_e[:].unsqueeze(1).broadcast_to([P, QT, E]),
                                  e_f[:].unsqueeze(2).broadcast_to([P, QT, E]), ALU.is_equal).then_inc(hot_ready, 1)
                steps.link(dve.reciprocal(weight[:], total[:]))
                steps.link(dve.tensor_scalar(weight[:], weight[:], tanh_g[:, 1:2], None, ALU.mult))
                dve.wait_ge(hot_ready, b + 1)
                dve.wait_ge(acc_ready, 2 * (b + 1))
                if b:
                    dve.wait_ge(stored, 16 * b)
                for s in tiles:
                    for e in range(E):
                        dve.wait_ge(ex_full, 4 * (QT * b + s) + e // 2 + 1)
                        ins = dve.scalar_tensor_tensor(acc[:, s, :], ex[e // 2][:, e % 2, :], hot[:, s, e:e + 1],
                                                       acc[:, s, :], ALU.mult, ALU.add)
                        ins.then_inc(ex_read, 1)
                        dve.wait_ge(ex_read, E * (QT * b + s) + e + 1)
                    steps.link(dve.tensor_scalar(acc[:, s, :], acc[:, s, :], 0.0, weight[:, s:s + 1], ALU.max, ALU.mult))
                    ins = dve.tensor_tensor(res[:, s, :], acc[:, s, :], xin[:, b, s, :], ALU.add)
                ins.then_inc(res_ready, 1)


INPUTS = ["x", "ctx_1024", "mask_Bx1xSxS2_ik1", "mask_BxS2_bf1", "g_xattn", "g_ffn",
          "L0_xattn_wq", "L0_xattn_bq", "L0_xattn_wk", "L0_xattn_bk", "L0_xattn_wv", "L0_xattn_bv", "L0_xattn_wo",
          "L0_xattn_bo", "L0_ffn_expert_tokens", "L0_ffn_W1", "L0_ffn_b1", "L0_ffn_W2", "L0_ffn_b2", "L0_ffn_W3",
          "L0_ffn_b3", "L1_xattn_gamma", "L1_xattn_w_q", "L1_xattn_w_kv", "L1_xattn_null_kv", "L1_xattn_w_out",
          "L1_xattn_out_gamma", "L1_ffn_Wg", "L1_ffn_bg", "L1_ffn_We", "L1_ffn_be"]


def build(nc, a, out):
    def scratch(name, shape, dt=F32):
        return nc.dram_tensor(name, shape, dt).ap()

    k0s, v0s = scratch("k0s", (2, B, D, CTX)), scratch("v0s", (B, CTX, D))
    k1s, v1s = scratch("k1s", (2, B, I1, CTX)), scratch("v1s", (B, CTX, I1))
    bias0, bias1 = scratch("bias0", (B, S, CTX), BF16), scratch("bias1", (B, CTX), BF16)
    q0s, q1s = scratch("q0s", (2, B, D, S)), scratch("q1s", (2, B, I1, S))
    o0s, o1s = scratch("o0s", (B, D, S)), scratch("o1s", (B, I1, S))
    x1s, x2s = scratch("x1s", (B, S, D)), scratch("x2s", (B, S, D))
    xgs, ys = scratch("xgs", (SLOTS + T, D)), scratch("ys", (SLOTS, D))
    pos_s, tile_s = scratch("pos_s", (P, TOP, NB), I32), scratch("tile_s", (1, J + 2), I32)
    bias_s, null_s = scratch("bias_s", (E, P, BW)), scratch("null_s", (B, P, H1, QT))

    stage_context(nc, a["ctx_1024"], a["L0_xattn_wk"], a["L0_xattn_bk"], a["L0_xattn_wv"], a["L0_xattn_bv"],
                  a["L1_xattn_w_kv"], a["mask_Bx1xSxS2_ik1"].rearrange("b a q k -> (b a) q k"), a["mask_BxS2_bf1"],
                  k0s, v0s, k1s, v1s, bias0, bias1)
    stage_queries(nc, a["x"], a["L0_xattn_wq"], a["L0_xattn_bq"], q0s)
    stage_attention(nc, "a0", H0, D0, P // D0, q0s, k0s, v0s, o0s, bias0)
    stage_route(nc, a["x"], o0s, a["L0_xattn_wo"], a["L0_xattn_bo"], a["g_xattn"], a["L0_ffn_expert_tokens"],
                a["L0_ffn_b1"], a["L0_ffn_b2"], a["L0_ffn_b3"], x1s, xgs, pos_s, tile_s, bias_s)
    stage_experts(nc, xgs, tile_s, bias_s, a["L0_ffn_W1"], a["L0_ffn_W2"], a["L0_ffn_W3"], ys)
    stage_gather(nc, x1s, ys, pos_s, a["g_ffn"], a["L1_xattn_gamma"], a["L1_xattn_w_q"], a["L1_xattn_null_kv"],
                 x2s, q1s, null_s)
    stage_attention(nc, "a1", H1, D1, P // D1, q1s, k1s, v1s, o1s, bias1, null_s, a["L1_xattn_null_kv"])
    stage_final(nc, x2s, o1s, a["L1_xattn_w_out"], a["L1_xattn_out_gamma"], a["g_xattn"], a["g_ffn"],
                a["L1_ffn_Wg"], a["L1_ffn_bg"], a["L1_ffn_We"], a["L1_ffn_be"], out)


def kernel(**inputs):
    import numpy as _np
    import concourse.bacc as _bacc
    from concourse import mybir as _mybir
    from concourse.bass_utils import run_bass_kernel_spmd as _run

    nc = _bacc.Bacc("TRN2", target_bir_lowering=False, num_devices=1)
    arrays, args = {}, {}
    for name in INPUTS:
        a = _np.ascontiguousarray(inputs[name])
        if a.dtype == bool:
            a = a.view(_np.uint8)
        arrays[f"in_{name}_dram"] = a
        args[name] = nc.dram_tensor(f"in_{name}_dram", a.shape, _mybir.dt.from_np(a.dtype), kind="ExternalInput").ap()
    out = nc.dram_tensor("out_0_dram", (B, S, D), F32, kind="ExternalOutput").ap()
    build(nc, args, out)
    r = _run(nc, [arrays], core_ids=[0])
    return r.results[0]["out_0_dram"]
```

```python
from contextlib import ExitStack

import numpy as np

import concourse.bass as bass
import concourse.mybir as mybir
from concourse.alu_op_type import AluOpType as ALU

F32 = mybir.dt.float32
F32R = mybir.dt.float32r
BF16 = mybir.dt.bfloat16
I32 = mybir.dt.int32
U32 = mybir.dt.uint32
U8 = mybir.dt.uint8
ACT = mybir.ActivationFunctionType
AX = mybir.AxisListType

P = 128
B, S, D, CTX = 4, 512, 256, 1024
N = B * S
KC = D // P
NT = 512
QT = S // P
KT = CTX // P
H0, D0 = 16, 16
H1, D1 = 8, 64
I1 = H1 * D1
E, HID = 8, 1024
EPS = 1e-5
BIG = 3e38


class Steps:

    def __init__(self, eng, sem, per=0, rnd=0):
        self.eng, self.sem, self.per, self.rnd, self.n = eng, sem, per, rnd, 0

    def did(self, ins):
        self.n += 1
        ins.then_inc(self.sem, 1)

    def wait(self):
        self.eng.wait_ge(self.sem, self.rnd * self.per + self.n)

    def link(self, ins):
        self.did(ins)
        self.wait()

    def close(self):
        assert self.n == self.per, (self.n, self.per)


class Space:

    def __init__(self, nc, tag):
        self.nc, self.tag, self.ctx, self.sems = nc, tag, ExitStack(), []

    def __enter__(self):
        return self

    def __exit__(self, *a):
        self.ctx.__exit__(*a)
        if a[0] is None:
            self.nc.clear_and_free_semaphores(self.sems)
            self.nc.all_engine_barrier()

    def sb(self, name, shape, dt=F32):
        return self.ctx.enter_context(self.nc.sbuf_tensor(f"{self.tag}_{name}", shape, dt))

    def ps(self, name, shape, dt=F32):
        return self.ctx.enter_context(self.nc.psum_tensor(f"{self.tag}_{name}", shape, dt))

    def sem(self, name):
        self.sems.append(self.nc.alloc_semaphore(f"{self.tag}_{name}"))
        return self.sems[-1]

    def block(self):
        return self.ctx.enter_context(self.nc.Block())


def apart(eng, spare):
    eng.sem_inc(spare, 1)


def product3(pe, out, pairs, start=True, stop=True):
    n = 3 * len(pairs)
    k = 0
    for (s_hi, s_lo), (m_hi, m_lo) in pairs:
        for s, m in ((s_hi, m_hi), (s_hi, m_lo), (s_lo, m_hi)):
            ins = pe.matmul(out, s, m, start=start and k == 0, stop=stop and k == n - 1)
            k += 1
    return ins


def row_of(vec, n):
    return vec.rearrange("(a n) -> a n", a=1).broadcast_to([P, n])


def make_identity(pool, sp, ident, made):
    pool.memset(ident[:], 0.0).then_inc(made, 1)
    pool.wait_ge(made, 1)
    pool.affine_select(out=ident[:], in_=ident[:], compare_op=ALU.not_equal, fill=1.0, base=0,
                       pattern=[[-1, P]], channel_multiplier=1).then_inc(made, 1)


def stage_context(nc, ctx, wk, bk, wv, bv, wkv, mask0, mask1, k0s, v0s, k1s, v1s, bias0, bias1):
    with Space(nc, "c") as sp:
        W = D + D + 2 * I1
        w_raw = sp.sb("w_raw", [P, KC, W])
        w_hi = sp.sb("w_hi", [P, KC, W], F32R)
        w_lo = sp.sb("w_lo", [P, KC, W], F32R)
        bk_col = sp.sb("bk_col", [P, KC])
        bv_row = sp.sb("bv_row", [P, D])
        ident = sp.sb("ident", [P, P])
        rows = [sp.sb(f"rows{i}", [P, QT, D]) for i in range(2)]
        t_hi = [sp.sb(f"t_hi{i}", [P, KC, NT], F32R) for i in range(2)]
        t_lo = [sp.sb(f"t_lo{i}", [P, KC, NT], F32R) for i in range(2)]
        k_hi = [sp.sb(f"k_hi{i}", [P, 6, NT], F32R) for i in range(2)]
        k_lo = [sp.sb(f"k_lo{i}", [P, 6, NT], F32R) for i in range(2)]
        v1_st = [sp.sb(f"v1_st{i}", [P, QT, I1]) for i in range(2)]
        v0_st = [sp.sb(f"v0_st{i}", [P, QT, D]) for i in range(2)]
        m_raw = [sp.sb(f"m_raw{i}", [P, CTX], I32) for i in range(2)]
        m_bias = [sp.sb(f"m_bias{i}", [P, CTX], BF16) for i in range(2)]
        m1_raw, m1_bias = sp.sb("m1_raw", [B, CTX], U8), sp.sb("m1_bias", [B, CTX], BF16)
        tp = [sp.ps(f"tp{i}", [P, NT]) for i in range(KC)]
        bank = [sp.ps(f"bank{i}", [P, NT]) for i in range(6)]

        w_loaded, made = sp.sem("w_loaded"), sp.sem("made")
        w_hi_ready, w_ready = sp.sem("w_hi_ready"), sp.sem("w_ready")
        rows_loaded = [sp.sem(f"rows_loaded{i}") for i in range(2)]
        rows_free = sp.sem("rows_free")
        turned, t_hi_ready, t_ready = sp.sem("turned"), sp.sem("t_hi_ready"), sp.sem("t_ready")
        bank_full, act_free, dve_free = sp.sem("bank_full"), sp.sem("act_free"), sp.sem("dve_free")
        k_hi_ready = sp.sem("k_hi_ready")
        stored = [sp.sem(f"stored{i}") for i in range(2)]
        m_loaded = [sp.sem(f"m_loaded{i}") for i in range(2)]
        m_made, m_stored = sp.sem("m_made"), sp.sem("m_stored")
        m1_loaded, spare = sp.sem("m1_loaded"), sp.sem("spare")
        STORES = 6
        block = sp.block()

        @block.gpsimd
        def _(pool):
            make_identity(pool, sp, ident, made)
            pool.sem_inc(rows_free, 2)
            pool.wait_ge(m1_loaded, 16)
            pool.tensor_scalar(m1_bias[:], m1_raw[:], 0.0, BIG, ALU.is_equal, ALU.mult).then_inc(m_made, 1)
            with pool.Fori(0, B) as b:
                for half in range(2):
                    pool.wait_ge(rows_free, b * 2 + half + 1)
                    pool.dma_start(rows[half][:], ctx[b, half * NT:(half + 1) * NT, :].rearrange(
                        "(s p) d -> p s d", p=P)).then_inc(rows_loaded[half], 16)
                    for i in range(2):
                        n = (b * 2 + half) * 2 + i
                        pool.wait_ge(m_loaded[i], (b * 2 + half) * 16 + 16)
                        pool.wait_ge(m_stored, n * 16 + 16)
                        apart(pool, spare)
                        pool.tensor_scalar(m_bias[i][:], m_raw[i][:], 0.0, BIG, ALU.is_equal, ALU.mult
                                           ).then_inc(m_made, 1)

        @block.sync
        def _(sync):
            sync.dma_start(w_raw[:, :, 0:D], wk.rearrange("(c p) n -> p c n", p=P)).then_inc(w_loaded, 16)
            sync.dma_start(w_raw[:, :, D:2 * D], wv.rearrange("(c p) n -> p c n", p=P)).then_inc(w_loaded, 16)
            sync.dma_start(w_raw[:, :, 2 * D:], wkv.rearrange("(c p) n -> p c n", p=P)).then_inc(w_loaded, 16)
            sync.dma_start(bk_col[:], bk.rearrange("(c p) -> p c", p=P),
                           allow_slow_non_contiguous=True).then_inc(w_loaded, 16)
            sync.dma_start(bv_row[:], row_of(bv, D)).then_inc(w_loaded, 16)
            sync.dma_start(m1_raw[:], mask1).then_inc(m1_loaded, 16)
            sync.wait_ge(m_made, 1)
            sync.dma_start(bias1, m1_bias[:]).then_inc(m_stored, 16)
            with sync.Fori(0, B) as b:
                for half in range(2):
                    n = b * 2 + half
                    cols = slice(half * NT, (half + 1) * NT)
                    for i in range(2):
                        rows_m = slice((half * 2 + i) * P, (half * 2 + i + 1) * P)
                        sync.dma_start(m_raw[i][:], mask0[b, rows_m, :]).then_inc(m_loaded[i], 16)
                        sync.wait_ge(m_made, n * 2 + i + 2)
                        apart(sync, spare)
                        sync.dma_start(bias0[b, rows_m, :], m_bias[i][:]).then_inc(m_stored, 16)
                    sync.wait_ge(dve_free, n * 8 + 2 + 6)
                    for part, src in ((0, k_hi[half]), (1, k_lo[half])):
                        sync.dma_start(k0s[part, b, :, cols].rearrange("(c p) t -> p c t", p=P),
                                       src[:, 0:2, :].bitcast(F32)).then_inc(stored[half], 16)
                        sync.dma_start(k1s[part, b, :, cols].rearrange("(c p) t -> p c t", p=P),
                                       src[:, 2:6, :].bitcast(F32)).then_inc(stored[half], 16)
                    sync.wait_ge(act_free, n * 4 + 4 + 4)
                    sync.dma_start(v1s[b, cols, :].rearrange("(s p) n -> p s n", p=P),
                                   v1_st[half][:]).then_inc(stored[half], 16)
                    sync.wait_ge(dve_free, n * 8 + 2 + 8)
                    sync.dma_start(v0s[b, cols, :].rearrange("(s p) n -> p s n", p=P),
                                   v0_st[half][:]).then_inc(stored[half], 16)
            for half in range(2):
                sync.wait_ge(stored[half], 16 * STORES * B + 1)
            sync.wait_ge(m_stored, 16 * (1 + 2 * 2 * B))

        @block.tensor
        def _(pe):
            pe.wait_ge(made, 2)
            pe.wait_ge(w_ready, KC)
            with pe.Fori(0, B) as b:
                for half in range(2):
                    n = b * 2 + half
                    pe.wait_ge(rows_loaded[half], b * 16 + 16)
                    for c in range(KC):
                        for s in range(QT):
                            ins = pe.transpose(tp[c][:, s * P:(s + 1) * P], rows[half][:, s, c * P:(c + 1) * P],
                                               ident[:])
                        ins.then_inc(turned, 1)
                    pe.wait_ge(t_ready, n * KC + KC)
                    hi, lo = t_hi[half], t_lo[half]
                    for j in range(6):
                        col = j * P if j < 2 else 2 * D + (j - 2) * P
                        if j < 4:
                            pe.wait_ge(act_free, n * 4 + j + 1)
                        else:
                            pe.wait_ge(dve_free, n * 8 + (j - 4) + 1)
                        product3(pe, bank[j][:], [((w_hi[:, c, col:col + P], w_lo[:, c, col:col + P]),
                                                   (hi[:, c, :], lo[:, c, :])) for c in range(KC)]
                                 ).then_inc(bank_full, 1)
                    for s in range(QT):
                        pe.wait_ge(dve_free, n * 8 + 2 + s + 1)
                        product3(pe, bank[s][:], [((hi[:, c, s * P:(s + 1) * P], lo[:, c, s * P:(s + 1) * P]),
                                                   (w_hi[:, c, 2 * D + I1:], w_lo[:, c, 2 * D + I1:]))
                                                  for c in range(KC)]).then_inc(bank_full, 1)
                    for j in range(2):
                        pe.wait_ge(dve_free, n * 8 + 2 + 4 + j + 1)
                        for s in (2 * j, 2 * j + 1):
                            ins = product3(pe, bank[4 + j][:, (s % 2) * D:(s % 2 + 1) * D],
                                           [((hi[:, c, s * P:(s + 1) * P], lo[:, c, s * P:(s + 1) * P]),
                                             (w_hi[:, c, D:2 * D], w_lo[:, c, D:2 * D])) for c in range(KC)])
                        ins.then_inc(bank_full, 1)

        @block.scalar
        def _(act):
            act.wait_ge(w_loaded, 80)
            for c in range(KC):
                act.activation(w_hi[:, c, :], w_raw[:, c, :], ACT.Copy).then_inc(w_hi_ready, 1)
            act.sem_inc(act_free, 4)
            act.sem_inc(stored[0], 1)
            act.sem_inc(stored[1], 1)
            with act.Fori(0, B) as b:
                for half in range(2):
                    n = b * 2 + half
                    for c in range(KC):
                        act.wait_ge(turned, n * KC + c + 1)
                        act.activation(t_hi[half][:, c, :], tp[c][:], ACT.Copy).then_inc(t_hi_ready, 1)
                    act.wait_ge(stored[half], b * (16 * STORES) + 1)
                    for j in range(6):
                        act.wait_ge(bank_full, n * 12 + j + 1)
                        if j < 2:
                            ins = act.activation(k_hi[half][:, j, :], bank[j][:], ACT.Identity, bias=bk_col[:, j:j + 1])
                        else:
                            ins = act.activation(k_hi[half][:, j, :], bank[j][:], ACT.Copy)
                        ins.then_inc(k_hi_ready, 1)
                    for s in range(QT):
                        act.wait_ge(bank_full, n * 12 + 6 + s + 1)
                        act.activation(v1_st[half][:, s, :], bank[s][:], ACT.Copy).then_inc(act_free, 1)

        @block.vector
        def _(dve):
            dve.sem_inc(dve_free, 2)
            for c in range(KC):
                dve.wait_ge(w_hi_ready, c + 1)
                dve.tensor_tensor(w_lo[:, c, :], w_raw[:, c, :], w_hi[:, c, :].bitcast(F32),
                                  ALU.subtract).then_inc(w_ready, 1)
            with dve.Fori(0, B) as b:
                for half in range(2):
                    n = b * 2 + half
                    for c in range(KC):
                        dve.wait_ge(t_hi_ready, n * KC + c + 1)
                        dve.tensor_tensor(t_lo[half][:, c, :], tp[c][:], t_hi[half][:, c, :].bitcast(F32),
                                          ALU.subtract).then_inc(t_ready, 1)
                    dve.sem_inc(rows_free, 1)
                    dve.wait_ge(stored[half], b * (16 * STORES) + 1)
                    for j in range(6):
                        dve.wait_ge(k_hi_ready, n * 6 + j + 1)
                        if j < 2:
                            ins = dve.scalar_tensor_tensor(k_lo[half][:, j, :], bank[j][:], bk_col[:, j:j + 1],
                                                           k_hi[half][:, j, :].bitcast(F32), ALU.add, ALU.subtract)
                        else:
                            ins = dve.tensor_tensor(k_lo[half][:, j, :], bank[j][:],
                                                    k_hi[half][:, j, :].bitcast(F32), ALU.subtract)
                        ins.then_inc(dve_free, 1)
                    for j in range(2):
                        dve.wait_ge(bank_full, n * 12 + 10 + j + 1)
                        for s in range(2):
                            ins = dve.tensor_tensor(v0_st[half][:, 2 * j + s, :], bank[4 + j][:, s * D:(s + 1) * D],
                                                    bv_row[:], ALU.add)
                        ins.then_inc(dve_free, 1)


class Norm:

    def __init__(self, sp, tag):
        self.stats = sp.sb(f"{tag}_stats", [P, QT, 6])
        self.mv = sp.sb(f"{tag}_mv", [P, QT, 2])
        self.dev = sp.sb(f"{tag}_dev", [P, QT])
        self.rstd = sp.sb(f"{tag}_rstd", [P, QT])
        self.sums_ready, self.roots_ready = sp.sem(f"{tag}_sums_ready"), sp.sem(f"{tag}_roots_ready")

    def vector(self, dve, steps, rnd, src, dst, gamma=None):
        for s in range(QT):
            ins = dve.bn_stats(self.stats[:, s, :], src[s])
        steps.link(ins)
        for s in range(QT):
            ins = dve.bn_aggr(self.mv[:, s, :], self.stats[:, s, :])
        ins.then_inc(self.sums_ready, 1)
        dve.wait_ge(self.roots_ready, rnd + 1)
        steps.link(dve.reciprocal(self.rstd[:], self.dev[:]))
        for s in range(QT):
            ins = dve.tensor_scalar(dst[s], src[s], self.mv[:, s, 0:1], self.rstd[:, s:s + 1],
                                    ALU.subtract, ALU.mult)
        if gamma is not None:
            steps.link(ins)
            for s in range(QT):
                ins = dve.tensor_tensor(dst[s], dst[s], gamma, ALU.mult)
        steps.link(ins)

    def scalar(self, act, rnd, eps):
        act.wait_ge(self.sums_ready, rnd + 1)
        act.activation(self.dev[:], self.mv[:, :, 1], ACT.Sqrt, bias=eps).then_inc(self.roots_ready, 1)


def stage_queries(nc, x, wq, bq, q0s):
    with Space(nc, "q") as sp:
        neg_scale = -float(D0) ** -0.5
        w_raw = sp.sb("w_raw", [P, KC, D])
        w_hi, w_lo = sp.sb("w_hi", [P, KC, D], F32R), sp.sb("w_lo", [P, KC, D], F32R)
        bq_raw, bq_col = sp.sb("bq_raw", [P, KC]), sp.sb("bq_col", [P, KC])
        eps, ident = sp.sb("eps", [P, 1]), sp.sb("ident", [P, P])
        xin = sp.sb("xin", [P, B, QT, D])
        xn = sp.sb("xn", [P, QT, D])
        t_hi, t_lo = sp.sb("t_hi", [P, KC, NT], F32R), sp.sb("t_lo", [P, KC, NT], F32R)
        q_hi, q_lo = sp.sb("q_hi", [P, KC, NT], F32R), sp.sb("q_lo", [P, KC, NT], F32R)
        tp = [sp.ps(f"tp{i}", [P, NT]) for i in range(KC)]
        bank = [sp.ps(f"bank{i}", [P, NT]) for i in range(KC)]
        norm = Norm(sp, "norm")
        loaded, x_loaded, made = sp.sem("loaded"), sp.sem("x_loaded"), sp.sem("made")
        w_hi_ready, w_ready = sp.sem("w_hi_ready"), sp.sem("w_ready")
        xn_ready, turned, t_hi_ready, t_ready = (sp.sem(n) for n in ("xn_ready", "turned", "t_hi_ready", "t_ready"))
        full, q_hi_ready, q_ready, stored = (sp.sem(n) for n in ("full", "q_hi_ready", "q_ready", "stored"))
        own = sp.sem("own")
        block = sp.block()

        @block.gpsimd
        def _(pool):
            pool.memset(eps[:], EPS).then_inc(made, 1)
            pool.memset(ident[:], 0.0).then_inc(made, 1)
            pool.wait_ge(made, 2)
            pool.affine_select(out=ident[:], in_=ident[:], compare_op=ALU.not_equal, fill=1.0, base=0,
                               pattern=[[-1, P]], channel_multiplier=1).then_inc(made, 1)

        @block.sync
        def _(sync):
            sync.dma_start(xin[:], x.rearrange("b (s p) d -> p b s d", p=P)).then_inc(x_loaded, 16)
            sync.dma_start(w_raw[:], wq.rearrange("(c p) n -> p c n", p=P)).then_inc(loaded, 16)
            sync.dma_start(bq_raw[:], bq.rearrange("(c p) -> p c", p=P),
                           allow_slow_non_contiguous=True).then_inc(loaded, 16)
            for b in range(B):
                sync.wait_ge(q_ready, KC * (b + 1))
                for part, src in ((0, q_hi), (1, q_lo)):
                    sync.dma_start(q0s[part, b].rearrange("(c p) t -> p c t", p=P),
                                   src[:].bitcast(F32)).then_inc(stored, 16)
            sync.wait_ge(stored, 32 * B)

        @block.tensor
        def _(pe):
            pe.wait_ge(made, 3)
            pe.wait_ge(w_ready, KC)
            for b in range(B):
                pe.wait_ge(xn_ready, b + 1)
                for c in range(KC):
                    for s in range(QT):
                        ins = pe.transpose(tp[c][:, s * P:(s + 1) * P], xn[:, s, c * P:(c + 1) * P], ident[:])
                    ins.then_inc(turned, 1)
                pe.wait_ge(t_ready, KC * (b + 1))
                for j in range(KC):
                    if b:
                        pe.wait_ge(q_ready, KC * (b - 1) + j + 1)
                    product3(pe, bank[j][:], [((w_hi[:, c, j * P:(j + 1) * P], w_lo[:, c, j * P:(j + 1) * P]),
                                               (t_hi[:, c, :], t_lo[:, c, :])) for c in range(KC)]).then_inc(full, 1)

        @block.scalar
        def _(act):
            act.wait_ge(loaded, 32)
            for c in range(KC):
                act.activation(w_hi[:, c, :], w_raw[:, c, :], ACT.Copy, scale=neg_scale).then_inc(w_hi_ready, 1)
            act.activation(bq_col[:], bq_raw[:], ACT.Copy, scale=neg_scale).then_inc(w_hi_ready, 1)
            act.wait_ge(w_hi_ready, KC + 1)
            act.wait_ge(made, 3)
            for b in range(B):
                norm.scalar(act, b, eps[:])
                for c in range(KC):
                    act.wait_ge(turned, KC * b + c + 1)
                    act.activation(t_hi[:, c, :], tp[c][:], ACT.Copy).then_inc(t_hi_ready, 1)
                if b:
                    act.wait_ge(stored, 32 * b)
                for j in range(KC):
                    act.wait_ge(full, KC * b + j + 1)
                    act.activation(q_hi[:, j, :], bank[j][:], ACT.Identity, bias=bq_col[:, j:j + 1]
                                   ).then_inc(q_hi_ready, 1)

        @block.vector
        def _(dve):
            steps = Steps(dve, own)
            for c in range(KC):
                dve.wait_ge(w_hi_ready, c + 1)
                dve.scalar_tensor_tensor(w_lo[:, c, :], w_raw[:, c, :], neg_scale, w_hi[:, c, :].bitcast(F32),
                                         ALU.mult, ALU.subtract).then_inc(w_ready, 1)
            dve.wait_ge(x_loaded, 16)
            for b in range(B):
                if b:
                    dve.wait_ge(turned, KC * b)
                norm.vector(dve, steps, b, [xin[:, b, s, :] for s in range(QT)], [xn[:, s, :] for s in range(QT)])
                dve.sem_inc(xn_ready, 1)
                for c in range(KC):
                    dve.wait_ge(t_hi_ready, KC * b + c + 1)
                    dve.tensor_tensor(t_lo[:, c, :], tp[c][:], t_hi[:, c, :].bitcast(F32),
                                      ALU.subtract).then_inc(t_ready, 1)
                for j in range(KC):
                    dve.wait_ge(q_hi_ready, KC * b + j + 1)
                    dve.scalar_tensor_tensor(q_lo[:, j, :], bank[j][:], bq_col[:, j:j + 1],
                                             q_hi[:, j, :].bitcast(F32), ALU.add, ALU.subtract).then_inc(q_ready, 1)


class Count:

    def __init__(self, sem, prime):
        self.sem, self.prime = sem, prime

    def start(self, eng):
        eng.sem_inc(self.sem, self.prime)

    def wait(self, eng, n):
        eng.wait_ge(self.sem, n + self.prime)


def stage_attention(nc, tag, heads, dh, native, q_s, k_s, v_s, o_s, bias_s, null_s=None, null_kv=None):
    with Space(nc, tag) as sp:
        null = null_kv is not None
        WIDE = P // 2
        group, GC = WIDE // dh, 4
        groups, CH = heads // group, GC * (WIDE // dh)
        chunks = heads // CH
        R = 2 * CH if null else CH
        RR = 3 * R if null else 2 * R
        stacked = 3 * dh <= P
        per_query = len(bias_s.shape) == 3
        rows_q = 3 * dh if stacked else 2 * dh
        NP, NB4 = 4, 4
        qs = [sp.sb(f"qs{i}", [rows_q, S], F32R) for i in range(2)]
        ks = [sp.sb(f"ks{i}", [rows_q, CTX], F32R) for i in range(2)]
        kl = None if stacked else [sp.sb(f"kl{i}", [dh, CTX], F32R) for i in range(2)]
        v_raw = [sp.sb(f"v_raw{i}", [P, KT, WIDE]) for i in range(2)]
        vz = [sp.sb(f"vz{i}", [P, KT, group, P], F32R) for i in range(2)]
        bias = sp.sb("bias", [P, QT if per_query else 1, CTX], BF16)
        p = [sp.sb(f"p{i}", [P, QT, CTX]) for i in range(NP)]
        pt_hi = [sp.sb(f"pt_hi{i}", [P, NT], F32R) for i in range(NB4)]
        pt_lo = [sp.sb(f"pt_lo{i}", [P, NT], F32R) for i in range(NB4)]
        pt_all = sp.sb("pt_all", [P, NT])
        nmax, sums = sp.sb("nmax", [P, heads, QT]), sp.sb("sums", [P, heads, QT])
        dn, tot = sp.sb("dn", [P, CH, QT]), sp.sb("tot", [P, CH, QT])
        wcols, rcols, rrows = sp.sb("wcols", [P, QT, R]), sp.sb("rcols", [P, QT, RR], F32R), sp.sb("rrows", [RR, S], F32R)
        ident = sp.sb("ident", [P, P])
        sel_raw = sp.sb("sel_raw", [R, GC, 2, WIDE])
        sel = sp.sb("sel", [RR, GC, P], F32R)
        o_raw, o_out = sp.sb("o_raw", [P, GC, S]), [sp.sb(f"o_out{i}", [P, S]) for i in range(2)]
        s_ps = [sp.ps(f"s{i}", [P, CTX]) for i in range(2)]
        t_ps = [sp.ps(f"t{i}", [P, NT]) for i in range(2)]
        o_ps, f_ps = sp.ps("o", [P, NT]), sp.ps("f", [P, NT])
        if null:
            nv_raw = sp.sb("nv_raw", [R, GC, 2, WIDE])
            nv_hi, nv_lo = sp.sb("nv_hi", [R, GC, P], F32R), sp.sb("nv_lo", [R, GC, P], F32R)
            nv = sp.sb("nv", [RR, GC, P], F32R)
            sn = sp.sb("sn", [P, heads, QT])
            pn = sp.sb("pn", [P, CH, QT])

        split = [t for t in range(KT) if t not in native]
        NS = len(split)
        if null:
            ENDS = [(2, 0, 0), (3, 0, 1), (4, 1, 0), (5, 1, 1), (6, 2, 0), (7, 2, 1), (12, 3, 0), (13, 3, 1)]
        else:
            ENDS = [(2, 0, 0), (3, 1, 0), (4, 2, 0), (12, 3, 0)]
        NE, PARTS = len(ENDS), 2 if null else 1
        LAST = [max(n for n, e in enumerate(ENDS) if e[1] == g) for g in range(GC)]
        COLS, TOT = 7, 2 if null else 4
        QK = 6 if stacked else 5
        SCORE_AT = MAX_AT = {0: 6, 2: 7, 4: 8, 6: 9}
        EXP_AT = {0: 5, 2: 6, 4: 7, 6: 8}

        made, nv_loaded, sel_put = sp.sem("made"), sp.sem("nv_loaded"), sp.sem("sel_put")
        qk_loaded = [sp.sem(f"qk_loaded{i}") for i in range(2)]
        v_loaded = [sp.sem(f"v_loaded{i}") for i in range(2)]
        v_hi_ready, v_split = sp.sem("v_hi_ready"), Count(sp.sem("v_split"), group + 1)
        bias_loaded = [sp.sem(f"bias_loaded{t}") for t in range(QT)]
        sn_loaded = sp.sem("sn_loaded")
        scored = Count(sp.sem("scored"), 2 * QT)
        maxed = Count(sp.sem("maxed"), heads * QT)
        exped = Count(sp.sem("exped"), 2)
        turned = Count(sp.sem("turned"), NP * KT)
        hi_moved = Count(sp.sem("hi_moved"), 2)
        lo_moved = Count(sp.sem("lo_moved"), 2)
        weighed = Count(sp.sem("weighed"), 2 * KT * group)
        o_copied = Count(sp.sem("o_copied"), 1)
        cols = Count(sp.sem("cols"), COLS)
        null_exped = sp.sem("null_exped")
        rows_turned = Count(sp.sem("rows_turned"), 1)
        rows_ready = sp.sem("rows_ready")
        f_made = Count(sp.sem("f_made"), 1)
        f_used = Count(sp.sem("f_used"), NE + 1)
        stored = [Count(sp.sem(f"stored{i}"), 32) for i in range(2)]
        spare = sp.sem("spare")
        MADE = 13 if null else 8
        block = sp.block()

        def end_at(j, t):
            if j > 0 and j % CH == CH - 1:
                chunk, slot = j // CH, t
            elif j % CH == 0 and j:
                chunk, slot = j // CH - 1, KT + t
            else:
                return None
            for n, (at, g, part) in enumerate(ENDS):
                if at == slot:
                    return chunk, n, g, part
            return None

        def tile_at(course, b, j, t):
            tile = QT * j + course[t] if t in course else None
            if tile is not None and isinstance(b, int) and b == B - 1 and tile >= heads * QT:
                return None
            return tile

        def run(eng, slot):
            for t in range(KT):
                slot(0, 0, t)
            with eng.Fori(0, B - 1) as b:
                for j in range(1, heads + 1):
                    for t in range(KT):
                        slot(b, j, t)
            for j in range(1, heads):
                for t in range(KT):
                    slot(B - 1, j, t)

        @block.gpsimd
        def _(pool):
            v_split.start(pool)
            pool.memset(ident[:], 0.0).then_inc(made, 1)
            pool.memset(sel_raw[:], 1.0).then_inc(made, 1)
            pool.wait_ge(made, 2)
            pool.affine_select(out=ident[:], in_=ident[:], compare_op=ALU.not_equal, fill=1.0, base=0,
                               pattern=[[-1, P]], channel_multiplier=1).then_inc(made, 1)
            for i in range(2):
                pool.memset(vz[i][:].bitcast(F32), 0.0).then_inc(made, 1)
            pool.memset(sel[:].bitcast(F32), 0.0).then_inc(made, 1)
            n = 6

            def only(raw, first, n):
                pool.affine_select(out=raw[:], in_=raw[:], compare_op=ALU.is_ge, fill=0.0, base=dh * first,
                                   pattern=[[WIDE, GC], [0, 2], [1, WIDE]], channel_multiplier=-dh).then_inc(made, 1)
                pool.wait_ge(made, n + 1)
                pool.affine_select(out=raw[:], in_=raw[:], compare_op=ALU.is_ge, fill=0.0,
                                   base=dh - 1 - dh * first, pattern=[[-WIDE, GC], [0, 2], [-1, WIDE]],
                                   channel_multiplier=dh).then_inc(made, 1)
                pool.wait_ge(made, n + 2)
            only(sel_raw, 0, n)
            if null:
                pool.memset(nv_raw[:, :, 1, :], 0.0).then_inc(made, 1)
                pool.wait_ge(made, n + 3)
                pool.wait_ge(nv_loaded, 16 * GC)
                only(nv_raw, CH, n + 3)
                flat = nv_raw[:].rearrange("r g a c -> r g (a c)")
                pool.tensor_copy(nv_hi[:], flat).then_inc(made, 1)
                pool.wait_ge(made, n + 6)
                pool.tensor_tensor(nv_lo[:], flat, nv_hi[:].bitcast(F32), ALU.subtract).then_inc(made, 1)

            def split_v(b, g):
                i, k = g % 2, b * groups + g
                pool.wait_ge(v_loaded[i], (b * (groups // 2) + g // 2) * 16 + 16)
                weighed.wait(pool, (k - 1) * KT * group)
                apart(pool, spare)
                for e in range(group):
                    pool.tensor_copy(vz[i][:, :, e, e * dh:(e + 1) * dh], v_raw[i][:, :, e * dh:(e + 1) * dh]
                                     ).then_inc(v_hi_ready, 1)
                pool.wait_ge(v_hi_ready, k * group + group)
                apart(pool, spare)
                for e in range(group):
                    ins = pool.tensor_tensor(vz[i][:, :, e, WIDE + e * dh:WIDE + (e + 1) * dh],
                                             v_raw[i][:, :, e * dh:(e + 1) * dh],
                                             vz[i][:, :, e, e * dh:(e + 1) * dh].bitcast(F32), ALU.subtract)
                    ins.then_inc(v_split.sem, 1)

            with pool.Fori(0, B) as b:
                for g in range(groups):
                    split_v(b, g)

        @block.sync
        def _(sync):
            if null:
                for g in range(GC):
                    sync.dma_start(nv_raw[:, g, 0, :], null_kv[1:2, :].broadcast_to([R, dh])).then_inc(nv_loaded, 16)
            sync.wait_ge(made, MADE)
            flat = sel_raw[:].rearrange("r g a c -> r g (a c)")
            for i in range(RR // R):
                if i < 2:
                    sync.dma_start(sel[i * R:(i + 1) * R].bitcast(F32), flat).then_inc(sel_put, 16)
                if null:
                    sync.dma_start(nv[i * R:(i + 1) * R].bitcast(F32), (nv_hi, nv_hi, nv_lo)[i][:].bitcast(F32)).then_inc(sel_put, 16)

            def load_qk(b, j):
                i, rows = j % 2, slice(j * dh, (j + 1) * dh)
                scored.wait(sync, (b * heads + j - 1) * QT)
                apart(sync, spare)
                for n, part in enumerate((0, 1, 0) if stacked else (0, 1)):
                    sync.dma_start(qs[i][n * dh:(n + 1) * dh, :].bitcast(F32), q_s[part, b, rows, :]
                                   ).then_inc(qk_loaded[i], 16)
                for n, part in enumerate((0, 0, 1) if stacked else (0, 0)):
                    sync.dma_start(ks[i][n * dh:(n + 1) * dh, :].bitcast(F32), k_s[part, b, rows, :]
                                   ).then_inc(qk_loaded[i], 16)
                if not stacked:
                    sync.dma_start(kl[i][:].bitcast(F32), k_s[1, b, rows, :]).then_inc(qk_loaded[i], 16)

            def load_v(b, g):
                v_split.wait(sync, (b * groups + g - 1) * group)
                sync.dma_start(v_raw[g % 2][:], v_s[b, :, g * WIDE:(g + 1) * WIDE].rearrange("(t p) d -> p t d", p=P)
                               ).then_inc(v_loaded[g % 2], 16)

            def load_bias(b, t):
                maxed.wait(sync, ((b - 1) * heads + heads - 1) * QT + t + 1)
                apart(sync, spare)
                if per_query:
                    sync.dma_start(bias[:, t, :], bias_s[b, t * P:(t + 1) * P, :]).then_inc(bias_loaded[t], 16)
                elif t == 0:
                    maxed.wait(sync, b * heads * QT)
                    sync.dma_start(bias[:, 0, :], bias_s[bass.ds(b, 1), :].broadcast_to([P, CTX])
                                   ).then_inc(bias_loaded[0], 16)

            with sync.Fori(0, B) as b:
                for j in range(heads):
                    load_qk(b, j)
                    if j == 0:
                        for t in range(QT if per_query else 1):
                            load_bias(b, t)
                        if null:
                            cols.wait(sync, (b * chunks - 1) * COLS + 1)
                            apart(sync, spare)
                            sync.dma_start(sn[:], null_s[b]).then_inc(sn_loaded, 16)
                    if j % group == 0:
                        load_v(b, j // group)

        @block.tensor
        def _(pe):
            scored.start(pe)
            turned.start(pe)
            weighed.start(pe)
            rows_turned.start(pe)
            f_made.start(pe)
            pe.wait_ge(made, MADE)
            pe.wait_ge(sel_put, 16 * (5 if null else 2))

            def scores(b, tile):
                j, t = tile // QT, tile % QT
                i = j % 2
                if t == 0:
                    pe.wait_ge(qk_loaded[i], (b * (heads // 2) + j // 2 + 1) * 16 * QK)
                exped.wait(pe, b * heads * QT + tile - 1)
                for half in range(2):
                    at = slice(half * NT, (half + 1) * NT)
                    out = s_ps[t % 2][:, at]
                    ins = pe.matmul(out, qs[i][:, t * P:(t + 1) * P], ks[i][:, at], start=True, stop=stacked)
                    if not stacked:
                        ins = pe.matmul(out, qs[i][0:dh, t * P:(t + 1) * P], kl[i][:, at], start=False, stop=True)
                ins.then_inc(scored.sem, 1)

            def turn(b, j, t):
                h = b * heads + j
                if t == 0:
                    exped.wait(pe, h * QT + QT)
                j2, t2 = (h, t - 2) if t >= 2 else (h - 1, KT + t - 2)
                if t2 in native:
                    hi_moved.wait(pe, j2 * KT + t2 + 1)
                else:
                    lo_moved.wait(pe, j2 * NS + split.index(t2) + 1)
                for u in range(QT):
                    ins = pe.transpose(t_ps[t % 2][:, u * P:(u + 1) * P], p[j % NP][:, u, t * P:(t + 1) * P], ident[:])
                ins.then_inc(turned.sem, 1)

            def weigh(b, j, t):
                if t < 0:
                    j, t = j - 1, t + KT
                h, g, e = b * heads + j, j // group, j % group
                i = g % 2
                if t == 0 and e == 0:
                    v_split.wait(pe, (b * groups + g + 1) * group)
                    o_copied.wait(pe, b * groups + g)
                first, last = t == 0 and e == 0, t == KT - 1 and e == group - 1
                if t in native:
                    hi_moved.wait(pe, h * KT + t + 1)
                    ins = pe.matmul(o_ps[:], vz[i][:, t, e, :].bitcast(F32), pt_all[:], start=first, stop=last)
                else:
                    lo_moved.wait(pe, h * NS + split.index(t) + 1)
                    pe.matmul(o_ps[:], vz[i][:, t, e, :], pt_hi[t % NB4][:], start=first, stop=False)
                    ins = pe.matmul(o_ps[:], vz[i][:, t, e, :], pt_lo[t % NB4][:], start=False, stop=last)
                ins.then_inc(weighed.sem, 1)

            def turn_rows(b, chunk):
                k = b * chunks + chunk
                cols.wait(pe, k * COLS + COLS)
                f_used.wait(pe, k * NE)
                for u in range(QT):
                    ins = pe.transpose(f_ps[0:RR, u * P:(u + 1) * P], rcols[:, u, :].bitcast(F32), ident[:])
                ins.then_inc(rows_turned.sem, 1)

            def factors(b, chunk, n, g, part):
                k = b * chunks + chunk
                if n == 0:
                    pe.wait_ge(rows_ready, k + 1)
                f_used.wait(pe, k * NE + n)
                pe.matmul(f_ps[:], (nv if part else sel)[:, g, :], rrows[:], start=True, stop=True
                          ).then_inc(f_made.sem, 1)

            def slot(b, j, t):
                turn(b, j, t)
                if t % 2 == 0 and (j or t >= 4):
                    weigh(b, j, t - 3)
                if tile_at(SCORE_AT, b, j, t):
                    scores(b, tile_at(SCORE_AT, b, j, t))
                if j % CH == CH - 1 and t == 0:
                    turn_rows(b, j // CH)
                if end_at(j, t):
                    factors(b, *end_at(j, t))
                if t % 2 == 0 and (j or t >= 2):
                    weigh(b, j, t - 2)

            for tile in range(6):
                scores(0, tile)
            run(pe, slot)
            for t in range(KT - 3, KT):
                weigh(B - 1, heads - 1, t)
            for t in range(KT):
                if end_at(heads, t):
                    factors(B - 1, *end_at(heads, t))

        @block.scalar
        def _(act):
            exped.start(act)
            hi_moved.start(act)
            o_copied.start(act)
            for i in range(2):
                stored[i].start(act)

            def exps(b, tile):
                j, t = tile // QT, tile % QT
                jb = j % heads
                maxed.wait(act, b * heads * QT + tile + 1)
                turned.wait(act, (b * heads + j + 1 - NP) * KT)
                if tile == heads * QT:
                    cols.wait(act, (b * chunks + chunks - 1) * COLS + TOT)
                act.activation(p[j % NP][:, t, :], s_ps[t % 2][:], ACT.Exp, bias=nmax[:, jb, t:t + 1], scale=-1.0,
                               accum_out=sums[:, jb, t:t + 1]).then_inc(exped.sem, 1)

            def move(b, j, t):
                n = (b * heads + j) * KT + t
                turned.wait(act, n + 1)
                weighed.wait(act, n - NB4 + 1 if t not in native else n - KT + 1)
                act.activation(pt_all[:] if t in native else pt_hi[t % NB4][:], t_ps[t % 2][:], ACT.Copy
                               ).then_inc(hi_moved.sem, 1)

            def copy_o(b, g):
                k = b * groups + g
                weighed.wait(act, (k + 1) * KT * group)
                f_used.wait(act, (b * chunks + g // GC - 1) * NE + LAST[g % GC] + 1)
                act.activation(o_raw[:, g % GC, :], o_ps[:], ACT.Copy).then_inc(o_copied.sem, 1)

            def null_exps(b, chunk):
                k = b * chunks + chunk
                cols.wait(act, k * COLS + 1)
                act.activation(pn[:], dn[:], ACT.Exp).then_inc(null_exped, 1)

            def copy_rows(b, chunk):
                k = b * chunks + chunk
                rows_turned.wait(act, k + 1)
                f_made.wait(act, k * NE)
                act.activation(rrows[:], f_ps[0:RR, :], ACT.Copy).then_inc(rows_ready, 1)

            def store(b, chunk, n, g):
                k = b * chunks + chunk
                i, at = g % 2, slice((chunk * GC + g) * WIDE, (chunk * GC + g + 1) * WIDE)
                f_used.wait(act, k * NE + n + 1)
                for part in range(2):
                    act.dma_start(o_s[b, part, at, :], o_out[i][part * WIDE:(part + 1) * WIDE, :]
                                  ).then_inc(stored[i].sem, 16)

            def slot(b, j, t):
                move(b, j, t)
                if t == 3 and null and (j + 1) % CH == CH - 1:
                    null_exps(b, j // CH)
                if j and j % group == 0 and t == 2:
                    copy_o(b, j // group - 1)
                if tile_at(EXP_AT, b, j, t):
                    exps(b, tile_at(EXP_AT, b, j, t))
                if j % CH == CH - 1 and t == 0:
                    copy_rows(b, j // CH)
                before = end_at(j, t - 1) if t else end_at(j - 1, KT - 1)
                if before:
                    chunk, n, g, _ = before
                    if n == LAST[g]:
                        store(b, chunk, n, g)

            for tile in range(5):
                exps(0, tile)
            run(act, slot)
            copy_o(B - 1, groups - 1)
            for before in [end_at(heads - 1, KT - 1)] + [end_at(heads, t) for t in range(KT)]:
                if before and before[1] == LAST[before[2]]:
                    store(B - 1, *before[:3])
            for i in range(2):
                stored[i].wait(act, 32 * B * groups // 2)

        @block.vector
        def _(dve):
            maxed.start(dve)
            lo_moved.start(dve)
            cols.start(dve)
            f_used.start(dve)

            def biased_max(b, tile):
                j, t = tile // QT, tile % QT
                jb, rows = j % heads, b * heads + j - j % heads
                if jb == 0 and (per_query or t == 0):
                    dve.wait_ge(bias_loaded[t], (b + j // heads) * 16 + 16)
                    if null and t == 0:
                        dve.wait_ge(sn_loaded, (b + j // heads) * 16 + 16)
                if tile == heads * QT:
                    cols.wait(dve, (b * chunks + chunks - 1) * COLS + 1)
                scored.wait(dve, b * heads * QT + tile + 1)
                apart(dve, spare)
                dve.tensor_tensor_reduce(s_ps[t % 2][:], s_ps[t % 2][:], bias[:, t if per_query else 0, :],
                                         1.0, sn[:, jb, t:t + 1] if null else BIG, ALU.add, ALU.min,
                                         nmax[:, jb, t:t + 1]).then_inc(maxed.sem, 1)

            def move(b, j, t):
                n = (b * heads + j) * KT + t
                hi_moved.wait(dve, n + 1)
                weighed.wait(dve, n - NB4 + 1)
                dve.tensor_tensor(pt_lo[t % NB4][:], t_ps[t % 2][:], pt_hi[t % NB4][:].bitcast(F32), ALU.subtract
                                  ).then_inc(lo_moved.sem, 1)

            def column_step(b, chunk, n):
                k = b * chunks + chunk
                hs = slice(chunk * CH, (chunk + 1) * CH)
                heads_first = wcols[:, :, 0:CH].rearrange("p t e -> p e t")
                if n > 1:
                    cols.wait(dve, k * COLS + n - 1)
                if n == 1:
                    maxed.wait(dve, (b * heads + (chunk + 1) * CH) * QT)
                if n == TOT:
                    exped.wait(dve, (b * heads + (chunk + 1) * CH) * QT)
                if null:
                    if n == 1:
                        ins = dve.tensor_tensor(dn[:], nmax[:, hs, :], sn[:, hs, :], ALU.subtract)
                    elif n == 2:
                        dve.wait_ge(null_exped, k + 1)
                        ins = dve.tensor_tensor(tot[:], sums[:, hs, :], pn[:], ALU.add)
                    elif n == 3:
                        ins = dve.reciprocal(heads_first, tot[:])
                    elif n == 4:
                        ins = dve.tensor_tensor(wcols[:, :, CH:R].rearrange("p t e -> p e t"), heads_first, pn[:],
                                                ALU.mult)
                else:
                    if n == 1:
                        ins = dve.tensor_scalar(dn[:], nmax[:, hs, :], BIG / 2, BIG, ALU.is_ge, ALU.mult)
                    elif n == 2:
                        ins = dve.tensor_scalar(dn[:], dn[:], 4.0, None, ALU.mult)
                    elif n == 3:
                        ins = dve.tensor_tensor(dn[:], dn[:], dn[:], ALU.subtract)
                    elif n == 4:
                        ins = dve.tensor_tensor(tot[:], sums[:, hs, :], dn[:], ALU.add)
                    elif n == 5:
                        ins = dve.reciprocal(heads_first, tot[:])
                if n == COLS - (2 if null else 1):
                    rows_turned.wait(dve, k)
                    ins = dve.tensor_copy(rcols[:, :, 0:R], wcols[:])
                elif n == COLS - (1 if null else 0):
                    ins = dve.tensor_tensor(rcols[:, :, R:2 * R], wcols[:], rcols[:, :, 0:R].bitcast(F32), ALU.subtract)
                elif n == COLS:
                    ins = dve.tensor_copy(rcols[:, :, 2 * R:], rcols[:, :, 0:R].bitcast(F32))
                ins.then_inc(cols.sem, 1)

            def use(b, chunk, n, g, part):
                k = b * chunks + chunk
                i = g % 2
                f_made.wait(dve, k * NE + n + 1)
                if part == 0:
                    o_copied.wait(dve, k * GC + g + 1)
                    stored[i].wait(dve, (k * (GC // 2) + g // 2) * 32)
                    ins = dve.tensor_tensor(o_out[i][:], o_raw[:, g, :], f_ps[:], ALU.mult)
                else:
                    f_used.wait(dve, k * NE + n)
                    ins = dve.tensor_tensor(o_out[i][:], o_out[i][:], f_ps[:], ALU.add)
                ins.then_inc(f_used.sem, 1)

            def slot(b, j, t):
                if t not in native:
                    move(b, j, t)
                if tile_at(MAX_AT, b, j, t):
                    biased_max(b, tile_at(MAX_AT, b, j, t))
                if (j + 1) % CH == CH - 1:
                    for n in {2: (1,), 5: range(2, COLS + 1)}.get(t, ()):
                        column_step(b, j // CH, n)
                if end_at(j, t):
                    use(b, *end_at(j, t))

            for tile in range(6):
                biased_max(0, tile)
            run(dve, slot)
            for t in range(KT):
                if end_at(heads, t):
                    use(B - 1, *end_at(heads, t))




T = 384
TS = T // P
TOP = 2
J = (TOP * N - E) // T + E
SLOTS = J * T
NB = N // P
HC = HID // P
BW = 2 * HC + KC


def stage_route(nc, x, o0s, wo, bo, gate, tokens, b1, b2, b3, x1s, xgs, pos_s, tile_s, bias_s):
    with Space(nc, "r") as sp:
        w_raw = sp.sb("w_raw", [P, KC, D])
        w_hi, w_lo = sp.sb("w_hi", [P, KC, D], F32R), sp.sb("w_lo", [P, KC, D], F32R)
        bo_row, tanh_g, g_raw = sp.sb("bo_row", [P, D]), sp.sb("tanh_g", [P, 1]), sp.sb("g_raw", [P, 1])
        eps, ident, ones, tri = (sp.sb("eps", [P, 1]), sp.sb("ident", [P, P]), sp.sb("ones", [P, P]),
                                 sp.sb("tri", [P, P]))
        zeros = sp.sb("zeros", [P, 8, D])
        tok_t = sp.sb("tok_t", [P, KC, E])
        tok_raw = sp.sb("tok_raw", [E, D])
        brows = [sp.sb("b1rows", [E * HC, P]), sp.sb("b2rows", [E * HC, P]), sp.sb("b3rows", [E * KC, P])]
        bcols = sp.sb("bcols", [P, E, BW])
        iota_e = sp.sb("iota_e", [P, NB, E])
        iota_j = sp.sb("iota_j", [P, J + 2])
        xin = sp.sb("xin", [P, B, QT, D])
        xn = sp.sb("xn", [P, NB, D])
        ot = [sp.sb(f"ot{i}", [P, KC, NT]) for i in range(2)]
        ot2 = [sp.sb(f"ot2_{i}", [P, KC, NT]) for i in range(2)]
        ot_hi, ot_lo = sp.sb("ot_hi", [P, KC, NT], F32R), sp.sb("ot_lo", [P, KC, NT], F32R)
        tmp = sp.sb("tmp", [P, QT, D])
        xt = sp.sb("xt", [P, KC, NT])
        scores = sp.sb("scores", [P, NB, E])
        best, best_i = sp.sb("best", [P, NB, 8]), sp.sb("best_i", [P, NB, 8], U32)
        pick = sp.sb("pick", [P, TOP, NB])
        hot = sp.sb("hot", [P, TOP, NB, E])
        both, before = sp.sb("both", [P, NB, E]), sp.sb("before", [P, NB + 1, E])
        tiles, cum = sp.sb("tiles", [P, E]), sp.sb("cum", [P, E + 1])
        slot, mine = sp.sb("slot", [P, NB, E]), sp.sb("mine", [P, TOP, NB, E])
        pos_f, pos = sp.sb("pos_f", [P, TOP, NB]), sp.sb("pos", [P, TOP, NB], I32)
        tile_f, tile_i = sp.sb("tile_f", [P, J + 2]), sp.sb("tile_i", [P, J + 2], I32)
        bank = [sp.ps(f"bank{i}", [P, 2, D]) for i in range(2)]
        tp = [sp.ps(f"tp{i}", [P, NT]) for i in range(KC)]
        sc_ps, rank_ps, tot_ps = sp.ps("sc", [P, QT, E]), sp.ps("rank", [P, NB, E]), sp.ps("tot", [P, NB, E])
        b_ps = sp.ps("b_ps", [P, 2 * E * HC + E * KC + KC * E])
        norm = Norm(sp, "norm")

        loaded, x_loaded, made = sp.sem("loaded"), sp.sem("x_loaded"), sp.sem("made")
        o_loaded = [sp.sem(f"o_loaded{i}") for i in range(2)]
        w_hi_ready, w_ready = sp.sem("w_hi_ready"), sp.sem("w_ready")
        o_whole = sp.sem("o_whole")
        o_hi_ready, o_ready, full = sp.sem("o_hi_ready"), sp.sem("o_ready"), sp.sem("full")
        xn_ready, turned, xt_ready = sp.sem("xn_ready"), sp.sem("turned"), sp.sem("xt_ready")
        scored, sc_moved, zeroed = sp.sem("scored"), sp.sem("sc_moved"), sp.sem("zeroed")
        b_turned, b_moved, counted, both_ready = (sp.sem("b_turned"), sp.sem("b_moved"), sp.sem("counted"),
                                                  sp.sem("both_ready"))
        placed, scattered, stored, own = sp.sem("placed"), sp.sem("scattered"), sp.sem("stored"), sp.sem("own")
        x1_ready = sp.sem("x1_ready")
        MADE = 8
        ZR = 8 * P
        NZ = (SLOTS + T) // ZR
        ZREST = (SLOTS + T - NZ * ZR) // P
        block = sp.block()
        BC = [0, E * HC, 2 * E * HC, 2 * E * HC + E * KC]

        @block.gpsimd
        def _(pool):
            pool.memset(zeros[:], 0.0).then_inc(made, 1)
            pool.memset(eps[:], EPS).then_inc(made, 1)
            pool.memset(ident[:], 0.0).then_inc(made, 1)
            pool.memset(ones[:], 1.0).then_inc(made, 1)
            pool.wait_ge(made, 4)
            pool.affine_select(out=ident[:], in_=ident[:], compare_op=ALU.not_equal, fill=1.0, base=0,
                               pattern=[[-1, P]], channel_multiplier=1).then_inc(made, 1)
            pool.affine_select(out=tri[:], in_=ones[:], compare_op=ALU.is_ge, fill=0.0, base=-1,
                               pattern=[[1, P]], channel_multiplier=-1).then_inc(made, 1)
            pool.iota(iota_e[:], [[0, NB], [1, E]], base=0, channel_multiplier=0,
                      allow_small_or_imprecise_dtypes=True).then_inc(made, 1)
            pool.iota(iota_j[:], [[1, J + 2]], base=0, channel_multiplier=0,
                      allow_small_or_imprecise_dtypes=True).then_inc(made, 1)
            for b in range(B):
                pool.wait_ge(o_loaded[b % 2], 32 * (b // 2 + 1))
                pool.tensor_tensor(ot[b % 2][:], ot[b % 2][:], ot2[b % 2][:], ALU.add).then_inc(o_whole, 1)
            pool.wait_ge(placed, 1)
            pool.wait_ge(zeroed, 16 * (NZ + 1))
            for t in range(NB):
                for k in range(TOP):
                    pool.indirect_dma_start(xgs, bass.IndirectOffsetOnAxis(ap=pos[:, k, t:t + 1], axis=0),
                                            xn[:, t, :], None).then_inc(scattered, 16)
            pool.wait_ge(scattered, 16 * NB * TOP)

        @block.sync
        def _(sync):
            sync.dma_start(w_raw[:], wo.rearrange("(c p) n -> p c n", p=P)).then_inc(loaded, 16)
            sync.dma_start(bo_row[:], row_of(bo, D)).then_inc(loaded, 16)
            sync.dma_start(g_raw[:], row_of(gate, 2)[:, 0:1]).then_inc(loaded, 16)
            sync.dma_start(tok_raw[:], tokens).then_inc(loaded, 16)
            sync.dma_start(brows[0][:], b1.rearrange("e (c p) -> (e c) p", p=P)).then_inc(loaded, 16)
            sync.dma_start(brows[1][:], b2.rearrange("e (c p) -> (e c) p", p=P)).then_inc(loaded, 16)
            sync.dma_start(brows[2][:], b3.rearrange("e (c p) -> (e c) p", p=P)).then_inc(loaded, 16)
            sync.dma_start(xin[:], x.rearrange("b (s p) d -> p b s d", p=P)).then_inc(x_loaded, 16)

            def load_o(b):
                for part, to in enumerate((ot, ot2)):
                    sync.dma_start(to[b % 2][:], o0s[b, part].rearrange("(c p) t -> p c t", p=P)
                                   ).then_inc(o_loaded[b % 2], 16)
            for b in range(2):
                load_o(b)
            sync.wait_ge(made, MADE)
            for z in range(NZ):
                sync.dma_start(xgs[z * ZR:(z + 1) * ZR, :].rearrange("(s p) d -> p s d", p=P),
                               zeros[:]).then_inc(zeroed, 16)
            sync.dma_start(xgs[NZ * ZR:SLOTS + T, :].rearrange("(s p) d -> p s d", p=P),
                           zeros[:, 0:ZREST, :]).then_inc(zeroed, 16)
            for b in range(2, B):
                sync.wait_ge(o_ready, KC * (b - 1))
                load_o(b)
            sync.wait_ge(x1_ready, B)
            sync.dma_start(x1s.rearrange("b (s p) d -> p b s d", p=P), xin[:]).then_inc(stored, 16)
            sync.wait_ge(b_moved, 2)
            sync.dma_start(bias_s.rearrange("e p c -> p e c"), bcols[:]).then_inc(stored, 16)
            sync.wait_ge(placed, 1)
            sync.dma_start(pos_s, pos[:]).then_inc(stored, 16)
            sync.dma_start(tile_s, tile_i[0:1, :]).then_inc(stored, 16)
            sync.wait_ge(stored, 64)

        @block.tensor
        def _(pe):
            pe.wait_ge(made, MADE)
            pe.wait_ge(loaded, 16 * 7)
            for i in range(3):
                n = brows[i].shape[0]
                pe.transpose(b_ps[:, BC[i]:BC[i] + n], brows[i][:], ident[0:n, 0:n])
            for c in range(KC):
                ins = pe.transpose(b_ps[:, BC[3] + c * E:BC[3] + (c + 1) * E], tok_raw[:, c * P:(c + 1) * P],
                                   ident[0:E, 0:E])
            ins.then_inc(b_turned, 1)
            pe.wait_ge(w_ready, KC)
            pe.wait_ge(b_moved, 2)
            for b in range(B):
                pe.wait_ge(o_ready, KC * (b + 1))
                if b:
                    pe.wait_ge(x1_ready, b)
                for s in range(QT):
                    ins = product3(pe, bank[s // 2][:, s % 2, :],
                                   [((ot_hi[:, c, s * P:(s + 1) * P], ot_lo[:, c, s * P:(s + 1) * P]),
                                     (w_hi[:, c, :], w_lo[:, c, :])) for c in range(KC)])
                ins.then_inc(full, 1)
                pe.wait_ge(xn_ready, b + 1)
                for c in range(KC):
                    for s in range(QT):
                        ins = pe.transpose(tp[c][:, s * P:(s + 1) * P], xn[:, b * QT + s, c * P:(c + 1) * P], ident[:])
                    ins.then_inc(turned, 1)
                pe.wait_ge(xt_ready, KC * (b + 1))
                if b:
                    pe.wait_ge(sc_moved, b)
                for s in range(QT):
                    for c in range(KC):
                        ins = pe.matmul(sc_ps[:, s, :], xt[:, c, s * P:(s + 1) * P], tok_t[:, c, :],
                                        start=(c == 0), stop=(c == KC - 1))
                ins.then_inc(scored, 1)
            pe.wait_ge(both_ready, 1)
            flat = both[:].rearrange("p t e -> p (t e)")
            pe.matmul(rank_ps[:].rearrange("p t e -> p (t e)"), tri[:], flat, start=True, stop=True)
            pe.matmul(tot_ps[:].rearrange("p t e -> p (t e)"), ones[:], flat, start=True, stop=True).then_inc(counted, 1)

        @block.scalar
        def _(act):
            act.wait_ge(loaded, 16 * 7)
            for c in range(KC):
                act.activation(w_hi[:, c, :], w_raw[:, c, :], ACT.Copy).then_inc(w_hi_ready, 1)
            act.activation(tanh_g[:], g_raw[:], ACT.Tanh).then_inc(w_hi_ready, 1)
            act.wait_ge(made, MADE)
            for b in range(B):
                act.wait_ge(o_whole, b + 1)
                if b:
                    act.wait_ge(full, b)
                for c in range(KC):
                    act.activation(ot_hi[:, c, :], ot[b % 2][:, c, :], ACT.Copy).then_inc(o_hi_ready, 1)
                norm.scalar(act, b, eps[:])
                if b:
                    act.wait_ge(scored, b)
                for c in range(KC):
                    act.wait_ge(turned, KC * b + c + 1)
                    act.activation(xt[:, c, :], tp[c][:], ACT.Copy).then_inc(xt_ready, 1)

        @block.vector
        def _(dve):
            steps = Steps(dve, own)
            for c in range(KC):
                dve.wait_ge(w_hi_ready, c + 1)
                dve.tensor_tensor(w_lo[:, c, :], w_raw[:, c, :], w_hi[:, c, :].bitcast(F32),
                                  ALU.subtract).then_inc(w_ready, 1)
            dve.wait_ge(b_turned, 1)
            for i, (at, n) in enumerate(((0, HC), (HC, HC), (2 * HC, KC))):
                ins = dve.tensor_copy(bcols[:, :, at:at + n],
                                      b_ps[:, BC[i]:BC[i] + E * n].rearrange("p (e c) -> p e c", e=E))
            ins.then_inc(b_moved, 1)
            dve.tensor_copy(tok_t[:], b_ps[:, BC[3]:BC[3] + KC * E].rearrange("p (c e) -> p c e", c=KC)
                            ).then_inc(b_moved, 1)
            dve.wait_ge(x_loaded, 16)
            dve.wait_ge(w_hi_ready, KC + 1)
            for b in range(B):
                if b:
                    dve.wait_ge(full, b)
                for c in range(KC):
                    dve.wait_ge(o_hi_ready, KC * b + c + 1)
                    dve.tensor_tensor(ot_lo[:, c, :], ot[b % 2][:, c, :], ot_hi[:, c, :].bitcast(F32),
                                      ALU.subtract).then_inc(o_ready, 1)
                dve.wait_ge(full, b + 1)
                for i in range(2):
                    ins = dve.tensor_tensor(tmp[:, 2 * i:2 * i + 2, :], bank[i][:],
                                            bo_row[:].unsqueeze(1).broadcast_to([P, 2, D]), ALU.add)
                steps.link(ins)
                ins = dve.scalar_tensor_tensor(xin[:, b], tmp[:], tanh_g[:, 0:1], xin[:, b], ALU.mult, ALU.add)
                ins.then_inc(x1_ready, 1)
                dve.wait_ge(x1_ready, b + 1)
                norm.vector(dve, steps, b, [xin[:, b, s, :] for s in range(QT)],
                            [xn[:, b * QT + s, :] for s in range(QT)])
                dve.sem_inc(xn_ready, 1)
                dve.wait_ge(scored, b + 1)
                dve.tensor_copy(scores[:, b * QT:(b + 1) * QT, :], sc_ps[:]).then_inc(sc_moved, 1)
            dve.wait_ge(sc_moved, B)
            for t in range(NB):
                ins = dve.max(best[:, t, :], scores[:, t, :])
            steps.link(ins)
            for t in range(NB):
                ins = dve.max_index(best_i[:, t, :], best[:, t, :], scores[:, t, :])
            steps.link(ins)
            steps.link(dve.tensor_copy(pick[:].rearrange("p k t -> p t k"), best_i[:, :, 0:TOP]))
            for k in range(TOP):
                ins = dve.tensor_tensor(hot[:, k], iota_e[:], pick[:, k, :].unsqueeze(2).broadcast_to([P, NB, E]),
                                        ALU.is_equal)
            steps.link(ins)
            dve.tensor_tensor(both[:], hot[:, 0], hot[:, 1], ALU.add).then_inc(both_ready, 1)
            steps.link(dve.memset(before[:, 0, :], 0.0))
            dve.wait_ge(counted, 1)
            for t in range(NB):
                steps.link(dve.tensor_tensor(before[:, t + 1, :], before[:, t, :], tot_ps[:, t, :], ALU.add))
            steps.link(dve.tensor_scalar(tiles[:], before[:, NB, :], 0.0, None, ALU.is_gt))
            for i in range(1, -(-N // T)):
                steps.link(dve.scalar_tensor_tensor(tiles[:], before[:, NB, :], float(i * T), tiles[:],
                                                    ALU.is_gt, ALU.add))
            steps.link(dve.memset(cum[:, 0:1], 0.0))
            for e in range(E):
                steps.link(dve.tensor_tensor(cum[:, e + 1:e + 2], cum[:, e:e + 1], tiles[:, e:e + 1], ALU.add))
            steps.link(dve.tensor_tensor(slot[:], rank_ps[:], before[:, 0:NB, :], ALU.add))
            steps.link(dve.scalar_tensor_tensor(slot[:], cum[:, 0:E].unsqueeze(1).broadcast_to([P, NB, E]), float(T),
                                                slot[:], ALU.mult, ALU.add))
            for k in range(TOP):
                ins = dve.tensor_tensor(mine[:, k], hot[:, k], slot[:], ALU.mult)
            steps.link(ins)
            steps.link(dve.tensor_reduce(pos_f[:], mine[:], AX.X, ALU.add))
            dve.tensor_copy(pos[:], pos_f[:])
            steps.link(dve.tensor_scalar(tile_f[:], iota_j[:], cum[:, 1:2], None, ALU.is_ge))
            for e in range(1, E):
                steps.link(dve.scalar_tensor_tensor(tile_f[:], iota_j[:], cum[:, e + 1:e + 2], tile_f[:],
                                                    ALU.is_ge, ALU.add))
            steps.link(dve.tensor_scalar(tile_f[:], tile_f[:], float(E - 1), None, ALU.min))
            dve.tensor_copy(tile_i[:], tile_f[:]).then_inc(placed, 1)


def stage_experts(nc, xgs, tile_s, bias_s, w1, w2, w3, ys):
    with Space(nc, "e") as sp:
        RING = 6
        CH = 2 + HC + 2
        W2C, W3C = 2, 2 + HC
        raw = [sp.sb(f"raw{i}", [P, HID]) for i in range(RING)]
        w_hi, w_lo = sp.sb("w_hi", [P, CH, HID], F32R), sp.sb("w_lo", [P, CH, HID], F32R)
        b1_t, b2_t, b3_t = sp.sb("b1_t", [P, HC]), sp.sb("b2_t", [P, HC]), sp.sb("b3_t", [P, KC])
        rows = sp.sb("rows", [P, TS, D])
        x_hi, x_lo = sp.sb("x_hi", [P, KC, T], F32R), sp.sb("x_lo", [P, KC, T], F32R)
        h_hi = [sp.sb(f"h{i}_hi", [P, HC, T], F32R) for i in range(2)]
        h_lo = [sp.sb(f"h{i}_lo", [P, HC, T], F32R) for i in range(2)]
        g = [sp.sb(f"g{i}", [P, T]) for i in range(2)]
        y_t, y_rows = sp.sb("y_t", [P, KC, T]), sp.sb("y_rows", [P, TS, D])
        ident = sp.sb("ident", [P, P])
        tile_e = sp.sb("tile_e", [1, J + 2], I32)
        RB = 3
        bank = [sp.ps(f"bank{i}", [P, NT]) for i in range(RB)]
        tp = [sp.ps(f"tp{i}", [P, NT]) for i in range(KC)]
        yp = [sp.ps(f"yp{i}", [P, 2, D]) for i in range(2)]

        made, te_loaded = sp.sem("made"), sp.sem("te_loaded")
        raw_loaded = [sp.sem(f"raw_loaded{i}") for i in range(RING)]
        split_hi = sp.sem("split_hi")
        split = Count(sp.sem("split"), RING)
        b1_loaded, b2_loaded, b3_loaded, rows_loaded = (sp.sem(n) for n in ("b1_loaded", "b2_loaded", "b3_loaded",
                                                                            "rows_loaded"))
        x_turned, x_hi_ready, x_ready = sp.sem("x_turned"), sp.sem("x_hi_ready"), sp.sem("x_ready")
        full = Count(sp.sem("full"), 2 * HC + KC)
        read = Count(sp.sem("read"), 2 * HC + KC)
        h_ready = Count(sp.sem("h_ready"), 2)
        y_turned, y_moved = sp.sem("y_turned"), Count(sp.sem("y_moved"), 1)
        y_stored, y_free = sp.sem("y_stored"), Count(sp.sem("y_free"), 1)
        spare = sp.sem("spare")
        NBK = 2 * HC + KC
        assert NBK % RB == 0
        block = sp.block()
        ORDER = list(range(W2C, CH)) + [0, 1]

        @block.gpsimd
        def _(pool):
            make_identity(pool, sp, ident, made)
            y_free.start(pool)
            with pool.Fori(0, J) as t:
                y_moved.wait(pool, t + 1)
                pool.dma_start(ys[bass.ds(t * T, T), :].rearrange("(s p) d -> p s d", p=P), y_rows[:]
                               ).then_inc(y_stored, 16)
                pool.wait_ge(y_stored, t * 16 + 16)
                pool.sem_inc(y_free.sem, 1)

        @block.sync
        def _(sync):
            sync.dma_start(tile_e[:], tile_s).then_inc(te_loaded, 16)
            sync.wait_ge(te_loaded, 16)

            def load_chunk(q, e, n, slot):
                split.wait(sync, n - RING + 1)
                apart(sync, spare)
                if q < W2C:
                    src, dst = w1[e, q * P:(q + 1) * P, :], raw[slot][:]
                elif q < W3C:
                    src, dst = w2[e, (q - W2C) * P:(q - W2C + 1) * P, :], raw[slot][:]
                else:
                    r = (q - W3C) * 4 * P
                    src = w3[e, r:r + 4 * P, :].rearrange("(c p) n -> p c n", p=P)
                    dst = raw[slot][:].rearrange("p (c n) -> p c n", c=4)
                sync.dma_start(dst, src).then_inc(raw_loaded[slot], 16)

            e0 = sync.value_load(tile_e[0:1, 0:1], min_val=0, max_val=E - 1)
            sync.dma_start(rows[:], xgs[0:T, :].rearrange("(s p) d -> p s d", p=P)).then_inc(rows_loaded, 16)
            sync.dma_start(b1_t[:], bias_s[e0, :, 0:HC]).then_inc(b1_loaded, 16)
            for q in (0, 1):
                split.wait(sync, q - RING + 1)
                sync.dma_start(raw[q][:], w1[e0, q * P:(q + 1) * P, :]).then_inc(raw_loaded[q], 16)
            with sync.Fori(0, J) as t:
                e = sync.value_load(tile_e[0:1, bass.ds(t, 1)], min_val=0, max_val=E - 1)
                en = sync.value_load(tile_e[0:1, bass.ds(t + 1, 1)], min_val=0, max_val=E - 1)
                read.wait(sync, t * NBK - KC)
                apart(sync, spare)
                sync.dma_start(b2_t[:], bias_s[e, :, HC:2 * HC]).then_inc(b2_loaded, 16)
                for i, q in enumerate(ORDER):
                    if i == HC:
                        read.wait(sync, t * NBK)
                        apart(sync, spare)
                        sync.dma_start(b3_t[:], bias_s[e, :, 2 * HC:BW]).then_inc(b3_loaded, 16)
                    if i == HC + 2:
                        sync.wait_ge(x_turned, t * KC + KC)
                        apart(sync, spare)
                        sync.dma_start(rows[:], xgs[bass.ds((t + 1) * T, T), :].rearrange("(s p) d -> p s d", p=P)
                                       ).then_inc(rows_loaded, 16)
                        read.wait(sync, t * NBK + HC)
                        apart(sync, spare)
                        sync.dma_start(b1_t[:], bias_s[en, :, 0:HC]).then_inc(b1_loaded, 16)
                    load_chunk(q, en if q < W2C else e, t * CH + 2 + i, (2 + i) % RING)

        @block.tensor
        def _(pe):
            full.start(pe)
            pe.wait_ge(made, 2)

            def turn_rows(t):
                pe.wait_ge(rows_loaded, t * 16 + 16)
                for c in range(KC):
                    for s in range(TS):
                        ins = pe.transpose(tp[c][:, s * P:(s + 1) * P], rows[:, s, c * P:(c + 1) * P], ident[:])
                    ins.then_inc(x_turned, 1)

            def block_of(t, m, pairs, waits):
                read.wait(pe, t * NBK + m - RB + 1)
                for i, (stat, mov) in enumerate(pairs):
                    if waits[i]:
                        waits[i]()
                    ins = product3(pe, bank[m % RB][:, 0:T], [(stat, mov)], start=(i == 0), stop=(i == len(pairs) - 1))
                ins.then_inc(full.sem, 1)

            def weights(q, col):
                return w_hi[:, q, col:col + P], w_lo[:, q, col:col + P]

            turn_rows(0)
            with pe.Fori(0, J) as t:
                for m in range(HC):
                    def first(c):
                        if m == 0:
                            pe.wait_ge(x_ready, t * KC + c + 1)
                            split.wait(pe, t * CH + c + 1)
                    block_of(t, m, [(weights(c, m * P), (x_hi[:, c, :], x_lo[:, c, :])) for c in range(KC)],
                             [(lambda c=c: first(c)) for c in range(KC)])
                for m in range(HC):
                    def second(c):
                        if m == 0:
                            h_ready.wait(pe, t * 2 * HC + c + 1)
                            split.wait(pe, t * CH + 2 + c + 1)
                    block_of(t, HC + m, [(weights(W2C + c, m * P), (h_hi[0][:, c, :], h_lo[0][:, c, :]))
                                         for c in range(HC)], [(lambda c=c: second(c)) for c in range(HC)])
                    if m == 3:
                        turn_rows(t + 1)
                for m in range(KC):
                    def third(c):
                        if m == 0:
                            h_ready.wait(pe, t * 2 * HC + HC + c + 1)
                            split.wait(pe, t * CH + 2 + HC + c // 4 + 1)
                    block_of(t, 2 * HC + m, [(weights(W3C + c // 4, (c % 4) * D + m * P),
                                              (h_hi[1][:, c, :], h_lo[1][:, c, :])) for c in range(HC)],
                             [(lambda c=c: third(c)) for c in range(HC)])
                y_moved.wait(pe, t)
                for m in range(KC):
                    read.wait(pe, t * NBK + 2 * HC + m + 1)
                    for s in range(TS):
                        ins = pe.transpose(yp[s // 2][:, s % 2, m * P:(m + 1) * P], y_t[:, m, s * P:(s + 1) * P],
                                           ident[:])
                ins.then_inc(y_turned, 1)

        @block.scalar
        def _(act):
            read.start(act)

            def high(n, q, slot, t):
                act.wait_ge(raw_loaded[slot], (n // RING + 1) * 16 if isinstance(n, int) else t)
                act.activation(w_hi[:, q, :], raw[slot][:], ACT.Copy).then_inc(split_hi, 1)

            def chunk(t, i):
                q, slot = ORDER[i], (2 + i) % RING
                last = HC if q < W2C else 2 * HC - NBK if q < W3C else 2 * HC + KC - NBK
                full.wait(act, t * NBK + last)
                high(None, q, slot, (t * (CH // RING) + (2 + i) // RING + 1) * 16)

            def gelu(t, m):
                layer, c = m // HC, m % HC
                bias = (b1_t, b2_t)[layer]
                if c == 0:
                    act.wait_ge((b1_loaded, b2_loaded)[layer], t * 16 + 16)
                    full.wait(act, (t - 1) * NBK + (2 * HC + KC if layer else 2 * HC))
                full.wait(act, t * NBK + m + 1)
                h_ready.wait(act, t * 2 * HC + m - 1)
                act.activation(g[m % 2][:], bank[m % RB][:, 0:T], ACT.Gelu, bias=bias[:, c:c + 1])
                act.activation(h_hi[layer][:, c, :], bank[m % RB][:, 0:T], ACT.Gelu, bias=bias[:, c:c + 1]
                               ).then_inc(read.sem, 1)

            def rows_high(t):
                for c in range(KC):
                    act.wait_ge(x_turned, t * KC + c + 1)
                    act.activation(x_hi[:, c, :], tp[c][:, 0:T], ACT.Copy).then_inc(x_hi_ready, 1)

            for c in range(KC):
                act.wait_ge(raw_loaded[c], 16)
                act.activation(w_hi[:, c, :], raw[c][:], ACT.Copy).then_inc(split_hi, 1)
            rows_high(0)
            with act.Fori(0, J) as t:
                for i in range(4):
                    chunk(t, i)
                for m in range(HC):
                    gelu(t, m)
                    if m % 2 == 0:
                        chunk(t, 4 + m // 2)
                for i in range(HC, CH):
                    chunk(t, i)
                for m in range(HC, HC + 4):
                    gelu(t, m)
                rows_high(t + 1)
                for m in range(HC + 4, 2 * HC):
                    gelu(t, m)
                act.wait_ge(b3_loaded, t * 16 + 16)
                for m in range(KC):
                    full.wait(act, t * NBK + 2 * HC + m + 1)
                    act.activation(y_t[:, m, :], bank[(2 * HC + m) % RB][:, 0:T], ACT.Identity, bias=b3_t[:, m:m + 1]
                                   ).then_inc(read.sem, 1)

        @block.vector
        def _(dve):
            split.start(dve)
            h_ready.start(dve)
            y_moved.start(dve)

            def low(n, q, slot):
                dve.wait_ge(split_hi, n + 1)
                dve.tensor_tensor(w_lo[:, q, :], raw[slot][:], w_hi[:, q, :].bitcast(F32), ALU.subtract
                                  ).then_inc(split.sem, 1)

            def chunk(t, i):
                low(t * CH + 2 + i, ORDER[i], (2 + i) % RING)

            def rest(t, m):
                layer, c = m // HC, m % HC
                read.wait(dve, t * NBK + m + 1)
                dve.tensor_tensor(h_lo[layer][:, c, :], g[m % 2][:], h_hi[layer][:, c, :].bitcast(F32), ALU.subtract
                                  ).then_inc(h_ready.sem, 1)

            def rows_low(t):
                for c in range(KC):
                    dve.wait_ge(x_hi_ready, t * KC + c + 1)
                    dve.tensor_tensor(x_lo[:, c, :], tp[c][:, 0:T], x_hi[:, c, :].bitcast(F32), ALU.subtract
                                      ).then_inc(x_ready, 1)

            for c in range(KC):
                low(c, c, c)
            rows_low(0)
            with dve.Fori(0, J) as t:
                for i in range(4):
                    chunk(t, i)
                for m in range(HC):
                    rest(t, m)
                    if m % 2 == 0:
                        chunk(t, 4 + m // 2)
                for i in range(HC, CH):
                    chunk(t, i)
                for m in range(HC, HC + 4):
                    rest(t, m)
                rows_low(t + 1)
                for m in range(HC + 4, 2 * HC):
                    rest(t, m)
                dve.wait_ge(y_turned, t + 1)
                y_free.wait(dve, t)
                for s in range(TS):
                    ins = dve.tensor_copy(y_rows[:, s, :], yp[s // 2][:, s % 2, :])
                ins.then_inc(y_moved.sem, 1)


def stage_gather(nc, x1s, ys, pos_s, gate, gamma, wq, null_kv, x2s, q1s, null_s):
    with Space(nc, "g") as sp:
        neg_scale = -float(D1) ** -0.5
        QC = I1 // P
        w_raw = sp.sb("w_raw", [P, KC, I1])
        w_hi, w_lo = sp.sb("w_hi", [P, KC, I1], F32R), sp.sb("w_lo", [P, KC, I1], F32R)
        half_g, g_raw, gamma_row = sp.sb("half_g", [P, 1]), sp.sb("g_raw", [P, 1]), sp.sb("gamma_row", [P, D])
        tanh_g = sp.sb("tanh_g", [P, 1])
        eps, ident = sp.sb("eps", [P, 1]), sp.sb("ident", [P, P])
        nk_col = sp.sb("nk_col", [P, 1])
        nk, nk_hi, nk_lo = sp.sb("nk", [P, QC, H1]), sp.sb("nk_hi", [P, QC, H1], F32R), sp.sb("nk_lo", [P, QC, H1], F32R)
        pos = sp.sb("pos", [P, TOP, NB], I32)
        xin = sp.sb("xin", [P, B, QT, D])
        yg = [sp.sb(f"yg{i}", [P, TOP, QT, D]) for i in range(B)]
        tmp, xn = sp.sb("tmp", [P, QT, D]), sp.sb("xn", [P, QT, D])
        t_hi, t_lo = sp.sb("t_hi", [P, KC, NT], F32R), sp.sb("t_lo", [P, KC, NT], F32R)
        q_hi, q_lo = sp.sb("q_hi", [P, QC, NT], F32R), sp.sb("q_lo", [P, QC, NT], F32R)
        sn = sp.sb("sn", [P, H1, QT])
        tp = [sp.ps(f"tp{i}", [P, NT]) for i in range(KC)]
        bank = [sp.ps(f"bank{i}", [P, NT]) for i in range(QC)]
        sn_ps = sp.ps("sn_ps", [P, QT, H1])
        norm_a, norm_b = Norm(sp, "norm_a"), Norm(sp, "norm_b")
        loaded, x_loaded, pos_loaded, made = sp.sem("loaded"), sp.sem("x_loaded"), sp.sem("pos_loaded"), sp.sem("made")
        gathered = [sp.sem(f"gathered{i}") for i in range(B)]
        w_hi_ready, w_ready, nk_ready = sp.sem("w_hi_ready"), sp.sem("w_ready"), sp.sem("nk_ready")
        xn_ready, turned, t_hi_ready, t_ready = (sp.sem(n) for n in ("xn_ready", "turned", "t_hi_ready", "t_ready"))
        full, q_hi_ready, q_ready, n_scored = (sp.sem(n) for n in ("full", "q_hi_ready", "q_ready", "n_scored"))
        x2_ready, sn_ready, stored, own = sp.sem("x2_ready"), sp.sem("sn_ready"), sp.sem("stored"), sp.sem("own")
        block = sp.block()

        @block.gpsimd
        def _(pool):
            pool.memset(eps[:], EPS).then_inc(made, 1)
            pool.memset(ident[:], 0.0).then_inc(made, 1)
            pool.wait_ge(made, 2)
            pool.affine_select(out=ident[:], in_=ident[:], compare_op=ALU.not_equal, fill=1.0, base=0,
                               pattern=[[-1, P]], channel_multiplier=1).then_inc(made, 1)
            pool.wait_ge(pos_loaded, 16)
            for b in range(B):
                for s in range(QT):
                    for k in range(TOP):
                        t = b * QT + s
                        pool.indirect_dma_start(yg[b][:, k, s, :], None, ys,
                                                bass.IndirectOffsetOnAxis(ap=pos[:, k, t:t + 1], axis=0)
                                                ).then_inc(gathered[b], 16)

        @block.sync
        def _(sync):
            sync.dma_start(pos[:], pos_s).then_inc(pos_loaded, 16)
            sync.dma_start(w_raw[:], wq.rearrange("(c p) n -> p c n", p=P)).then_inc(loaded, 16)
            sync.dma_start(g_raw[:], row_of(gate, 2)[:, 0:1]).then_inc(loaded, 16)
            sync.dma_start(gamma_row[:], row_of(gamma, D)).then_inc(loaded, 16)
            for e in range(2):
                sync.dma_start(nk_col[e * D1:(e + 1) * D1, :], null_kv[0, :].rearrange("(d a) -> d a", a=1),
                               allow_slow_non_contiguous=True).then_inc(loaded, 16)
            sync.dma_start(xin[:], x1s.rearrange("b (s p) d -> p b s d", p=P)).then_inc(x_loaded, 16)
            for b in range(B):
                sync.wait_ge(q_ready, QC * (b + 1))
                for part, src in ((0, q_hi), (1, q_lo)):
                    sync.dma_start(q1s[part, b].rearrange("(c p) t -> p c t", p=P),
                                   src[:].bitcast(F32)).then_inc(stored, 16)
                sync.wait_ge(sn_ready, b + 1)
                sync.dma_start(null_s[b], sn[:]).then_inc(stored, 16)
                if b == B - 1:
                    sync.wait_ge(x2_ready, B)
                    sync.dma_start(x2s.rearrange("b (s p) d -> p b s d", p=P), xin[:]).then_inc(stored, 16)
            sync.wait_ge(stored, 48 * B + 16)

        @block.tensor
        def _(pe):
            pe.wait_ge(made, 3)
            pe.wait_ge(w_ready, KC)
            pe.wait_ge(nk_ready, 4)
            for b in range(B):
                pe.wait_ge(xn_ready, b + 1)
                for c in range(KC):
                    for s in range(QT):
                        ins = pe.transpose(tp[c][:, s * P:(s + 1) * P], xn[:, s, c * P:(c + 1) * P], ident[:])
                    ins.then_inc(turned, 1)
                pe.wait_ge(t_ready, KC * (b + 1))
                for j in range(QC):
                    if b:
                        pe.wait_ge(q_ready, QC * (b - 1) + j + 1)
                    product3(pe, bank[j][:], [((w_hi[:, c, j * P:(j + 1) * P], w_lo[:, c, j * P:(j + 1) * P]),
                                               (t_hi[:, c, :], t_lo[:, c, :])) for c in range(KC)]).then_inc(full, 1)
                pe.wait_ge(q_ready, QC * (b + 1))
                if b:
                    pe.wait_ge(sn_ready, b)
                for s in range(QT):
                    ins = product3(pe, sn_ps[:, s, :], [((q_hi[:, c, s * P:(s + 1) * P], q_lo[:, c, s * P:(s + 1) * P]),
                                                         (nk_hi[:, c, :], nk_lo[:, c, :])) for c in range(QC)])
                ins.then_inc(n_scored, 1)

        @block.scalar
        def _(act):
            act.wait_ge(loaded, 80)
            for c in range(KC):
                act.activation(w_hi[:, c, :], w_raw[:, c, :], ACT.Copy, scale=neg_scale).then_inc(w_hi_ready, 1)
            act.activation(tanh_g[:], g_raw[:], ACT.Tanh).then_inc(w_hi_ready, 1)
            act.wait_ge(w_hi_ready, KC + 1)
            act.activation(half_g[:], tanh_g[:], ACT.Copy, scale=1.0 / TOP).then_inc(w_hi_ready, 1)
            act.wait_ge(made, 3)
            for b in range(B):
                norm_a.scalar(act, b, eps[:])
                norm_b.scalar(act, b, eps[:])
                for c in range(KC):
                    act.wait_ge(turned, KC * b + c + 1)
                    act.activation(t_hi[:, c, :], tp[c][:], ACT.Copy).then_inc(t_hi_ready, 1)
                if b:
                    act.wait_ge(stored, 48 * b)
                    act.wait_ge(n_scored, b)
                for j in range(QC):
                    act.wait_ge(full, QC * b + j + 1)
                    act.activation(q_hi[:, j, :], bank[j][:], ACT.Copy).then_inc(q_hi_ready, 1)

        @block.vector
        def _(dve):
            steps = Steps(dve, own)
            dve.memset(nk[:], 0.0).then_inc(nk_ready, 1)
            dve.wait_ge(nk_ready, 1)
            dve.wait_ge(loaded, 80)
            for h in range(H1):
                rows = slice((h % 2) * D1, (h % 2 + 1) * D1)
                ins = dve.tensor_copy(nk[rows, h // 2, h:h + 1], nk_col[rows, :])
                steps.did(ins)
            steps.wait()
            dve.tensor_copy(nk_hi[:], nk[:]).then_inc(nk_ready, 1)
            dve.wait_ge(nk_ready, 2)
            dve.tensor_tensor(nk_lo[:], nk[:], nk_hi[:].bitcast(F32), ALU.subtract).then_inc(nk_ready, 2)
            for c in range(KC):
                dve.wait_ge(w_hi_ready, c + 1)
                dve.scalar_tensor_tensor(w_lo[:, c, :], w_raw[:, c, :], neg_scale, w_hi[:, c, :].bitcast(F32),
                                         ALU.mult, ALU.subtract).then_inc(w_ready, 1)
            dve.wait_ge(w_hi_ready, KC + 2)
            dve.wait_ge(x_loaded, 16)
            for b in range(B):
                dve.wait_ge(gathered[b], 16 * TOP * QT)
                steps.link(dve.tensor_tensor(tmp[:], yg[b][:, 0], yg[b][:, 1], ALU.add))
                dve.scalar_tensor_tensor(xin[:, b], tmp[:], half_g[:, 0:1], xin[:, b], ALU.mult, ALU.add
                                         ).then_inc(x2_ready, 1)
                dve.wait_ge(x2_ready, b + 1)
                if b:
                    dve.wait_ge(turned, KC * b)
                norm_a.vector(dve, steps, b, [xin[:, b, s, :] for s in range(QT)], [xn[:, s, :] for s in range(QT)])
                steps.wait()
                norm_b.vector(dve, steps, b, [xn[:, s, :] for s in range(QT)], [xn[:, s, :] for s in range(QT)],
                              gamma_row[:])
                dve.sem_inc(xn_ready, 1)
                for c in range(KC):
                    dve.wait_ge(t_hi_ready, KC * b + c + 1)
                    dve.tensor_tensor(t_lo[:, c, :], tp[c][:], t_hi[:, c, :].bitcast(F32),
                                      ALU.subtract).then_inc(t_ready, 1)
                for j in range(QC):
                    dve.wait_ge(q_hi_ready, QC * b + j + 1)
                    dve.tensor_tensor(q_lo[:, j, :], bank[j][:], q_hi[:, j, :].bitcast(F32), ALU.subtract
                                      ).then_inc(q_ready, 1)
                dve.wait_ge(n_scored, b + 1)
                if b:
                    dve.wait_ge(stored, 48 * b)
                dve.tensor_copy(sn[:].rearrange("p h t -> p t h"), sn_ps[:]).then_inc(sn_ready, 1)


def stage_final(nc, x2s, o1s, wo, out_gamma, gates, gate2, wg, bg, we, be, out):
    with Space(nc, "f") as sp:
        OC = I1 // P
        EW = E * D
        WN = OC * D + KC * D + KC * EW
        w_raw = [sp.sb(f"w_raw{i}", [P, EW]) for i in range(2)]
        w_hi, w_lo = sp.sb("w_hi", [P, WN], F32R), sp.sb("w_lo", [P, WN], F32R)
        g_raw, tanh_g = sp.sb("g_raw", [P, 2]), sp.sb("tanh_g", [P, 2])
        gamma_row, bg_row, be_sb = sp.sb("gamma_row", [P, D]), sp.sb("bg_row", [P, D]), sp.sb("be_sb", [E, D])
        eps, ident, iota_e = sp.sb("eps", [P, 1]), sp.sb("ident", [P, P]), sp.sb("iota_e", [P, E])
        xin = sp.sb("xin", [P, B, QT, D])
        ot = [sp.sb(f"ot{i}", [P, OC, NT]) for i in range(2)]
        ot2 = [sp.sb(f"ot2_{i}", [P, OC, NT]) for i in range(2)]
        ot_hi, ot_lo = sp.sb("ot_hi", [P, OC, NT], F32R), sp.sb("ot_lo", [P, OC, NT], F32R)
        att, xn = sp.sb("att", [P, QT, D]), sp.sb("xn", [P, QT, D])
        t_hi, t_lo = sp.sb("t_hi", [P, KC, NT], F32R), sp.sb("t_lo", [P, KC, NT], F32R)
        logits, probs = sp.sb("logits", [P, QT, D]), sp.sb("probs", [P, QT, D])
        top, top_i = sp.sb("top", [P, QT, 8]), sp.sb("top_i", [P, QT, 8], U32)
        neg_max, total, weight = sp.sb("neg_max", [P, QT]), sp.sb("total", [P, QT]), sp.sb("weight", [P, QT])
        e_i, e_f, hot = sp.sb("e_i", [P, QT], U32), sp.sb("e_f", [P, QT]), sp.sb("hot", [P, QT, E])
        hot_t = sp.sb("hot_t", [E, QT, P])
        acc, res = sp.sb("acc", [P, QT, D]), sp.sb("res", [P, QT, D])
        ex = [sp.ps(f"ex{i}", [P, 2, D]) for i in range(4)]
        tp = [sp.ps(f"tp{i}", [P, NT]) for i in range(KC)]
        lg = [sp.ps(f"lg{i}", [P, 2, D]) for i in range(2)]
        norms = [Norm(sp, f"norm{i}") for i in range(3)]
        loaded, x_loaded, made = sp.sem("loaded"), sp.sem("x_loaded"), sp.sem("made")
        w_loaded = [sp.sem(f"w_loaded{i}") for i in range(2)]
        o_loaded = [sp.sem(f"o_loaded{i}") for i in range(2)]
        w_hi_ready, w_ready, tanh_ready = sp.sem("w_hi_ready"), sp.sem("w_ready"), sp.sem("tanh_ready")
        o_whole = sp.sem("o_whole")
        o_hi_ready, o_ready, projected, att_ready = (sp.sem(n) for n in ("o_hi_ready", "o_ready", "projected", "att_ready"))
        xn_ready, turned, t_hi_ready, t_ready = (sp.sem(n) for n in ("xn_ready", "turned", "t_hi_ready", "t_ready"))
        gated, max_ready, exped, hot_ready = (sp.sem(n) for n in ("gated", "max_ready", "exped", "hot_ready"))
        hot_turned, hot_moved, be_ready, acc_ready = (sp.sem(n) for n in ("hot_turned", "hot_moved", "be_ready", "acc_ready"))
        ex_full, ex_read, res_ready, stored, own = (sp.sem(n) for n in ("ex_full", "ex_read", "res_ready", "stored", "own"))
        WO, WG, WE = 0, OC * D, OC * D + KC * D
        pieces = [(WO, OC * D, wo.rearrange("(c p) n -> p c n", p=P), OC),
                  (WG, KC * D, wg.rearrange("(c p) n -> p c n", p=P), KC)]
        for c in range(KC):
            pieces.append((WE + c * EW, EW, we[:, c * P:(c + 1) * P, :].rearrange("e p n -> p e n"), E))
        block = sp.block()

        @block.gpsimd
        def _(pool):
            pool.memset(eps[:], EPS).then_inc(made, 1)
            pool.memset(ident[:], 0.0).then_inc(made, 1)
            pool.wait_ge(made, 2)
            pool.affine_select(out=ident[:], in_=ident[:], compare_op=ALU.not_equal, fill=1.0, base=0,
                               pattern=[[-1, P]], channel_multiplier=1).then_inc(made, 1)
            pool.iota(iota_e[:], [[1, E]], base=0, channel_multiplier=0,
                      allow_small_or_imprecise_dtypes=True).then_inc(made, 1)
            for b in range(B):
                pool.wait_ge(o_loaded[b % 2], 32 * (b // 2 + 1))
                pool.tensor_tensor(ot[b % 2][:], ot[b % 2][:], ot2[b % 2][:], ALU.add).then_inc(o_whole, 1)

        @block.sync
        def _(sync):
            def load_o(b):
                for part, to in enumerate((ot, ot2)):
                    sync.dma_start(to[b % 2][:], o1s[b, part].rearrange("(c p) t -> p c t", p=P)
                                   ).then_inc(o_loaded[b % 2], 16)
            for i, (at, n, src, c) in enumerate(pieces):
                if i >= 2:
                    sync.wait_ge(w_ready, i - 1)
                sync.dma_start(w_raw[i % 2][:, 0:n].rearrange("p (c n) -> p c n", c=c), src).then_inc(w_loaded[i % 2], 16)
                if i == 0:
                    load_o(0)
                    sync.dma_start(g_raw[:, 0:1], row_of(gates, 2)[:, 1:2]).then_inc(loaded, 16)
                    sync.dma_start(g_raw[:, 1:2], row_of(gate2, 2)[:, 1:2]).then_inc(loaded, 16)
                    sync.dma_start(gamma_row[:], row_of(out_gamma, D)).then_inc(loaded, 16)
                    sync.dma_start(bg_row[:], row_of(bg, D)).then_inc(loaded, 16)
                    sync.dma_start(be_sb[:], be).then_inc(loaded, 16)
                    sync.dma_start(xin[:], x2s.rearrange("b (s p) d -> p b s d", p=P)).then_inc(x_loaded, 16)
            for b in range(1, B):
                if b >= 2:
                    sync.wait_ge(o_ready, b - 1)
                load_o(b)
            for b in range(B):
                sync.wait_ge(res_ready, b + 1)
                sync.dma_start(out[b].rearrange("(s p) d -> p s d", p=P), res[:]).then_inc(stored, 16)
            sync.wait_ge(stored, 16 * B)

        @block.tensor
        def _(pe):
            pe.wait_ge(made, 4)
            for b in range(B):
                if b == 0:
                    pe.wait_ge(w_ready, 1)
                pe.wait_ge(o_ready, b + 1)
                if b:
                    pe.wait_ge(ex_read, 4 * E * b)
                for s in range(QT):
                    ins = product3(pe, ex[s // 2][:, s % 2, :],
                                   [((ot_hi[:, c, s * P:(s + 1) * P], ot_lo[:, c, s * P:(s + 1) * P]),
                                     (w_hi[:, WO + c * D:WO + (c + 1) * D], w_lo[:, WO + c * D:WO + (c + 1) * D]))
                                    for c in range(OC)])
                ins.then_inc(projected, 1)
                pe.wait_ge(xn_ready, b + 1)
                for c in range(KC):
                    for s in range(QT):
                        ins = pe.transpose(tp[c][:, s * P:(s + 1) * P], xn[:, s, c * P:(c + 1) * P], ident[:])
                    ins.then_inc(turned, 1)
                pe.wait_ge(t_ready, KC * (b + 1))
                if b == 0:
                    pe.wait_ge(w_ready, len(pieces))

                def stat(s):
                    return [(t_hi[:, c, s * P:(s + 1) * P], t_lo[:, c, s * P:(s + 1) * P]) for c in range(KC)]
                for s in range(QT):
                    ins = product3(pe, lg[s // 2][:, s % 2, :],
                                   [(stat(s)[c], (w_hi[:, WG + c * D:WG + (c + 1) * D],
                                                  w_lo[:, WG + c * D:WG + (c + 1) * D])) for c in range(KC)])
                ins.then_inc(gated, 1)

                def experts(s):
                    for i in range(4):
                        if s:
                            pe.wait_ge(ex_read, 4 * E * b + E * (s - 1) + 2 * (i + 1))
                        cols = [slice(WE + c * EW + i * NT, WE + c * EW + (i + 1) * NT) for c in range(KC)]
                        product3(pe, ex[i][:].rearrange("p a n -> p (a n)"),
                                 [(stat(s)[c], (w_hi[:, cols[c]], w_lo[:, cols[c]])) for c in range(KC)]
                                 ).then_inc(ex_full, 1)
                pe.wait_ge(att_ready, b + 1)
                experts(0)
                pe.wait_ge(hot_ready, b + 1)
                for s in range(QT):
                    ins = pe.transpose(tp[0][0:E, s * P:(s + 1) * P], hot[:, s, :], ident[:])
                ins.then_inc(hot_turned, 1)
                pe.wait_ge(hot_moved, b + 1)
                for s in range(QT):
                    ins = pe.matmul(lg[s // 2][:, s % 2, :], hot_t[:, s, :], be_sb[:], start=True, stop=True)
                ins.then_inc(be_ready, 1)
                for s in range(1, QT):
                    experts(s)

        @block.scalar
        def _(act):
            act.wait_ge(made, 4)
            for i, (at, n, src, c) in enumerate(pieces):
                act.wait_ge(w_loaded[i % 2], 16 * (i // 2 + 1))
                act.activation(w_hi[:, at:at + n], w_raw[i % 2][:, 0:n], ACT.Copy).then_inc(w_hi_ready, 1)
                if i == 0:
                    act.wait_ge(o_whole, 1)
                    act.activation(ot_hi[:], ot[0][:], ACT.Copy).then_inc(o_hi_ready, 1)
            act.wait_ge(loaded, 80)
            act.activation(tanh_g[:], g_raw[:], ACT.Tanh).then_inc(tanh_ready, 1)
            for b in range(B):
                if b:
                    act.wait_ge(o_whole, b + 1)
                    act.wait_ge(projected, b)
                    act.activation(ot_hi[:], ot[b % 2][:], ACT.Copy).then_inc(o_hi_ready, 1)
                for norm in norms[:2]:
                    norm.scalar(act, b, eps[:])
                for c in range(KC):
                    act.wait_ge(turned, KC * b + c + 1)
                    act.activation(t_hi[:, c, :], tp[c][:], ACT.Copy).then_inc(t_hi_ready, 1)
                act.wait_ge(max_ready, b + 1)
                for s in range(QT):
                    act.activation(probs[:, s, :], logits[:, s, :], ACT.Exp, bias=neg_max[:, s:s + 1],
                                   accum_out=total[:, s:s + 1]).then_inc(exped, 1)
                act.wait_ge(hot_turned, b + 1)
                act.activation(hot_t[:].rearrange("e s p -> e (s p)"), tp[0][0:E, :], ACT.Copy).then_inc(hot_moved, 1)
                act.wait_ge(be_ready, b + 1)
                for i in range(2):
                    act.activation(acc[:, 2 * i:2 * i + 2, :], lg[i][:], ACT.Copy).then_inc(acc_ready, 1)

        @block.vector
        def _(dve):
            steps = Steps(dve, own)

            def split_o(b):
                dve.wait_ge(o_hi_ready, b + 1)
                dve.tensor_tensor(ot_lo[:], ot[b % 2][:], ot_hi[:].bitcast(F32), ALU.subtract).then_inc(o_ready, 1)
            for i, (at, n, src, c) in enumerate(pieces):
                dve.wait_ge(w_hi_ready, i + 1)
                dve.tensor_tensor(w_lo[:, at:at + n], w_raw[i % 2][:, 0:n], w_hi[:, at:at + n].bitcast(F32),
                                  ALU.subtract).then_inc(w_ready, 1)
                if i == 0:
                    split_o(0)
            dve.wait_ge(x_loaded, 16)
            dve.wait_ge(tanh_ready, 1)
            tiles = range(QT)
            for b in range(B):
                if b:
                    split_o(b)
                dve.wait_ge(projected, b + 1)
                norms[0].vector(dve, steps, b, [ex[s // 2][:, s % 2, :] for s in tiles], [att[:, s, :] for s in tiles],
                                gamma_row[:])
                steps.link(dve.scalar_tensor_tensor(xin[:, b], att[:], tanh_g[:, 0:1], xin[:, b], ALU.mult, ALU.add))
                dve.sem_inc(att_ready, 1)
                norms[1].vector(dve, steps, b, [xin[:, b, s, :] for s in tiles], [xn[:, s, :] for s in tiles])
                dve.sem_inc(xn_ready, 1)
                for c in range(KC):
                    dve.wait_ge(t_hi_ready, KC * b + c + 1)
                    dve.tensor_tensor(t_lo[:, c, :], tp[c][:], t_hi[:, c, :].bitcast(F32),
                                      ALU.subtract).then_inc(t_ready, 1)
                dve.wait_ge(gated, b + 1)
                for i in range(2):
                    ins = dve.tensor_tensor(logits[:, 2 * i:2 * i + 2, :], lg[i][:],
                                            bg_row[:].unsqueeze(1).broadcast_to([P, 2, D]), ALU.add)
                steps.link(ins)
                steps.link(dve.tensor_reduce(neg_max[:], logits[:], AX.X, ALU.max))
                dve.tensor_scalar(neg_max[:], neg_max[:], -1.0, None, ALU.mult).then_inc(max_ready, 1)
                for s in tiles:
                    dve.wait_ge(exped, QT * b + s + 1)
                    ins = dve.max(top[:, s, :], probs[:, s, :])
                steps.link(ins)
                for s in tiles:
                    ins = dve.max_index(top_i[:, s, :], top[:, s, :], probs[:, s, :])
                steps.link(ins)
                steps.link(dve.tensor_scalar(e_i[:], top_i[:, :, 0], E - 1, None, ALU.bitwise_and))
                steps.link(dve.tensor_copy(e_f[:], e_i[:]))
                dve.tensor_tensor(hot[:], iota_e[:].unsqueeze(1).broadcast_to([P, QT, E]),
                                  e_f[:].unsqueeze(2).broadcast_to([P, QT, E]), ALU.is_equal).then_inc(hot_ready, 1)
                steps.link(dve.reciprocal(weight[:], total[:]))
                steps.link(dve.tensor_scalar(weight[:], weight[:], tanh_g[:, 1:2], None, ALU.mult))
                dve.wait_ge(hot_ready, b + 1)
                dve.wait_ge(acc_ready, 2 * (b + 1))
                if b:
                    dve.wait_ge(stored, 16 * b)
                for s in tiles:
                    for e in range(E):
                        dve.wait_ge(ex_full, 4 * (QT * b + s) + e // 2 + 1)
                        ins = dve.scalar_tensor_tensor(acc[:, s, :], ex[e // 2][:, e % 2, :], hot[:, s, e:e + 1],
                                                       acc[:, s, :], ALU.mult, ALU.add)
                        ins.then_inc(ex_read, 1)
                        dve.wait_ge(ex_read, E * (QT * b + s) + e + 1)
                    steps.link(dve.tensor_scalar(acc[:, s, :], acc[:, s, :], 0.0, weight[:, s:s + 1], ALU.max, ALU.mult))
                    ins = dve.tensor_tensor(res[:, s, :], acc[:, s, :], xin[:, b, s, :], ALU.add)
                ins.then_inc(res_ready, 1)


INPUTS = ["x", "ctx_1024", "mask_Bx1xSxS2_ik1", "mask_BxS2_bf1", "g_xattn", "g_ffn",
          "L0_xattn_wq", "L0_xattn_bq", "L0_xattn_wk", "L0_xattn_bk", "L0_xattn_wv", "L0_xattn_bv", "L0_xattn_wo",
          "L0_xattn_bo", "L0_ffn_expert_tokens", "L0_ffn_W1", "L0_ffn_b1", "L0_ffn_W2", "L0_ffn_b2", "L0_ffn_W3",
          "L0_ffn_b3", "L1_xattn_gamma", "L1_xattn_w_q", "L1_xattn_w_kv", "L1_xattn_null_kv", "L1_xattn_w_out",
          "L1_xattn_out_gamma", "L1_ffn_Wg", "L1_ffn_bg", "L1_ffn_We", "L1_ffn_be"]


def build(nc, a, out):
    def scratch(name, shape, dt=F32):
        return nc.dram_tensor(name, shape, dt).ap()

    k0s, v0s = scratch("k0s", (2, B, D, CTX)), scratch("v0s", (B, CTX, D))
    k1s, v1s = scratch("k1s", (2, B, I1, CTX)), scratch("v1s", (B, CTX, I1))
    bias0, bias1 = scratch("bias0", (B, S, CTX), BF16), scratch("bias1", (B, CTX), BF16)
    q0s, q1s = scratch("q0s", (2, B, D, S)), scratch("q1s", (2, B, I1, S))
    o0s, o1s = scratch("o0s", (B, 2, D, S)), scratch("o1s", (B, 2, I1, S))
    x1s, x2s = scratch("x1s", (B, S, D)), scratch("x2s", (B, S, D))
    xgs, ys = scratch("xgs", (SLOTS + T, D)), scratch("ys", (SLOTS, D))
    pos_s, tile_s = scratch("pos_s", (P, TOP, NB), I32), scratch("tile_s", (1, J + 2), I32)
    bias_s, null_s = scratch("bias_s", (E, P, BW)), scratch("null_s", (B, P, H1, QT))

    stage_context(nc, a["ctx_1024"], a["L0_xattn_wk"], a["L0_xattn_bk"], a["L0_xattn_wv"], a["L0_xattn_bv"],
                  a["L1_xattn_w_kv"], a["mask_Bx1xSxS2_ik1"].rearrange("b a q k -> (b a) q k"), a["mask_BxS2_bf1"],
                  k0s, v0s, k1s, v1s, bias0, bias1)
    stage_queries(nc, a["x"], a["L0_xattn_wq"], a["L0_xattn_bq"], q0s)
    stage_attention(nc, "a0", H0, D0, (KT - 1,), q0s, k0s, v0s, o0s, bias0)
    stage_route(nc, a["x"], o0s, a["L0_xattn_wo"], a["L0_xattn_bo"], a["g_xattn"], a["L0_ffn_expert_tokens"],
                a["L0_ffn_b1"], a["L0_ffn_b2"], a["L0_ffn_b3"], x1s, xgs, pos_s, tile_s, bias_s)
    stage_experts(nc, xgs, tile_s, bias_s, a["L0_ffn_W1"], a["L0_ffn_W2"], a["L0_ffn_W3"], ys)
    stage_gather(nc, x1s, ys, pos_s, a["g_ffn"], a["L1_xattn_gamma"], a["L1_xattn_w_q"], a["L1_xattn_null_kv"],
                 x2s, q1s, null_s)
    stage_attention(nc, "a1", H1, D1, (), q1s, k1s, v1s, o1s, bias1, null_s, a["L1_xattn_null_kv"])
    stage_final(nc, x2s, o1s, a["L1_xattn_w_out"], a["L1_xattn_out_gamma"], a["g_xattn"], a["g_ffn"],
                a["L1_ffn_Wg"], a["L1_ffn_bg"], a["L1_ffn_We"], a["L1_ffn_be"], out)


def kernel(**inputs):
    import numpy as _np
    import concourse.bacc as _bacc
    from concourse import mybir as _mybir
    from concourse.bass_utils import run_bass_kernel_spmd as _run

    nc = _bacc.Bacc("TRN2", target_bir_lowering=False, num_devices=1)
    arrays, args = {}, {}
    for name in INPUTS:
        a = _np.ascontiguousarray(inputs[name])
        if a.dtype == bool:
            a = a.view(_np.uint8)
        arrays[f"in_{name}_dram"] = a
        args[name] = nc.dram_tensor(f"in_{name}_dram", a.shape, _mybir.dt.from_np(a.dtype), kind="ExternalInput").ap()
    out = nc.dram_tensor("out_0_dram", (B, S, D), F32, kind="ExternalOutput").ap()
    build(nc, args, out)
    r = _run(nc, [arrays], core_ids=[0])
    return r.results[0]["out_0_dram"]
```

```python
from contextlib import ExitStack

import numpy as np

import concourse.bass as bass
import concourse.mybir as mybir
from concourse.alu_op_type import AluOpType as ALU

F32 = mybir.dt.float32
F32R = mybir.dt.float32r
BF16 = mybir.dt.bfloat16
I32 = mybir.dt.int32
U32 = mybir.dt.uint32
U8 = mybir.dt.uint8
ACT = mybir.ActivationFunctionType
AX = mybir.AxisListType

P = 128
B, S, D, CTX = 4, 512, 256, 1024
N = B * S
KC = D // P
NT = 512
QT = S // P
KT = CTX // P
H0, D0 = 16, 16
H1, D1 = 8, 64
I1 = H1 * D1
E, HID = 8, 1024
EPS = 1e-5
BIG = 3e38


class Steps:

    def __init__(self, eng, sem, per=0, rnd=0):
        self.eng, self.sem, self.per, self.rnd, self.n = eng, sem, per, rnd, 0

    def did(self, ins):
        self.n += 1
        ins.then_inc(self.sem, 1)

    def wait(self):
        self.eng.wait_ge(self.sem, self.rnd * self.per + self.n)

    def link(self, ins):
        self.did(ins)
        self.wait()

    def close(self):
        assert self.n == self.per, (self.n, self.per)


class Space:

    def __init__(self, nc, tag):
        self.nc, self.tag, self.ctx, self.sems = nc, tag, ExitStack(), []

    def __enter__(self):
        return self

    def __exit__(self, *a):
        self.ctx.__exit__(*a)
        if a[0] is None:
            self.nc.clear_and_free_semaphores(self.sems)
            self.nc.all_engine_barrier()

    def sb(self, name, shape, dt=F32):
        return self.ctx.enter_context(self.nc.sbuf_tensor(f"{self.tag}_{name}", shape, dt))

    def ps(self, name, shape, dt=F32):
        return self.ctx.enter_context(self.nc.psum_tensor(f"{self.tag}_{name}", shape, dt))

    def sem(self, name):
        self.sems.append(self.nc.alloc_semaphore(f"{self.tag}_{name}"))
        return self.sems[-1]

    def block(self):
        return self.ctx.enter_context(self.nc.Block())


def apart(eng, spare):
    eng.sem_inc(spare, 1)


def product3(pe, out, pairs, start=True, stop=True):
    n = 3 * len(pairs)
    k = 0
    for (s_hi, s_lo), (m_hi, m_lo) in pairs:
        for s, m in ((s_hi, m_hi), (s_hi, m_lo), (s_lo, m_hi)):
            ins = pe.matmul(out, s, m, start=start and k == 0, stop=stop and k == n - 1)
            k += 1
    return ins


def row_of(vec, n):
    return vec.rearrange("(a n) -> a n", a=1).broadcast_to([P, n])


def make_identity(pool, sp, ident, made):
    pool.memset(ident[:], 0.0).then_inc(made, 1)
    pool.wait_ge(made, 1)
    pool.affine_select(out=ident[:], in_=ident[:], compare_op=ALU.not_equal, fill=1.0, base=0,
                       pattern=[[-1, P]], channel_multiplier=1).then_inc(made, 1)


class Count:

    def __init__(self, sem, prime):
        self.sem, self.prime = sem, prime

    def start(self, eng):
        eng.sem_inc(self.sem, self.prime)

    def wait(self, eng, n):
        eng.wait_ge(self.sem, n + self.prime)


class Norm:

    def __init__(self, sp, tag):
        self.stats = sp.sb(f"{tag}_stats", [P, QT, 6])
        self.mv = sp.sb(f"{tag}_mv", [P, QT, 2])
        self.dev = sp.sb(f"{tag}_dev", [P, QT])
        self.rstd = sp.sb(f"{tag}_rstd", [P, QT])
        self.sums_ready, self.roots_ready = sp.sem(f"{tag}_sums_ready"), sp.sem(f"{tag}_roots_ready")

    def vector(self, dve, steps, rnd, src, dst, gamma=None, spare=None):
        for s in range(QT):
            ins = dve.bn_stats(self.stats[:, s, :], src[s])
        steps.link(ins)
        if spare is not None:
            apart(dve, spare)
        for s in range(QT):
            ins = dve.bn_aggr(self.mv[:, s, :], self.stats[:, s, :])
        ins.then_inc(self.sums_ready, 1)
        dve.wait_ge(self.roots_ready, rnd + 1)
        steps.link(dve.reciprocal(self.rstd[:], self.dev[:]))
        for s in range(QT):
            ins = dve.tensor_scalar(dst[s], src[s], self.mv[:, s, 0:1], self.rstd[:, s:s + 1],
                                    ALU.subtract, ALU.mult)
        if gamma is not None:
            steps.link(ins)
            for s in range(QT):
                ins = dve.tensor_tensor(dst[s], dst[s], gamma, ALU.mult)
        steps.link(ins)

    def scalar(self, act, rnd, eps):
        act.wait_ge(self.sums_ready, rnd + 1)
        act.activation(self.dev[:], self.mv[:, :, 1], ACT.Sqrt, bias=eps).then_inc(self.roots_ready, 1)


def stage_context(nc, ctx, wk, bk, wv, bv, wkv, mask0, mask1, x, wq, bq, k0s, v0s, k1s, v1s, bias0, bias1, q0s):
    with Space(nc, "c") as sp:
        W = D + D + 2 * I1
        w_raw = sp.sb("w_raw", [P, KC, W])
        w_hi = sp.sb("w_hi", [P, KC, W], F32R)
        w_lo = sp.sb("w_lo", [P, KC, W], F32R)
        bk_col = sp.sb("bk_col", [P, KC])
        bv_row = sp.sb("bv_row", [P, D])
        ident = sp.sb("ident", [P, P])
        rows = [sp.sb(f"rows{i}", [P, QT, D]) for i in range(2)]
        t_hi = [sp.sb(f"t_hi{i}", [P, KC, NT], F32R) for i in range(2)]
        t_lo = [sp.sb(f"t_lo{i}", [P, KC, NT], F32R) for i in range(2)]
        k_hi = [sp.sb(f"k_hi{i}", [P, 6, NT], F32R) for i in range(2)]
        k_lo = [sp.sb(f"k_lo{i}", [P, 6, NT], F32R) for i in range(2)]
        v1_st = [sp.sb(f"v1_st{i}", [P, QT, I1]) for i in range(2)]
        v0_st = [sp.sb(f"v0_st{i}", [P, QT, D]) for i in range(2)]
        m_raw = [sp.sb(f"m_raw{i}", [P, CTX], I32) for i in range(2)]
        m_bias = [sp.sb(f"m_bias{i}", [P, CTX], BF16) for i in range(2)]
        m1_raw, m1_bias = sp.sb("m1_raw", [B, CTX], U8), sp.sb("m1_bias", [B, CTX], BF16)
        neg_scale = -float(D0) ** -0.5
        wq_raw = sp.sb("wq_raw", [P, KC, D])
        wq_hi, wq_lo = sp.sb("wq_hi", [P, KC, D], F32R), sp.sb("wq_lo", [P, KC, D], F32R)
        bq_raw, bq_col, eps = sp.sb("bq_raw", [P, KC]), sp.sb("bq_col", [P, KC]), sp.sb("eps", [P, 1])
        xq, xn = sp.sb("xq", [P, QT, D]), sp.sb("xn", [P, QT, D])
        tq_hi, tq_lo = sp.sb("tq_hi", [P, KC, NT], F32R), sp.sb("tq_lo", [P, KC, NT], F32R)
        q_hi, q_lo = sp.sb("q_hi", [P, KC, NT], F32R), sp.sb("q_lo", [P, KC, NT], F32R)
        tp = [sp.ps(f"tp{i}", [P, NT]) for i in range(KC)]
        bank = [sp.ps(f"bank{i}", [P, NT]) for i in range(6)]
        norm = Norm(sp, "norm")

        wq_loaded, wq_hi_ready, wq_ready = sp.sem("wq_loaded"), sp.sem("wq_hi_ready"), sp.sem("wq_ready")
        x_loaded, xn_ready = sp.sem("x_loaded"), Count(sp.sem("xn_ready"), 1)
        q_turned, tq_hi_ready, tq_ready = Count(sp.sem("q_turned"), 1), sp.sem("tq_hi_ready"), sp.sem("tq_ready")
        q_full, q_hi_ready, q_ready = Count(sp.sem("q_full"), 1), sp.sem("q_hi_ready"), Count(sp.sem("q_ready"), 1)
        q_stored, own = Count(sp.sem("q_stored"), 1), sp.sem("own")
        w_loaded, made = sp.sem("w_loaded"), sp.sem("made")
        w_hi_ready, w_ready = sp.sem("w_hi_ready"), sp.sem("w_ready")
        rows_loaded = [sp.sem(f"rows_loaded{i}") for i in range(2)]
        rows_free = sp.sem("rows_free")
        turned, t_hi_ready, t_ready = sp.sem("turned"), sp.sem("t_hi_ready"), sp.sem("t_ready")
        bank_full, act_free, dve_free = sp.sem("bank_full"), sp.sem("act_free"), sp.sem("dve_free")
        k_hi_ready = sp.sem("k_hi_ready")
        stored = [sp.sem(f"stored{i}") for i in range(2)]
        m_loaded = [sp.sem(f"m_loaded{i}") for i in range(2)]
        m_made, m_stored = sp.sem("m_made"), [sp.sem(f"m_stored{i}") for i in range(2)]
        m1_loaded, spare = sp.sem("m1_loaded"), sp.sem("spare")
        STORES = 6
        block = sp.block()

        @block.gpsimd
        def _(pool):
            make_identity(pool, sp, ident, made)
            pool.memset(eps[:], EPS).then_inc(made, 1)
            pool.sem_inc(rows_free, 2)
            with pool.Fori(0, B) as b:
                xn_ready.wait(pool, b)
                pool.dma_start(xq[:], x[b].rearrange("(s p) d -> p s d", p=P)).then_inc(x_loaded, 16)
                for half in range(2):
                    pool.wait_ge(rows_free, b * 2 + half + 1)
                    pool.dma_start(rows[half][:], ctx[b, half * NT:(half + 1) * NT, :].rearrange(
                        "(s p) d -> p s d", p=P)).then_inc(rows_loaded[half], 16)

        @block.sync
        def _(sync):
            sync.dma_start(w_raw[:, :, 0:D], wk.rearrange("(c p) n -> p c n", p=P)).then_inc(w_loaded, 16)
            sync.dma_start(w_raw[:, :, D:2 * D], wv.rearrange("(c p) n -> p c n", p=P)).then_inc(w_loaded, 16)
            sync.dma_start(w_raw[:, :, 2 * D:], wkv.rearrange("(c p) n -> p c n", p=P)).then_inc(w_loaded, 16)
            sync.dma_start(bk_col[:], bk.rearrange("(c p) -> p c", p=P),
                           allow_slow_non_contiguous=True).then_inc(w_loaded, 16)
            sync.dma_start(bv_row[:], row_of(bv, D)).then_inc(w_loaded, 16)
            sync.dma_start(m1_raw[:], mask1).then_inc(m1_loaded, 16)
            sync.dma_start(wq_raw[:], wq.rearrange("(c p) n -> p c n", p=P)).then_inc(wq_loaded, 16)
            sync.dma_start(bq_raw[:], bq.rearrange("(c p) -> p c", p=P),
                           allow_slow_non_contiguous=True).then_inc(wq_loaded, 16)
            sync.wait_ge(m_made, 1)
            sync.dma_start(bias1, m1_bias[:]).then_inc(m1_loaded, 16)
            with sync.Fori(0, B) as b:
                for half in range(2):
                    n = b * 2 + half
                    cols = slice(half * NT, (half + 1) * NT)
                    mask_rows = [slice((half * 2 + i) * P, (half * 2 + i + 1) * P) for i in range(2)]
                    sync.wait_ge(m_made, n * 2 + 1)
                    apart(sync, spare)
                    for i in range(2):
                        sync.dma_start(m_raw[i][:], mask0[b, mask_rows[i], :]).then_inc(m_loaded[i], 16)
                    sync.wait_ge(dve_free, n * 8 + 2 + 6)
                    for part, src in ((0, k_hi[half]), (1, k_lo[half])):
                        sync.dma_start(k0s[part, b, :, cols].rearrange("(c p) t -> p c t", p=P),
                                       src[:, 0:2, :].bitcast(F32)).then_inc(stored[half], 16)
                        sync.dma_start(k1s[part, b, :, cols].rearrange("(c p) t -> p c t", p=P),
                                       src[:, 2:6, :].bitcast(F32)).then_inc(stored[half], 16)
                    sync.wait_ge(act_free, n * 4 + 4 + 4)
                    sync.dma_start(v1s[b, cols, :].rearrange("(s p) n -> p s n", p=P),
                                   v1_st[half][:]).then_inc(stored[half], 16)
                    sync.wait_ge(dve_free, n * 8 + 2 + 8)
                    sync.dma_start(v0s[b, cols, :].rearrange("(s p) n -> p s n", p=P),
                                   v0_st[half][:]).then_inc(stored[half], 16)
                    for i in range(2):
                        sync.wait_ge(m_made, n * 2 + i + 2)
                        apart(sync, spare)
                        sync.dma_start(bias0[b, mask_rows[i], :], m_bias[i][:]).then_inc(m_stored[i], 16)
                q_ready.wait(sync, b * KC + KC)
                for part, src in ((0, q_hi), (1, q_lo)):
                    sync.dma_start(q0s[part, b].rearrange("(c p) t -> p c t", p=P),
                                   src[:].bitcast(F32)).then_inc(q_stored.sem, 16)
            for half in range(2):
                sync.wait_ge(stored[half], 16 * STORES * B + 1)
                sync.wait_ge(m_stored[half], 16 * 2 * B + 1)
            sync.wait_ge(m1_loaded, 32)
            q_stored.wait(sync, 32 * B)

        @block.tensor
        def _(pe):
            q_turned.start(pe)
            q_full.start(pe)
            pe.wait_ge(made, 2)
            pe.wait_ge(w_ready, KC)
            with pe.Fori(0, B) as b:
                def turn(half):
                    pe.wait_ge(rows_loaded[half], b * 16 + 16)
                    for c in range(KC):
                        for s in range(QT):
                            ins = pe.transpose(tp[c][:, s * P:(s + 1) * P], rows[half][:, s, c * P:(c + 1) * P],
                                               ident[:])
                        ins.then_inc(turned, 1)
                turn(0)
                for half in range(2):
                    n = b * 2 + half
                    pe.wait_ge(t_ready, n * KC + KC)
                    hi, lo = t_hi[half], t_lo[half]
                    for j in range(6):
                        col = j * P if j < 2 else 2 * D + (j - 2) * P
                        if half == 0 and j == 0:
                            q_ready.wait(pe, b * KC)
                        if j < 4:
                            pe.wait_ge(act_free, n * 4 + j + 1)
                        else:
                            pe.wait_ge(dve_free, n * 8 + (j - 4) + 1)
                        product3(pe, bank[j][:], [((w_hi[:, c, col:col + P], w_lo[:, c, col:col + P]),
                                                   (hi[:, c, :], lo[:, c, :])) for c in range(KC)]
                                 ).then_inc(bank_full, 1)
                    if half == 0:
                        turn(1)
                    else:
                        xn_ready.wait(pe, b + 1)
                        for c in range(KC):
                            for s in range(QT):
                                ins = pe.transpose(tp[c][:, s * P:(s + 1) * P], xn[:, s, c * P:(c + 1) * P], ident[:])
                            ins.then_inc(q_turned.sem, 1)
                    for s in range(QT):
                        pe.wait_ge(dve_free, n * 8 + 2 + s + 1)
                        product3(pe, bank[s][:], [((hi[:, c, s * P:(s + 1) * P], lo[:, c, s * P:(s + 1) * P]),
                                                   (w_hi[:, c, 2 * D + I1:], w_lo[:, c, 2 * D + I1:]))
                                                  for c in range(KC)]).then_inc(bank_full, 1)
                    for j in range(2):
                        pe.wait_ge(dve_free, n * 8 + 2 + 4 + j + 1)
                        for s in (2 * j, 2 * j + 1):
                            ins = product3(pe, bank[4 + j][:, (s % 2) * D:(s % 2 + 1) * D],
                                           [((hi[:, c, s * P:(s + 1) * P], lo[:, c, s * P:(s + 1) * P]),
                                             (w_hi[:, c, D:2 * D], w_lo[:, c, D:2 * D])) for c in range(KC)])
                        ins.then_inc(bank_full, 1)
                pe.wait_ge(tq_ready, b * KC + KC)
                pe.wait_ge(wq_ready, KC)
                for j in range(KC):
                    pe.wait_ge(act_free, (b * 2 + 2) * 4 + j + 1)
                    product3(pe, bank[j][:], [((wq_hi[:, c, j * P:(j + 1) * P], wq_lo[:, c, j * P:(j + 1) * P]),
                                               (tq_hi[:, c, :], tq_lo[:, c, :])) for c in range(KC)]
                             ).then_inc(q_full.sem, 1)

        @block.scalar
        def _(act):
            act.wait_ge(w_loaded, 80)
            for c in range(KC):
                act.activation(w_hi[:, c, :], w_raw[:, c, :], ACT.Copy).then_inc(w_hi_ready, 1)
            act.wait_ge(wq_loaded, 32)
            for c in range(KC):
                act.activation(wq_hi[:, c, :], wq_raw[:, c, :], ACT.Copy, scale=neg_scale).then_inc(wq_hi_ready, 1)
            act.activation(bq_col[:], bq_raw[:], ACT.Copy, scale=neg_scale).then_inc(wq_hi_ready, 1)
            act.wait_ge(wq_hi_ready, KC + 1)
            act.wait_ge(made, 3)
            q_stored.start(act)
            act.sem_inc(act_free, 4)
            act.sem_inc(stored[0], 1)
            act.sem_inc(stored[1], 1)
            with act.Fori(0, B) as b:
                def rows_high(half):
                    for c in range(KC):
                        act.wait_ge(turned, (b * 2 + half) * KC + c + 1)
                        act.activation(t_hi[half][:, c, :], tp[c][:], ACT.Copy).then_inc(t_hi_ready, 1)
                rows_high(0)
                for half in range(2):
                    n = b * 2 + half
                    act.wait_ge(stored[half], b * (16 * STORES) + 1)
                    for j in range(6):
                        act.wait_ge(bank_full, n * 12 + j + 1)
                        if j < 2:
                            ins = act.activation(k_hi[half][:, j, :], bank[j][:], ACT.Identity, bias=bk_col[:, j:j + 1])
                        else:
                            ins = act.activation(k_hi[half][:, j, :], bank[j][:], ACT.Copy)
                        ins.then_inc(k_hi_ready, 1)
                    if half == 0:
                        rows_high(1)
                    else:
                        q_full.wait(act, b * KC)
                        for c in range(KC):
                            q_turned.wait(act, b * KC + c + 1)
                            act.activation(tq_hi[:, c, :], tp[c][:], ACT.Copy).then_inc(tq_hi_ready, 1)
                    for s in range(QT):
                        act.wait_ge(bank_full, n * 12 + 6 + s + 1)
                        act.activation(v1_st[half][:, s, :], bank[s][:], ACT.Copy).then_inc(act_free, 1)
                    if half == 0:
                        norm.scalar(act, b, eps[:])
                q_stored.wait(act, b * 32)
                for j in range(KC):
                    q_full.wait(act, b * KC + j + 1)
                    act.activation(q_hi[:, j, :], bank[j][:], ACT.Identity, bias=bq_col[:, j:j + 1]
                                   ).then_inc(q_hi_ready, 1)

        @block.vector
        def _(dve):
            dve.sem_inc(dve_free, 2)
            xn_ready.start(dve)
            q_ready.start(dve)
            for i in range(2):
                dve.sem_inc(m_stored[i], 1)
            dve.wait_ge(m1_loaded, 16)
            dve.tensor_scalar(m1_bias[:], m1_raw[:], 0.0, BIG, ALU.is_equal, ALU.mult).then_inc(m_made, 1)
            for c in range(KC):
                dve.wait_ge(w_hi_ready, c + 1)
                dve.tensor_tensor(w_lo[:, c, :], w_raw[:, c, :], w_hi[:, c, :].bitcast(F32),
                                  ALU.subtract).then_inc(w_ready, 1)
            for c in range(KC):
                dve.wait_ge(wq_hi_ready, c + 1)
                dve.scalar_tensor_tensor(wq_lo[:, c, :], wq_raw[:, c, :], neg_scale, wq_hi[:, c, :].bitcast(F32),
                                         ALU.mult, ALU.subtract).then_inc(wq_ready, 1)
            with dve.Fori(0, B) as b:
                steps = Steps(dve, own, 3, b)

                def rows_low(half):
                    for c in range(KC):
                        dve.wait_ge(t_hi_ready, (b * 2 + half) * KC + c + 1)
                        dve.tensor_tensor(t_lo[half][:, c, :], tp[c][:], t_hi[half][:, c, :].bitcast(F32),
                                          ALU.subtract).then_inc(t_ready, 1)
                    dve.sem_inc(rows_free, 1)
                rows_low(0)
                for half in range(2):
                    n = b * 2 + half
                    dve.wait_ge(stored[half], b * (16 * STORES) + 1)
                    for j in range(6):
                        dve.wait_ge(k_hi_ready, n * 6 + j + 1)
                        if j < 2:
                            ins = dve.scalar_tensor_tensor(k_lo[half][:, j, :], bank[j][:], bk_col[:, j:j + 1],
                                                           k_hi[half][:, j, :].bitcast(F32), ALU.add, ALU.subtract)
                        else:
                            ins = dve.tensor_tensor(k_lo[half][:, j, :], bank[j][:],
                                                    k_hi[half][:, j, :].bitcast(F32), ALU.subtract)
                        ins.then_inc(dve_free, 1)
                    if half == 0:
                        rows_low(1)
                    else:
                        for c in range(KC):
                            dve.wait_ge(tq_hi_ready, b * KC + c + 1)
                            dve.tensor_tensor(tq_lo[:, c, :], tp[c][:], tq_hi[:, c, :].bitcast(F32),
                                              ALU.subtract).then_inc(tq_ready, 1)
                    for j in range(2):
                        dve.wait_ge(bank_full, n * 12 + 10 + j + 1)
                        for s in range(2):
                            ins = dve.tensor_tensor(v0_st[half][:, 2 * j + s, :], bank[4 + j][:, s * D:(s + 1) * D],
                                                    bv_row[:], ALU.add)
                        ins.then_inc(dve_free, 1)
                    for i in range(2):
                        dve.wait_ge(m_loaded[i], n * 16 + 16)
                        dve.wait_ge(m_stored[i], n * 16 + 1)
                        apart(dve, spare)
                        dve.tensor_scalar(m_bias[i][:], m_raw[i][:], 0.0, BIG, ALU.is_equal, ALU.mult
                                          ).then_inc(m_made, 1)
                    if half == 0:
                        dve.wait_ge(x_loaded, b * 16 + 16)
                        q_turned.wait(dve, b * KC)
                        norm.vector(dve, steps, b, [xq[:, s, :] for s in range(QT)], [xn[:, s, :] for s in range(QT)],
                                    spare=spare)
                        dve.sem_inc(xn_ready.sem, 1)
                        steps.close()
                for j in range(KC):
                    dve.wait_ge(q_hi_ready, b * KC + j + 1)
                    dve.scalar_tensor_tensor(q_lo[:, j, :], bank[j][:], bq_col[:, j:j + 1],
                                             q_hi[:, j, :].bitcast(F32), ALU.add, ALU.subtract).then_inc(q_ready.sem, 1)


def stage_attention(nc, tag, heads, dh, q_s, k_s, v_s, o_s, bias_s, null_s=None, null_kv=None, clear=None):
    with Space(nc, tag) as sp:
        null = null_kv is not None
        WIDE = P // 2
        group, GC = WIDE // dh, 4
        groups, CH = heads // group, GC * (WIDE // dh)
        chunks = heads // CH
        R = 2 * CH if null else CH
        RR = 3 * R if null else 2 * R
        stacked = 3 * dh <= P
        per_query = len(bias_s.shape) == 3
        rows_q = 3 * dh if stacked else 2 * dh
        NP, NB4 = 4, 4
        qs = [sp.sb(f"qs{i}", [rows_q, S], F32R) for i in range(2)]
        ks = [sp.sb(f"ks{i}", [rows_q, CTX], F32R) for i in range(2)]
        kl = None if stacked else [sp.sb(f"kl{i}", [dh, CTX], F32R) for i in range(2)]
        v_raw = [sp.sb(f"v_raw{i}", [P, KT, WIDE]) for i in range(2)]
        vz = [sp.sb(f"vz{i}", [P, KT, group, P], F32R) for i in range(2)]
        bias = sp.sb("bias", [P, QT if per_query else 1, CTX], BF16)
        p = [sp.sb(f"p{i}", [P, QT, CTX]) for i in range(NP)]
        pt_hi = [sp.sb(f"pt_hi{i}", [P, NT], F32R) for i in range(NB4)]
        pt_lo = [sp.sb(f"pt_lo{i}", [P, NT], F32R) for i in range(NB4)]
        nmax, sums = sp.sb("nmax", [P, heads, QT]), sp.sb("sums", [P, heads, QT])
        dn, tot = sp.sb("dn", [P, CH, QT]), sp.sb("tot", [P, CH, QT])
        wcols, rcols = sp.sb("wcols", [P, QT, R]), sp.sb("rcols", [P, QT, RR], F32R)
        rrows = sp.sb("rrows", [RR, S], F32R)
        ident = sp.sb("ident", [P, P])
        sel_raw = sp.sb("sel_raw", [R, GC, 2, WIDE])
        sel = sp.sb("sel", [RR, GC, P], F32R)
        o_raw, o_out = sp.sb("o_raw", [P, GC, S]), [sp.sb(f"o_out{i}", [P, S]) for i in range(2)]
        s_ps = [sp.ps(f"s{i}", [P, CTX]) for i in range(2)]
        t_ps = [sp.ps(f"t{i}", [P, NT]) for i in range(2)]
        o_ps, f_ps = sp.ps("o", [P, NT]), sp.ps("f", [P, NT])
        if null:
            nv_raw = sp.sb("nv_raw", [R, GC, 2, WIDE])
            nv_hi, nv_lo = sp.sb("nv_hi", [R, GC, P], F32R), sp.sb("nv_lo", [R, GC, P], F32R)
            nv = sp.sb("nv", [RR, GC, P], F32R)
            sn = sp.sb("sn", [P, heads, QT])
            pn = sp.sb("pn", [P, CH, QT])

        if null:
            ENDS = [(2, 0, 0), (3, 0, 1), (4, 1, 0), (5, 1, 1), (6, 2, 0), (7, 2, 1), (12, 3, 0), (13, 3, 1)]
        else:
            ENDS = [(2, 0, 0), (3, 1, 0), (4, 2, 0), (12, 3, 0)]
        NE = len(ENDS)
        LAST = [max(n for n, e in enumerate(ENDS) if e[1] == g) for g in range(GC)]
        COLS, TOT = 7, 2 if null else 4
        if null:
            COLS_AT = {2: ((), (1,)), 5: ((2,), (3,)), 6: ((4,), (5,)), 7: ((6,), (7,))}
        else:
            COLS_AT = {2: ((), (1,)), 3: ((2,), ()), 4: ((3,), ()), 5: ((4,), ()), 6: ((5,), (6,)), 7: ((7,), ())}
        QK = 6 if stacked else 5
        SCORE_AT = MAX_AT = {0: 6, 2: 7, 4: 8, 6: 9}
        EXP_AT = {0: 5, 2: 6, 4: 7, 6: 8}

        made, nv_loaded, sel_put = sp.sem("made"), sp.sem("nv_loaded"), sp.sem("sel_put")
        qk_loaded = [sp.sem(f"qk_loaded{i}") for i in range(2)]
        v_loaded = [sp.sem(f"v_loaded{i}") for i in range(2)]
        v_hi_ready, v_split = sp.sem("v_hi_ready"), Count(sp.sem("v_split"), group + 1)
        bias_loaded = [sp.sem(f"bias_loaded{t}") for t in range(QT)]
        sn_loaded = sp.sem("sn_loaded")
        scored = Count(sp.sem("scored"), 2 * QT)
        maxed = Count(sp.sem("maxed"), heads * QT)
        exped = Count(sp.sem("exped"), 2)
        turned = Count(sp.sem("turned"), NP * KT)
        hi_moved = Count(sp.sem("hi_moved"), 2)
        lo_moved = Count(sp.sem("lo_moved"), 2)
        weighed = Count(sp.sem("weighed"), 2 * KT * group)
        o_copied = Count(sp.sem("o_copied"), 1)
        cols = Count(sp.sem("cols"), COLS)
        null_exped = sp.sem("null_exped")
        rows_turned = Count(sp.sem("rows_turned"), 1)
        rows_ready = sp.sem("rows_ready")
        f_made = Count(sp.sem("f_made"), 1)
        f_used = Count(sp.sem("f_used"), NE + 1)
        stored = [Count(sp.sem(f"stored{i}"), 32) for i in range(2)]
        spare = sp.sem("spare")
        if clear is not None:
            CB = clear.shape[0] // P
            CB_B = CB // B
            zeros = sp.sb("zeros", [P, CB_B, D])
            zeros_made, cleared = sp.sem("zeros_made"), sp.sem("cleared")

            def clear_blocks(eng, at, n):
                eng.dma_start(clear[bass.ds(at * P, n * P), :].rearrange("(s p) d -> p s d", p=P), zeros[:, 0:n, :]
                              ).then_inc(cleared, 16)
        MADE = 13 if null else 8
        block = sp.block()

        def end_at(j, t):
            if j > 0 and j % CH == CH - 1:
                chunk, slot = j // CH, t
            elif j % CH == 0 and j:
                chunk, slot = j // CH - 1, KT + t
            else:
                return None
            for n, (at, g, part) in enumerate(ENDS):
                if at == slot:
                    return chunk, n, g, part
            return None

        def tile_at(course, b, j, t):
            tile = QT * j + course[t] if t in course else None
            if tile is not None and isinstance(b, int) and b == B - 1 and tile >= heads * QT:
                return None
            return tile

        def run(eng, slot):
            for t in range(KT):
                slot(0, 0, t)
            with eng.Fori(0, B - 1) as b:
                for j in range(1, heads + 1):
                    for t in range(KT):
                        slot(b, j, t)
            for j in range(1, heads):
                for t in range(KT):
                    slot(B - 1, j, t)

        @block.gpsimd
        def _(pool):
            v_split.start(pool)
            pool.memset(ident[:], 0.0).then_inc(made, 1)
            pool.memset(sel_raw[:], 1.0).then_inc(made, 1)
            pool.wait_ge(made, 2)
            pool.affine_select(out=ident[:], in_=ident[:], compare_op=ALU.not_equal, fill=1.0, base=0,
                               pattern=[[-1, P]], channel_multiplier=1).then_inc(made, 1)
            for i in range(2):
                pool.memset(vz[i][:].bitcast(F32), 0.0).then_inc(made, 1)
            pool.memset(sel[:].bitcast(F32), 0.0).then_inc(made, 1)
            n = 6

            def only(raw, first, n):
                pool.affine_select(out=raw[:], in_=raw[:], compare_op=ALU.is_ge, fill=0.0, base=dh * first,
                                   pattern=[[WIDE, GC], [0, 2], [1, WIDE]], channel_multiplier=-dh).then_inc(made, 1)
                pool.wait_ge(made, n + 1)
                pool.affine_select(out=raw[:], in_=raw[:], compare_op=ALU.is_ge, fill=0.0,
                                   base=dh - 1 - dh * first, pattern=[[-WIDE, GC], [0, 2], [-1, WIDE]],
                                   channel_multiplier=dh).then_inc(made, 1)
                pool.wait_ge(made, n + 2)
            only(sel_raw, 0, n)
            if null:
                pool.memset(nv_raw[:, :, 1, :], 0.0).then_inc(made, 1)
                pool.wait_ge(made, n + 3)
                pool.wait_ge(nv_loaded, 16 * GC)
                only(nv_raw, CH, n + 3)
                flat = nv_raw[:].rearrange("r g a c -> r g (a c)")
                pool.tensor_copy(nv_hi[:], flat).then_inc(made, 1)
                pool.wait_ge(made, n + 6)
                pool.tensor_tensor(nv_lo[:], flat, nv_hi[:].bitcast(F32), ALU.subtract).then_inc(made, 1)

            pool.wait_ge(made, MADE)
            for i in range(RR // R):
                if i < 2:
                    pool.dma_start(sel[i * R:(i + 1) * R].bitcast(F32),
                                   sel_raw[:].rearrange("r g a c -> r g (a c)")).then_inc(sel_put, 16)
                if null:
                    pool.dma_start(nv[i * R:(i + 1) * R].bitcast(F32), (nv_hi, nv_hi, nv_lo)[i][:].bitcast(F32)
                                   ).then_inc(sel_put, 16)

            if clear is not None:
                pool.memset(zeros[:], 0.0).then_inc(zeros_made, 1)

            def split_v(b, g):
                i, k = g % 2, b * groups + g
                pool.wait_ge(v_loaded[i], (b * (groups // 2) + g // 2) * 16 + 16)
                weighed.wait(pool, (k - 1) * KT * group)
                apart(pool, spare)
                for e in range(group):
                    pool.tensor_copy(vz[i][:, :, e, e * dh:(e + 1) * dh], v_raw[i][:, :, e * dh:(e + 1) * dh]
                                     ).then_inc(v_hi_ready, 1)
                pool.wait_ge(v_hi_ready, k * group + group)
                apart(pool, spare)
                for e in range(group):
                    ins = pool.tensor_tensor(vz[i][:, :, e, WIDE + e * dh:WIDE + (e + 1) * dh],
                                             v_raw[i][:, :, e * dh:(e + 1) * dh],
                                             vz[i][:, :, e, e * dh:(e + 1) * dh].bitcast(F32), ALU.subtract)
                    ins.then_inc(v_split.sem, 1)

            with pool.Fori(0, B) as b:
                for g in range(groups):
                    split_v(b, g)

        @block.sync
        def _(sync):
            if null:
                for g in range(GC):
                    sync.dma_start(nv_raw[:, g, 0, :], null_kv[1:2, :].broadcast_to([R, dh])).then_inc(nv_loaded, 16)

            def load_qk(b, j):
                i, rows = j % 2, slice(j * dh, (j + 1) * dh)
                scored.wait(sync, (b * heads + j - 1) * QT)
                apart(sync, spare)
                for n, part in enumerate((0, 1, 0) if stacked else (0, 1)):
                    sync.dma_start(qs[i][n * dh:(n + 1) * dh, :].bitcast(F32), q_s[part, b, rows, :]
                                   ).then_inc(qk_loaded[i], 16)
                for n, part in enumerate((0, 0, 1) if stacked else (0, 0)):
                    sync.dma_start(ks[i][n * dh:(n + 1) * dh, :].bitcast(F32), k_s[part, b, rows, :]
                                   ).then_inc(qk_loaded[i], 16)
                if not stacked:
                    sync.dma_start(kl[i][:].bitcast(F32), k_s[1, b, rows, :]).then_inc(qk_loaded[i], 16)

            def load_v(b, g):
                v_split.wait(sync, (b * groups + g - 1) * group)
                sync.dma_start(v_raw[g % 2][:], v_s[b, :, g * WIDE:(g + 1) * WIDE].rearrange("(t p) d -> p t d", p=P)
                               ).then_inc(v_loaded[g % 2], 16)

            def load_bias(b, t):
                maxed.wait(sync, ((b - 1) * heads + heads - 1) * QT + t + 1)
                apart(sync, spare)
                if per_query:
                    sync.dma_start(bias[:, t, :], bias_s[b, t * P:(t + 1) * P, :]).then_inc(bias_loaded[t], 16)
                elif t == 0:
                    maxed.wait(sync, b * heads * QT)
                    sync.dma_start(bias[:, 0, :], bias_s[bass.ds(b, 1), :].broadcast_to([P, CTX])
                                   ).then_inc(bias_loaded[0], 16)

            with sync.Fori(0, B) as b:
                for j in range(heads):
                    load_qk(b, j)
                    if j == 0:
                        for t in range(QT if per_query else 1):
                            load_bias(b, t)
                        if null:
                            cols.wait(sync, (b * chunks - 1) * COLS + 1)
                            apart(sync, spare)
                            sync.dma_start(sn[:], null_s[b]).then_inc(sn_loaded, 16)
                    if j % group == 0:
                        load_v(b, j // group)
                    if clear is not None and j == heads // 2:
                        sync.wait_ge(zeros_made, 1)
                        clear_blocks(sync, b * CB_B, CB_B)
            if clear is not None:
                clear_blocks(sync, B * CB_B, CB - B * CB_B)
                sync.wait_ge(cleared, 16 * (B + 1))

        @block.tensor
        def _(pe):
            scored.start(pe)
            turned.start(pe)
            weighed.start(pe)
            rows_turned.start(pe)
            f_made.start(pe)
            pe.wait_ge(made, 3)

            def scores(b, tile):
                j, t = tile // QT, tile % QT
                i = j % 2
                if t == 0:
                    pe.wait_ge(qk_loaded[i], (b * (heads // 2) + j // 2 + 1) * 16 * QK)
                exped.wait(pe, b * heads * QT + tile - 1)
                for half in range(2):
                    at = slice(half * NT, (half + 1) * NT)
                    out = s_ps[t % 2][:, at]
                    ins = pe.matmul(out, qs[i][:, t * P:(t + 1) * P], ks[i][:, at], start=True, stop=stacked)
                    if not stacked:
                        ins = pe.matmul(out, qs[i][0:dh, t * P:(t + 1) * P], kl[i][:, at], start=False, stop=True)
                ins.then_inc(scored.sem, 1)

            def turn(b, j, t):
                h = b * heads + j
                if t == 0:
                    exped.wait(pe, h * QT + QT)
                lo_moved.wait(pe, h * KT + t - 1)
                for u in range(QT):
                    ins = pe.transpose(t_ps[t % 2][:, u * P:(u + 1) * P], p[j % NP][:, u, t * P:(t + 1) * P], ident[:])
                ins.then_inc(turned.sem, 1)

            def weigh(b, j, t):
                if t < 0:
                    j, t = j - 1, t + KT
                h, g, e = b * heads + j, j // group, j % group
                i = g % 2
                if t == 0 and e == 0:
                    v_split.wait(pe, (b * groups + g + 1) * group)
                    o_copied.wait(pe, b * groups + g)
                first, last = t == 0 and e == 0, t == KT - 1 and e == group - 1
                lo_moved.wait(pe, h * KT + t + 1)
                pe.matmul(o_ps[:], vz[i][:, t, e, :], pt_hi[t % NB4][:], start=first, stop=False)
                pe.matmul(o_ps[:], vz[i][:, t, e, :], pt_lo[t % NB4][:], start=False, stop=last
                          ).then_inc(weighed.sem, 1)

            def turn_rows(b, chunk):
                k = b * chunks + chunk
                pe.wait_ge(sel_put, 16 * (5 if null else 2))
                cols.wait(pe, k * COLS + COLS)
                f_used.wait(pe, k * NE)
                for u in range(QT):
                    ins = pe.transpose(f_ps[0:RR, u * P:(u + 1) * P], rcols[:, u, :].bitcast(F32), ident[:])
                ins.then_inc(rows_turned.sem, 1)

            def factors(b, chunk, n, g, part):
                k = b * chunks + chunk
                if n == 0:
                    pe.wait_ge(rows_ready, k + 1)
                f_used.wait(pe, k * NE + n)
                pe.matmul(f_ps[:], (nv if part else sel)[:, g, :], rrows[:], start=True, stop=True
                          ).then_inc(f_made.sem, 1)

            def slot(b, j, t):
                turn(b, j, t)
                if t % 2 == 0 and (j or t >= 4):
                    weigh(b, j, t - 3)
                if tile_at(SCORE_AT, b, j, t):
                    scores(b, tile_at(SCORE_AT, b, j, t))
                if j % CH == CH - 1 and t == 0:
                    turn_rows(b, j // CH)
                if end_at(j, t):
                    factors(b, *end_at(j, t))
                if t % 2 == 0 and (j or t >= 2):
                    weigh(b, j, t - 2)

            for tile in range(6):
                scores(0, tile)
            run(pe, slot)
            for t in range(KT - 3, KT):
                weigh(B - 1, heads - 1, t)
            for t in range(KT):
                if end_at(heads, t):
                    factors(B - 1, *end_at(heads, t))

        @block.scalar
        def _(act):
            exped.start(act)
            hi_moved.start(act)
            o_copied.start(act)
            for i in range(2):
                stored[i].start(act)

            def exps(b, tile):
                j, t = tile // QT, tile % QT
                jb = j % heads
                maxed.wait(act, b * heads * QT + tile + 1)
                turned.wait(act, (b * heads + j + 1 - NP) * KT)
                if tile == heads * QT:
                    cols.wait(act, (b * chunks + chunks - 1) * COLS + TOT)
                act.activation(p[j % NP][:, t, :], s_ps[t % 2][:], ACT.Exp, bias=nmax[:, jb, t:t + 1], scale=-1.0,
                               accum_out=sums[:, jb, t:t + 1]).then_inc(exped.sem, 1)

            def move(b, j, t):
                n = (b * heads + j) * KT + t
                turned.wait(act, n + 1)
                weighed.wait(act, n - NB4 + 1)
                act.activation(pt_hi[t % NB4][:], t_ps[t % 2][:], ACT.Copy).then_inc(hi_moved.sem, 1)

            def copy_o(b, g):
                k = b * groups + g
                weighed.wait(act, (k + 1) * KT * group)
                f_used.wait(act, (b * chunks + g // GC - 1) * NE + LAST[g % GC] + 1)
                act.activation(o_raw[:, g % GC, :], o_ps[:], ACT.Copy).then_inc(o_copied.sem, 1)

            def null_exps(b, chunk):
                k = b * chunks + chunk
                cols.wait(act, k * COLS + 1)
                act.activation(pn[:], dn[:], ACT.Exp).then_inc(null_exped, 1)

            def copy_rows(b, chunk):
                k = b * chunks + chunk
                rows_turned.wait(act, k + 1)
                f_made.wait(act, k * NE)
                act.activation(rrows[:], f_ps[0:RR, :], ACT.Copy).then_inc(rows_ready, 1)

            def store(b, chunk, n, g):
                k = b * chunks + chunk
                i, at = g % 2, slice((chunk * GC + g) * WIDE, (chunk * GC + g + 1) * WIDE)
                f_used.wait(act, k * NE + n + 1)
                for part in range(2):
                    act.dma_start(o_s[b, part, at, :], o_out[i][part * WIDE:(part + 1) * WIDE, :]
                                  ).then_inc(stored[i].sem, 16)

            def slot(b, j, t):
                move(b, j, t)
                if t == 3 and null and (j + 1) % CH == CH - 1:
                    null_exps(b, j // CH)
                if j and j % group == 0 and t == 2:
                    copy_o(b, j // group - 1)
                if tile_at(EXP_AT, b, j, t):
                    exps(b, tile_at(EXP_AT, b, j, t))
                if j % CH == CH - 1 and t == 0:
                    copy_rows(b, j // CH)
                before = end_at(j, t - 1) if t else end_at(j - 1, KT - 1)
                if before:
                    chunk, n, g, _ = before
                    if n == LAST[g]:
                        store(b, chunk, n, g)

            for tile in range(5):
                exps(0, tile)
            run(act, slot)
            copy_o(B - 1, groups - 1)
            for before in [end_at(heads - 1, KT - 1)] + [end_at(heads, t) for t in range(KT)]:
                if before and before[1] == LAST[before[2]]:
                    store(B - 1, *before[:3])
            for i in range(2):
                stored[i].wait(act, 32 * B * groups // 2)

        @block.vector
        def _(dve):
            maxed.start(dve)
            lo_moved.start(dve)
            cols.start(dve)
            f_used.start(dve)

            def biased_max(b, tile):
                j, t = tile // QT, tile % QT
                jb, rows = j % heads, b * heads + j - j % heads
                if jb == 0 and (per_query or t == 0):
                    dve.wait_ge(bias_loaded[t], (b + j // heads) * 16 + 16)
                    if null and t == 0:
                        dve.wait_ge(sn_loaded, (b + j // heads) * 16 + 16)
                if tile == heads * QT:
                    cols.wait(dve, (b * chunks + chunks - 1) * COLS + 1)
                scored.wait(dve, b * heads * QT + tile + 1)
                apart(dve, spare)
                dve.tensor_tensor_reduce(s_ps[t % 2][:], s_ps[t % 2][:], bias[:, t if per_query else 0, :],
                                         1.0, sn[:, jb, t:t + 1] if null else BIG, ALU.add, ALU.min,
                                         nmax[:, jb, t:t + 1]).then_inc(maxed.sem, 1)

            def move(b, j, t):
                n = (b * heads + j) * KT + t
                hi_moved.wait(dve, n + 1)
                weighed.wait(dve, n - NB4 + 1)
                dve.tensor_tensor(pt_lo[t % NB4][:], t_ps[t % 2][:], pt_hi[t % NB4][:].bitcast(F32), ALU.subtract
                                  ).then_inc(lo_moved.sem, 1)

            def column_step(b, chunk, n):
                k = b * chunks + chunk
                hs = slice(chunk * CH, (chunk + 1) * CH)
                heads_first = wcols[:, :, 0:CH].rearrange("p t e -> p e t")
                if n > 1:
                    cols.wait(dve, k * COLS + n - 1)
                if n == 1:
                    maxed.wait(dve, (b * heads + (chunk + 1) * CH) * QT)
                if n == TOT:
                    exped.wait(dve, (b * heads + (chunk + 1) * CH) * QT)
                if null:
                    if n == 1:
                        ins = dve.tensor_tensor(dn[:], nmax[:, hs, :], sn[:, hs, :], ALU.subtract)
                    elif n == 2:
                        dve.wait_ge(null_exped, k + 1)
                        ins = dve.tensor_tensor(tot[:], sums[:, hs, :], pn[:], ALU.add)
                    elif n == 3:
                        ins = dve.reciprocal(heads_first, tot[:])
                    elif n == 4:
                        ins = dve.tensor_tensor(wcols[:, :, CH:R].rearrange("p t e -> p e t"), heads_first, pn[:],
                                                ALU.mult)
                else:
                    if n == 1:
                        ins = dve.tensor_scalar(dn[:], nmax[:, hs, :], BIG / 2, BIG, ALU.is_ge, ALU.mult)
                    elif n == 2:
                        ins = dve.tensor_scalar(dn[:], dn[:], 4.0, None, ALU.mult)
                    elif n == 3:
                        ins = dve.tensor_tensor(dn[:], dn[:], dn[:], ALU.subtract)
                    elif n == 4:
                        ins = dve.tensor_tensor(tot[:], sums[:, hs, :], dn[:], ALU.add)
                    elif n == 5:
                        ins = dve.reciprocal(heads_first, tot[:])
                if n == COLS - (2 if null else 1):
                    rows_turned.wait(dve, k)
                    ins = dve.tensor_copy(rcols[:, :, 0:R], wcols[:])
                elif n == COLS - (1 if null else 0):
                    ins = dve.tensor_tensor(rcols[:, :, R:2 * R], wcols[:], rcols[:, :, 0:R].bitcast(F32), ALU.subtract)
                elif n == COLS:
                    ins = dve.tensor_copy(rcols[:, :, 2 * R:], rcols[:, :, 0:R].bitcast(F32))
                ins.then_inc(cols.sem, 1)

            def use(b, chunk, n, g, part):
                k = b * chunks + chunk
                i = g % 2
                f_made.wait(dve, k * NE + n + 1)
                if part == 0:
                    o_copied.wait(dve, k * GC + g + 1)
                    stored[i].wait(dve, (k * (GC // 2) + g // 2) * 32)
                    ins = dve.tensor_tensor(o_out[i][:], o_raw[:, g, :], f_ps[:], ALU.mult)
                else:
                    f_used.wait(dve, k * NE + n)
                    ins = dve.tensor_tensor(o_out[i][:], o_out[i][:], f_ps[:], ALU.add)
                ins.then_inc(f_used.sem, 1)

            def slot(b, j, t):
                steps = COLS_AT.get(t, ((), ())) if (j + 1) % CH == CH - 1 else ((), ())
                move(b, j, t)
                for n in steps[0]:
                    column_step(b, j // CH, n)
                if tile_at(MAX_AT, b, j, t):
                    biased_max(b, tile_at(MAX_AT, b, j, t))
                for n in steps[1]:
                    column_step(b, j // CH, n)
                if end_at(j, t):
                    use(b, *end_at(j, t))

            for tile in range(6):
                biased_max(0, tile)
            run(dve, slot)
            for t in range(KT):
                if end_at(heads, t):
                    use(B - 1, *end_at(heads, t))


T = 384
TS = T // P
TOP = 2
J = (TOP * N - E) // T + E
SLOTS = J * T
NB = N // P
HC = HID // P
BW = 2 * HC + KC


def stage_route(nc, x, o0s, wo, bo, gate, tokens, b1, b2, b3, x1s, xgs, pos_s, tile_s, bias_s):
    with Space(nc, "r") as sp:
        w_raw = sp.sb("w_raw", [P, KC, D])
        w_hi, w_lo = sp.sb("w_hi", [P, KC, D], F32R), sp.sb("w_lo", [P, KC, D], F32R)
        bo_row, tanh_g, g_raw = sp.sb("bo_row", [P, D]), sp.sb("tanh_g", [P, 1]), sp.sb("g_raw", [P, 1])
        eps, ident, ones, tri = (sp.sb("eps", [P, 1]), sp.sb("ident", [P, P]), sp.sb("ones", [P, P]),
                                 sp.sb("tri", [P, P]))
        tok_t = sp.sb("tok_t", [P, KC, E])
        tok_raw = sp.sb("tok_raw", [E, D])
        brows = [sp.sb("b1rows", [E * HC, P]), sp.sb("b2rows", [E * HC, P]), sp.sb("b3rows", [E * KC, P])]
        bcols = sp.sb("bcols", [P, E, BW])
        iota_e = sp.sb("iota_e", [P, NB, E])
        iota_j = sp.sb("iota_j", [P, J + 2])
        xin = sp.sb("xin", [P, B, QT, D])
        xn = sp.sb("xn", [P, NB, D])
        ot = [sp.sb(f"ot{i}", [P, KC, NT]) for i in range(2)]
        ot2 = [sp.sb(f"ot2_{i}", [P, KC, NT]) for i in range(2)]
        ot_hi, ot_lo = sp.sb("ot_hi", [P, KC, NT], F32R), sp.sb("ot_lo", [P, KC, NT], F32R)
        tmp = sp.sb("tmp", [P, QT, D])
        xt = sp.sb("xt", [P, KC, NT])
        scores = sp.sb("scores", [P, NB, E])
        best, best_i = sp.sb("best", [P, NB, 8]), sp.sb("best_i", [P, NB, 8], U32)
        pick = sp.sb("pick", [P, TOP, NB])
        hot = sp.sb("hot", [P, TOP, NB, E])
        both, before = sp.sb("both", [P, NB, E]), sp.sb("before", [P, NB + 1, E])
        tiles, cum = sp.sb("tiles", [P, E]), sp.sb("cum", [P, E + 1])
        slot, mine = sp.sb("slot", [P, NB, E]), sp.sb("mine", [P, TOP, NB, E])
        pos_f, pos = sp.sb("pos_f", [P, TOP, NB]), sp.sb("pos", [P, TOP, NB], I32)
        tile_f, tile_i = sp.sb("tile_f", [P, J + 2]), sp.sb("tile_i", [P, J + 2], I32)
        bank = [sp.ps(f"bank{i}", [P, 2, D]) for i in range(2)]
        tp = [sp.ps(f"tp{i}", [P, NT]) for i in range(KC)]
        sc_ps, rank_ps, tot_ps = sp.ps("sc", [P, QT, E]), sp.ps("rank", [P, NB, E]), sp.ps("tot", [P, NB, E])
        b_ps = sp.ps("b_ps", [P, 2 * E * HC + E * KC + KC * E])
        norm = Norm(sp, "norm")

        loaded, x_loaded, made = sp.sem("loaded"), [sp.sem(f"x_loaded{b}") for b in range(B)], sp.sem("made")
        o_loaded = [sp.sem(f"o_loaded{i}") for i in range(2)]
        w_hi_ready, w_ready = sp.sem("w_hi_ready"), sp.sem("w_ready")
        o_whole = sp.sem("o_whole")
        o_hi_ready, o_ready, full = sp.sem("o_hi_ready"), sp.sem("o_ready"), sp.sem("full")
        xn_ready, turned, xt_ready = sp.sem("xn_ready"), sp.sem("turned"), sp.sem("xt_ready")
        scored, sc_moved = sp.sem("scored"), sp.sem("sc_moved")
        b_turned, b_moved, counted, both_ready = (sp.sem("b_turned"), sp.sem("b_moved"), sp.sem("counted"),
                                                  sp.sem("both_ready"))
        placed, scattered, stored, own = sp.sem("placed"), sp.sem("scattered"), sp.sem("stored"), sp.sem("own")
        x1_ready = sp.sem("x1_ready")
        MADE = 7
        block = sp.block()
        BC = [0, E * HC, 2 * E * HC, 2 * E * HC + E * KC]

        @block.gpsimd
        def _(pool):
            pool.memset(eps[:], EPS).then_inc(made, 1)
            pool.memset(ident[:], 0.0).then_inc(made, 1)
            pool.memset(ones[:], 1.0).then_inc(made, 1)
            pool.wait_ge(made, 3)
            pool.affine_select(out=ident[:], in_=ident[:], compare_op=ALU.not_equal, fill=1.0, base=0,
                               pattern=[[-1, P]], channel_multiplier=1).then_inc(made, 1)
            pool.affine_select(out=tri[:], in_=ones[:], compare_op=ALU.is_ge, fill=0.0, base=-1,
                               pattern=[[1, P]], channel_multiplier=-1).then_inc(made, 1)
            pool.iota(iota_e[:], [[0, NB], [1, E]], base=0, channel_multiplier=0,
                      allow_small_or_imprecise_dtypes=True).then_inc(made, 1)
            pool.iota(iota_j[:], [[1, J + 2]], base=0, channel_multiplier=0,
                      allow_small_or_imprecise_dtypes=True).then_inc(made, 1)
            for b in range(B):
                pool.wait_ge(o_loaded[b % 2], 32 * (b // 2 + 1))
                pool.tensor_tensor(ot[b % 2][:], ot[b % 2][:], ot2[b % 2][:], ALU.add).then_inc(o_whole, 1)
            pool.wait_ge(placed, 1)
            for t in range(NB):
                for k in range(TOP):
                    pool.indirect_dma_start(xgs, bass.IndirectOffsetOnAxis(ap=pos[:, k, t:t + 1], axis=0),
                                            xn[:, t, :], None).then_inc(scattered, 16)
            pool.wait_ge(scattered, 16 * NB * TOP)

        @block.sync
        def _(sync):
            sync.dma_start(w_raw[:], wo.rearrange("(c p) n -> p c n", p=P)).then_inc(loaded, 16)
            sync.dma_start(bo_row[:], row_of(bo, D)).then_inc(loaded, 16)
            sync.dma_start(g_raw[:], row_of(gate, 2)[:, 0:1]).then_inc(loaded, 16)
            sync.dma_start(tok_raw[:], tokens).then_inc(loaded, 16)
            sync.dma_start(brows[0][:], b1.rearrange("e (c p) -> (e c) p", p=P)).then_inc(loaded, 16)
            sync.dma_start(brows[1][:], b2.rearrange("e (c p) -> (e c) p", p=P)).then_inc(loaded, 16)
            sync.dma_start(brows[2][:], b3.rearrange("e (c p) -> (e c) p", p=P)).then_inc(loaded, 16)

            def load_o(b):
                for part, to in enumerate((ot, ot2)):
                    sync.dma_start(to[b % 2][:], o0s[b, part].rearrange("(c p) t -> p c t", p=P)
                                   ).then_inc(o_loaded[b % 2], 16)
            for b in range(B):
                if b < 2:
                    load_o(b)
                sync.dma_start(xin[:, b], x[b].rearrange("(s p) d -> p s d", p=P)).then_inc(x_loaded[b], 16)
            for b in range(2, B):
                sync.wait_ge(o_ready, KC * (b - 1))
                load_o(b)
            sync.wait_ge(x1_ready, B)
            sync.dma_start(x1s.rearrange("b (s p) d -> p b s d", p=P), xin[:]).then_inc(stored, 16)
            sync.wait_ge(b_moved, 2)
            sync.dma_start(bias_s.rearrange("e p c -> p e c"), bcols[:]).then_inc(stored, 16)
            sync.wait_ge(placed, 1)
            sync.dma_start(pos_s, pos[:]).then_inc(stored, 16)
            sync.dma_start(tile_s, tile_i[0:1, :]).then_inc(stored, 16)
            sync.wait_ge(stored, 64)

        @block.tensor
        def _(pe):
            pe.wait_ge(made, MADE)
            pe.wait_ge(loaded, 16 * 7)
            for i in range(3):
                n = brows[i].shape[0]
                pe.transpose(b_ps[:, BC[i]:BC[i] + n], brows[i][:], ident[0:n, 0:n])
            for c in range(KC):
                ins = pe.transpose(b_ps[:, BC[3] + c * E:BC[3] + (c + 1) * E], tok_raw[:, c * P:(c + 1) * P],
                                   ident[0:E, 0:E])
            ins.then_inc(b_turned, 1)
            pe.wait_ge(w_ready, KC)
            pe.wait_ge(b_moved, 2)

            def project(b):
                pe.wait_ge(o_ready, KC * (b + 1))
                if b:
                    pe.wait_ge(x1_ready, b)
                for s in range(QT):
                    ins = product3(pe, bank[s // 2][:, s % 2, :],
                                   [((ot_hi[:, c, s * P:(s + 1) * P], ot_lo[:, c, s * P:(s + 1) * P]),
                                     (w_hi[:, c, :], w_lo[:, c, :])) for c in range(KC)])
                ins.then_inc(full, 1)
            project(0)
            for b in range(B):
                if b + 1 < B:
                    project(b + 1)
                pe.wait_ge(xn_ready, b + 1)
                for c in range(KC):
                    for s in range(QT):
                        ins = pe.transpose(tp[c][:, s * P:(s + 1) * P], xn[:, b * QT + s, c * P:(c + 1) * P], ident[:])
                    ins.then_inc(turned, 1)
                pe.wait_ge(xt_ready, KC * (b + 1))
                if b:
                    pe.wait_ge(sc_moved, b)
                for s in range(QT):
                    for c in range(KC):
                        ins = pe.matmul(sc_ps[:, s, :], xt[:, c, s * P:(s + 1) * P], tok_t[:, c, :],
                                        start=(c == 0), stop=(c == KC - 1))
                ins.then_inc(scored, 1)
            pe.wait_ge(both_ready, 1)
            flat = both[:].rearrange("p t e -> p (t e)")
            pe.matmul(rank_ps[:].rearrange("p t e -> p (t e)"), tri[:], flat, start=True, stop=True)
            pe.matmul(tot_ps[:].rearrange("p t e -> p (t e)"), ones[:], flat, start=True, stop=True).then_inc(counted, 1)

        @block.scalar
        def _(act):
            act.wait_ge(loaded, 16 * 7)
            for c in range(KC):
                act.activation(w_hi[:, c, :], w_raw[:, c, :], ACT.Copy).then_inc(w_hi_ready, 1)
            act.activation(tanh_g[:], g_raw[:], ACT.Tanh).then_inc(w_hi_ready, 1)
            act.wait_ge(made, MADE)

            def split_o(b):
                act.wait_ge(o_whole, b + 1)
                if b:
                    act.wait_ge(full, b)
                for c in range(KC):
                    act.activation(ot_hi[:, c, :], ot[b % 2][:, c, :], ACT.Copy).then_inc(o_hi_ready, 1)
            split_o(0)
            for b in range(B):
                if b + 1 < B:
                    split_o(b + 1)
                norm.scalar(act, b, eps[:])
                if b:
                    act.wait_ge(scored, b)
                for c in range(KC):
                    act.wait_ge(turned, KC * b + c + 1)
                    act.activation(xt[:, c, :], tp[c][:], ACT.Copy).then_inc(xt_ready, 1)

        @block.vector
        def _(dve):
            steps = Steps(dve, own)
            for c in range(KC):
                dve.wait_ge(w_hi_ready, c + 1)
                dve.tensor_tensor(w_lo[:, c, :], w_raw[:, c, :], w_hi[:, c, :].bitcast(F32),
                                  ALU.subtract).then_inc(w_ready, 1)
            dve.wait_ge(b_turned, 1)
            for i, (at, n) in enumerate(((0, HC), (HC, HC), (2 * HC, KC))):
                ins = dve.tensor_copy(bcols[:, :, at:at + n],
                                      b_ps[:, BC[i]:BC[i] + E * n].rearrange("p (e c) -> p e c", e=E))
            ins.then_inc(b_moved, 1)
            dve.tensor_copy(tok_t[:], b_ps[:, BC[3]:BC[3] + KC * E].rearrange("p (c e) -> p c e", c=KC)
                            ).then_inc(b_moved, 1)
            dve.wait_ge(w_hi_ready, KC + 1)

            def move_scores(b):
                dve.wait_ge(scored, b + 1)
                dve.tensor_copy(scores[:, b * QT:(b + 1) * QT, :], sc_ps[:]).then_inc(sc_moved, 1)

            def split_o(b):
                for c in range(KC):
                    dve.wait_ge(o_hi_ready, KC * b + c + 1)
                    dve.tensor_tensor(ot_lo[:, c, :], ot[b % 2][:, c, :], ot_hi[:, c, :].bitcast(F32),
                                      ALU.subtract).then_inc(o_ready, 1)
            split_o(0)
            for b in range(B):
                dve.wait_ge(full, b + 1)
                if b + 1 < B:
                    split_o(b + 1)
                for i in range(2):
                    ins = dve.tensor_tensor(tmp[:, 2 * i:2 * i + 2, :], bank[i][:],
                                            bo_row[:].unsqueeze(1).broadcast_to([P, 2, D]), ALU.add)
                steps.link(ins)
                dve.wait_ge(x_loaded[b], 16)
                ins = dve.scalar_tensor_tensor(xin[:, b], tmp[:], tanh_g[:, 0:1], xin[:, b], ALU.mult, ALU.add)
                ins.then_inc(x1_ready, 1)
                dve.wait_ge(x1_ready, b + 1)
                norm.vector(dve, steps, b, [xin[:, b, s, :] for s in range(QT)],
                            [xn[:, b * QT + s, :] for s in range(QT)])
                dve.sem_inc(xn_ready, 1)
                if b:
                    move_scores(b - 1)
            move_scores(B - 1)
            dve.wait_ge(sc_moved, B)
            for t in range(NB):
                ins = dve.max(best[:, t, :], scores[:, t, :])
            steps.link(ins)
            for t in range(NB):
                ins = dve.max_index(best_i[:, t, :], best[:, t, :], scores[:, t, :])
            steps.link(ins)
            steps.link(dve.tensor_copy(pick[:].rearrange("p k t -> p t k"), best_i[:, :, 0:TOP]))
            for k in range(TOP):
                ins = dve.tensor_tensor(hot[:, k], iota_e[:], pick[:, k, :].unsqueeze(2).broadcast_to([P, NB, E]),
                                        ALU.is_equal)
            steps.link(ins)
            dve.tensor_tensor(both[:], hot[:, 0], hot[:, 1], ALU.add).then_inc(both_ready, 1)
            steps.link(dve.memset(before[:, 0, :], 0.0))
            dve.wait_ge(counted, 1)
            for t in range(NB):
                steps.link(dve.tensor_tensor(before[:, t + 1, :], before[:, t, :], tot_ps[:, t, :], ALU.add))
            steps.link(dve.tensor_scalar(tiles[:], before[:, NB, :], 0.0, None, ALU.is_gt))
            for i in range(1, -(-N // T)):
                steps.link(dve.scalar_tensor_tensor(tiles[:], before[:, NB, :], float(i * T), tiles[:],
                                                    ALU.is_gt, ALU.add))
            steps.link(dve.memset(cum[:, 0:1], 0.0))
            for e in range(E):
                steps.link(dve.tensor_tensor(cum[:, e + 1:e + 2], cum[:, e:e + 1], tiles[:, e:e + 1], ALU.add))
            steps.link(dve.tensor_tensor(slot[:], rank_ps[:], before[:, 0:NB, :], ALU.add))
            steps.link(dve.scalar_tensor_tensor(slot[:], cum[:, 0:E].unsqueeze(1).broadcast_to([P, NB, E]), float(T),
                                                slot[:], ALU.mult, ALU.add))
            for k in range(TOP):
                ins = dve.tensor_tensor(mine[:, k], hot[:, k], slot[:], ALU.mult)
            steps.link(ins)
            steps.link(dve.tensor_reduce(pos_f[:], mine[:], AX.X, ALU.add))
            dve.tensor_copy(pos[:], pos_f[:])
            steps.link(dve.tensor_scalar(tile_f[:], iota_j[:], cum[:, 1:2], None, ALU.is_ge))
            for e in range(1, E):
                steps.link(dve.scalar_tensor_tensor(tile_f[:], iota_j[:], cum[:, e + 1:e + 2], tile_f[:],
                                                    ALU.is_ge, ALU.add))
            steps.link(dve.tensor_scalar(tile_f[:], tile_f[:], float(E - 1), None, ALU.min))
            dve.tensor_copy(tile_i[:], tile_f[:]).then_inc(placed, 1)


def stage_experts(nc, xgs, tile_s, bias_s, w1, w2, w3, ys):
    with Space(nc, "e") as sp:
        RING = 6
        CH = 2 + HC + 2
        W2C, W3C = 2, 2 + HC
        raw = [sp.sb(f"raw{i}", [P, HID]) for i in range(RING)]
        w_hi, w_lo = sp.sb("w_hi", [P, CH, HID], F32R), sp.sb("w_lo", [P, CH, HID], F32R)
        b1_t, b2_t, b3_t = sp.sb("b1_t", [P, HC]), sp.sb("b2_t", [P, HC]), sp.sb("b3_t", [P, KC])
        rows = sp.sb("rows", [P, TS, D])
        x_hi, x_lo = sp.sb("x_hi", [P, KC, T], F32R), sp.sb("x_lo", [P, KC, T], F32R)
        h_hi = [sp.sb(f"h{i}_hi", [P, HC, T], F32R) for i in range(2)]
        h_lo = [sp.sb(f"h{i}_lo", [P, HC, T], F32R) for i in range(2)]
        g = [sp.sb(f"g{i}", [P, T]) for i in range(2)]
        y_t, y_rows = sp.sb("y_t", [P, KC, T]), sp.sb("y_rows", [P, TS, D])
        ident = sp.sb("ident", [P, P])
        tile_e = sp.sb("tile_e", [1, J + 2], I32)
        RB = 3
        bank = [sp.ps(f"bank{i}", [P, NT]) for i in range(RB)]
        tp = [sp.ps(f"tp{i}", [P, NT]) for i in range(KC)]
        yp = [sp.ps(f"yp{i}", [P, 2, D]) for i in range(2)]

        G = 2 * HC
        NBK = G + KC
        assert NBK % RB == 0 and CH % RING == 0
        made, te_loaded = sp.sem("made"), sp.sem("te_loaded")
        raw_loaded = [sp.sem(f"raw_loaded{i}") for i in range(RING)]
        split_hi = sp.sem("split_hi")
        split = Count(sp.sem("split"), RING)
        b1_loaded, b2_loaded, b3_loaded, rows_loaded = (sp.sem(n) for n in ("b1_loaded", "b2_loaded", "b3_loaded",
                                                                            "rows_loaded"))
        x_turned, x_hi_ready, x_ready = sp.sem("x_turned"), sp.sem("x_hi_ready"), sp.sem("x_ready")
        full = Count(sp.sem("full"), NBK)
        read = Count(sp.sem("read"), G)
        y_read = Count(sp.sem("y_read"), KC)
        h_ready = Count(sp.sem("h_ready"), 2)
        y_turned, y_moved = sp.sem("y_turned"), Count(sp.sem("y_moved"), 1)
        y_stored, y_free = sp.sem("y_stored"), Count(sp.sem("y_free"), 1)
        spare = sp.sem("spare")
        ORDER = [W3C, W3C + 1, 0, 1] + list(range(W2C, W3C))
        FIRST = W3C
        block = sp.block()

        @block.gpsimd
        def _(pool):
            make_identity(pool, sp, ident, made)
            y_free.start(pool)
            with pool.Fori(0, J) as t:
                y_moved.wait(pool, t + 1)
                pool.dma_start(ys[bass.ds(t * T, T), :].rearrange("(s p) d -> p s d", p=P), y_rows[:]
                               ).then_inc(y_stored, 16)
                pool.wait_ge(y_stored, t * 16 + 16)
                pool.sem_inc(y_free.sem, 1)

        @block.sync
        def _(sync):
            sync.dma_start(tile_e[:], tile_s).then_inc(te_loaded, 16)
            sync.wait_ge(te_loaded, 16)

            def load_chunk(q, e, n, slot):
                split.wait(sync, n - RING + 1)
                apart(sync, spare)
                if q < W2C:
                    src, dst = w1[e, q * P:(q + 1) * P, :], raw[slot][:]
                elif q < W3C:
                    src, dst = w2[e, (q - W2C) * P:(q - W2C + 1) * P, :], raw[slot][:]
                else:
                    r = (q - W3C) * 4 * P
                    src = w3[e, r:r + 4 * P, :].rearrange("(c p) n -> p c n", p=P)
                    dst = raw[slot][:].rearrange("p (c n) -> p c n", c=4)
                sync.dma_start(dst, src).then_inc(raw_loaded[slot], 16)

            def load_next(t, e):
                def load(i):
                    load_chunk(ORDER[i], e, FIRST + t * CH + i, (FIRST + i) % RING)
                sync.wait_ge(x_turned, t * KC + KC)
                apart(sync, spare)
                sync.dma_start(rows[:], xgs[bass.ds((t + 1) * T, T), :].rearrange("(s p) d -> p s d", p=P)
                               ).then_inc(rows_loaded, 16)
                read.wait(sync, t * G + HC)
                apart(sync, spare)
                sync.dma_start(b1_t[:], bias_s[e, :, 0:HC]).then_inc(b1_loaded, 16)
                for i in range(2, CH - 2):
                    load(i)
                read.wait(sync, t * G + G)
                apart(sync, spare)
                sync.dma_start(b2_t[:], bias_s[e, :, HC:2 * HC]).then_inc(b2_loaded, 16)
                for i in range(CH - 2, CH):
                    load(i)
                y_read.wait(sync, t * KC + KC)
                apart(sync, spare)
                sync.dma_start(b3_t[:], bias_s[e, :, 2 * HC:BW]).then_inc(b3_loaded, 16)

            def load_w3(t, e):
                for i in range(2):
                    load_chunk(ORDER[i], e, FIRST + t * CH + i, (FIRST + i) % RING)

            e0 = sync.value_load(tile_e[0:1, 0:1], min_val=0, max_val=E - 1)
            sync.dma_start(rows[:], xgs[0:T, :].rearrange("(s p) d -> p s d", p=P)).then_inc(rows_loaded, 16)
            sync.dma_start(b1_t[:], bias_s[e0, :, 0:HC]).then_inc(b1_loaded, 16)
            sync.dma_start(b2_t[:], bias_s[e0, :, HC:2 * HC]).then_inc(b2_loaded, 16)
            sync.dma_start(b3_t[:], bias_s[e0, :, 2 * HC:BW]).then_inc(b3_loaded, 16)
            for q in range(W3C):
                load_chunk(q, e0, q, q % RING)
            with sync.Fori(0, J - 1) as t:
                load_w3(t, sync.value_load(tile_e[0:1, bass.ds(t, 1)], min_val=0, max_val=E - 1))
                load_next(t, sync.value_load(tile_e[0:1, bass.ds(t + 1, 1)], min_val=0, max_val=E - 1))
            load_w3(J - 1, sync.value_load(tile_e[0:1, J - 1:J], min_val=0, max_val=E - 1))

        @block.tensor
        def _(pe):
            full.start(pe)
            pe.wait_ge(made, 2)

            def turn_rows(t):
                pe.wait_ge(rows_loaded, t * 16 + 16)
                for c in range(KC):
                    for s in range(TS):
                        ins = pe.transpose(tp[c][:, s * P:(s + 1) * P], rows[:, s, c * P:(c + 1) * P], ident[:])
                    ins.then_inc(x_turned, 1)

            def block_of(t, m, pairs, wait):
                if m in (1, 2):
                    y_read.wait(pe, (t - 1) * KC + m)
                else:
                    read.wait(pe, t * G + max(m - RB + 1, 0))
                for i, (stat, mov) in enumerate(pairs):
                    if m % HC == 0:
                        wait(i)
                    ins = product3(pe, bank[m % RB][:, 0:T], [(stat, mov)], start=(i == 0), stop=(i == len(pairs) - 1))
                ins.then_inc(full.sem, 1)

            def weights(q, col):
                return w_hi[:, q, col:col + P], w_lo[:, q, col:col + P]

            def first_layer(t, between=None):
                def wait(c):
                    pe.wait_ge(x_ready, t * KC + c + 1)
                    split.wait(pe, t * CH + c + 1)
                for m in range(HC):
                    block_of(t, m, [(weights(c, m * P), (x_hi[:, c, :], x_lo[:, c, :])) for c in range(KC)], wait)
                    if m == 2 and between:
                        between()

            def second_layer(t, between=None):
                def wait(c):
                    h_ready.wait(pe, t * G + c + 1)
                    split.wait(pe, t * CH + W2C + c + 1)
                for m in range(HC):
                    block_of(t, HC + m, [(weights(W2C + c, m * P), (h_hi[0][:, c, :], h_lo[0][:, c, :]))
                                         for c in range(HC)], wait)
                    if m == 3 and between:
                        between()

            def third_layer(t):
                def wait(c):
                    h_ready.wait(pe, t * G + HC + c + 1)
                    split.wait(pe, t * CH + W3C + c // 4 + 1)
                for m in range(KC):
                    block_of(t, G + m, [(weights(W3C + c // 4, (c % 4) * D + m * P),
                                         (h_hi[1][:, c, :], h_lo[1][:, c, :])) for c in range(HC)], wait)

            def turn_output(t):
                y_moved.wait(pe, t)
                y_read.wait(pe, t * KC + KC)
                for m in range(KC):
                    for s in range(TS):
                        ins = pe.transpose(yp[s // 2][:, s % 2, m * P:(m + 1) * P], y_t[:, m, s * P:(s + 1) * P],
                                           ident[:])
                ins.then_inc(y_turned, 1)

            turn_rows(0)
            first_layer(0)
            with pe.Fori(0, J - 1) as t:
                second_layer(t, lambda: turn_rows(t + 1))
                third_layer(t)
                first_layer(t + 1, lambda: turn_output(t))
            second_layer(J - 1)
            third_layer(J - 1)
            turn_output(J - 1)

        @block.scalar
        def _(act):
            read.start(act)

            def chunk(t, i):
                q = ORDER[i]
                full.wait(act, t * NBK + (0 if q >= W3C else HC if q < W2C else G))
                act.wait_ge(raw_loaded[(FIRST + i) % RING], (t * (CH // RING) + (FIRST + i) // RING + 1) * 16)
                act.activation(w_hi[:, q, :], raw[(FIRST + i) % RING][:], ACT.Copy).then_inc(split_hi, 1)

            def gelu(t, m):
                layer, c = m // HC, m % HC
                bias = (b1_t, b2_t)[layer]
                if c == 0:
                    act.wait_ge((b1_loaded, b2_loaded)[layer], t * 16 + 16)
                    full.wait(act, (t - 1) * NBK + (NBK if layer else G))
                full.wait(act, t * NBK + m + 1)
                h_ready.wait(act, t * G + m - 1)
                act.activation(g[m % 2][:], bank[m % RB][:, 0:T], ACT.Gelu, bias=bias[:, c:c + 1])
                act.activation(h_hi[layer][:, c, :], bank[m % RB][:, 0:T], ACT.Gelu, bias=bias[:, c:c + 1]
                               ).then_inc(read.sem, 1)

            def rows_high(t):
                for c in range(KC):
                    act.wait_ge(x_turned, t * KC + c + 1)
                    act.activation(x_hi[:, c, :], tp[c][:, 0:T], ACT.Copy).then_inc(x_hi_ready, 1)

            rows_high(0)
            for q in range(W3C):
                act.wait_ge(raw_loaded[q % RING], (q // RING + 1) * 16)
                act.activation(w_hi[:, q, :], raw[q % RING][:], ACT.Copy).then_inc(split_hi, 1)
                if q >= W2C:
                    gelu(0, q - W2C)
            with act.Fori(0, J - 1) as t:
                for m in range(HC):
                    gelu(t, HC + m)
                    if m < 4:
                        chunk(t, m)
                    if m == 4:
                        rows_high(t + 1)
                for i in range(4, CH - 1):
                    chunk(t, i)
                for m in range(HC):
                    gelu(t + 1, m)
                    if m == 3:
                        chunk(t, CH - 1)
            for m in range(HC):
                gelu(J - 1, HC + m)
                if m < 2:
                    chunk(J - 1, m)

        @block.vector
        def _(dve):
            split.start(dve)
            y_read.start(dve)
            h_ready.start(dve)
            y_moved.start(dve)

            def low(n, q, slot):
                dve.wait_ge(split_hi, n + 1)
                dve.tensor_tensor(w_lo[:, q, :], raw[slot][:], w_hi[:, q, :].bitcast(F32), ALU.subtract
                                  ).then_inc(split.sem, 1)

            def chunk(t, i):
                low(FIRST + t * CH + i, ORDER[i], (FIRST + i) % RING)

            def rest(t, m):
                layer, c = m // HC, m % HC
                read.wait(dve, t * G + m + 1)
                dve.tensor_tensor(h_lo[layer][:, c, :], g[m % 2][:], h_hi[layer][:, c, :].bitcast(F32), ALU.subtract
                                  ).then_inc(h_ready.sem, 1)

            def rows_low(t):
                for c in range(KC):
                    dve.wait_ge(x_hi_ready, t * KC + c + 1)
                    dve.tensor_tensor(x_lo[:, c, :], tp[c][:, 0:T], x_hi[:, c, :].bitcast(F32), ALU.subtract
                                      ).then_inc(x_ready, 1)

            def output(t, m):
                if m == 0:
                    dve.wait_ge(b3_loaded, t * 16 + 16)
                    dve.wait_ge(y_turned, t)
                full.wait(dve, t * NBK + G + m + 1)
                dve.tensor_scalar(y_t[:, m, :], bank[(G + m) % RB][:, 0:T], b3_t[:, m:m + 1], None, ALU.add
                                  ).then_inc(y_read.sem, 1)

            def output_rows(t):
                dve.wait_ge(y_turned, t + 1)
                y_free.wait(dve, t)
                for s in range(TS):
                    ins = dve.tensor_copy(y_rows[:, s, :], yp[s // 2][:, s % 2, :])
                ins.then_inc(y_moved.sem, 1)

            rows_low(0)
            for q in range(W3C):
                low(q, q, q % RING)
                if q >= W2C:
                    rest(0, q - W2C)
            with dve.Fori(0, J - 1) as t:
                for m in range(HC):
                    rest(t, HC + m)
                    if m < 4:
                        chunk(t, m)
                    if m == 4:
                        rows_low(t + 1)
                for i in range(4, CH - 1):
                    chunk(t, i)
                    if i == 7:
                        output(t, 0)
                output(t, 1)
                for m in range(HC):
                    rest(t + 1, m)
                    if m == 1:
                        output_rows(t)
                    if m == 3:
                        chunk(t, CH - 1)
            for m in range(HC):
                rest(J - 1, HC + m)
                if m < 2:
                    chunk(J - 1, m)
            for m in range(KC):
                output(J - 1, m)
            output_rows(J - 1)


def stage_gather(nc, x1s, ys, pos_s, gate, gamma, wq, null_kv, x2s, q1s, null_s):
    with Space(nc, "g") as sp:
        neg_scale = -float(D1) ** -0.5
        QC = I1 // P
        w_raw = sp.sb("w_raw", [P, KC, I1])
        w_hi, w_lo = sp.sb("w_hi", [P, KC, I1], F32R), sp.sb("w_lo", [P, KC, I1], F32R)
        half_g, g_raw, gamma_row = sp.sb("half_g", [P, 1]), sp.sb("g_raw", [P, 1]), sp.sb("gamma_row", [P, D])
        tanh_g = sp.sb("tanh_g", [P, 1])
        eps, ident = sp.sb("eps", [P, 1]), sp.sb("ident", [P, P])
        nk_col = sp.sb("nk_col", [P, 1])
        nk, nk_hi, nk_lo = sp.sb("nk", [P, QC, H1]), sp.sb("nk_hi", [P, QC, H1], F32R), sp.sb("nk_lo", [P, QC, H1], F32R)
        pos = sp.sb("pos", [P, TOP, NB], I32)
        xin = sp.sb("xin", [P, B, QT, D])
        yg = [sp.sb(f"yg{i}", [P, TOP, QT, D]) for i in range(B)]
        tmp, xn = sp.sb("tmp", [P, QT, D]), sp.sb("xn", [P, QT, D])
        t_hi, t_lo = sp.sb("t_hi", [P, KC, NT], F32R), sp.sb("t_lo", [P, KC, NT], F32R)
        q_hi, q_lo = sp.sb("q_hi", [P, QC, NT], F32R), sp.sb("q_lo", [P, QC, NT], F32R)
        sn = sp.sb("sn", [P, H1, QT])
        tp = [sp.ps(f"tp{i}", [P, NT]) for i in range(KC)]
        bank = [sp.ps(f"bank{i}", [P, NT]) for i in range(QC)]
        sn_ps = sp.ps("sn_ps", [P, QT, H1])
        norm_a, norm_b = Norm(sp, "norm_a"), Norm(sp, "norm_b")
        loaded, x_loaded, pos_loaded, made = sp.sem("loaded"), sp.sem("x_loaded"), sp.sem("pos_loaded"), sp.sem("made")
        gathered = [sp.sem(f"gathered{i}") for i in range(B)]
        w_hi_ready, w_ready, nk_ready = sp.sem("w_hi_ready"), sp.sem("w_ready"), sp.sem("nk_ready")
        xn_ready, turned, t_hi_ready, t_ready = (sp.sem(n) for n in ("xn_ready", "turned", "t_hi_ready", "t_ready"))
        full, q_hi_ready, q_ready, n_scored = (sp.sem(n) for n in ("full", "q_hi_ready", "q_ready", "n_scored"))
        x2_ready, sn_ready, stored, own = sp.sem("x2_ready"), sp.sem("sn_ready"), sp.sem("stored"), sp.sem("own")
        sn_stored = sp.sem("sn_stored")
        block = sp.block()

        @block.gpsimd
        def _(pool):
            pool.memset(eps[:], EPS).then_inc(made, 1)
            pool.memset(ident[:], 0.0).then_inc(made, 1)
            pool.wait_ge(made, 2)
            pool.affine_select(out=ident[:], in_=ident[:], compare_op=ALU.not_equal, fill=1.0, base=0,
                               pattern=[[-1, P]], channel_multiplier=1).then_inc(made, 1)
            pool.wait_ge(pos_loaded, 16)
            for b in range(B):
                for s in range(QT):
                    for k in range(TOP):
                        t = b * QT + s
                        pool.indirect_dma_start(yg[b][:, k, s, :], None, ys,
                                                bass.IndirectOffsetOnAxis(ap=pos[:, k, t:t + 1], axis=0)
                                                ).then_inc(gathered[b], 16)

        @block.sync
        def _(sync):
            sync.dma_start(pos[:], pos_s).then_inc(pos_loaded, 16)
            sync.dma_start(w_raw[:], wq.rearrange("(c p) n -> p c n", p=P)).then_inc(loaded, 16)
            sync.dma_start(g_raw[:], row_of(gate, 2)[:, 0:1]).then_inc(loaded, 16)
            sync.dma_start(gamma_row[:], row_of(gamma, D)).then_inc(loaded, 16)
            for e in range(2):
                sync.dma_start(nk_col[e * D1:(e + 1) * D1, :], null_kv[0, :].rearrange("(d a) -> d a", a=1),
                               allow_slow_non_contiguous=True).then_inc(loaded, 16)
            sync.dma_start(xin[:], x1s.rearrange("b (s p) d -> p b s d", p=P)).then_inc(x_loaded, 16)
            for b in range(B):
                sync.wait_ge(q_ready, QC * (b + 1))
                for part, src in ((0, q_hi), (1, q_lo)):
                    sync.dma_start(q1s[part, b].rearrange("(c p) t -> p c t", p=P),
                                   src[:].bitcast(F32)).then_inc(stored, 16)
                sync.wait_ge(sn_ready, b + 1)
                sync.dma_start(null_s[b], sn[:]).then_inc(sn_stored, 16)
                if b == B - 1:
                    sync.wait_ge(x2_ready, B)
                    sync.dma_start(x2s.rearrange("b (s p) d -> p b s d", p=P), xin[:]).then_inc(stored, 16)
            sync.wait_ge(stored, 32 * B + 16)
            sync.wait_ge(sn_stored, 16 * B)

        @block.tensor
        def _(pe):
            pe.wait_ge(made, 3)
            pe.wait_ge(w_ready, KC)
            pe.wait_ge(nk_ready, 4)

            def turn(b):
                pe.wait_ge(xn_ready, b + 1)
                for c in range(KC):
                    for s in range(QT):
                        ins = pe.transpose(tp[c][:, s * P:(s + 1) * P], xn[:, s, c * P:(c + 1) * P], ident[:])
                    ins.then_inc(turned, 1)
            turn(0)
            for b in range(B):
                pe.wait_ge(t_ready, KC * (b + 1))
                for j in range(QC):
                    if b:
                        pe.wait_ge(q_ready, QC * (b - 1) + j + 1)
                    product3(pe, bank[j][:], [((w_hi[:, c, j * P:(j + 1) * P], w_lo[:, c, j * P:(j + 1) * P]),
                                               (t_hi[:, c, :], t_lo[:, c, :])) for c in range(KC)]).then_inc(full, 1)
                if b + 1 < B:
                    turn(b + 1)
                pe.wait_ge(q_ready, QC * (b + 1))
                if b:
                    pe.wait_ge(sn_ready, b)
                for s in range(QT):
                    ins = product3(pe, sn_ps[:, s, :], [((q_hi[:, c, s * P:(s + 1) * P], q_lo[:, c, s * P:(s + 1) * P]),
                                                         (nk_hi[:, c, :], nk_lo[:, c, :])) for c in range(QC)])
                ins.then_inc(n_scored, 1)

        @block.scalar
        def _(act):
            act.wait_ge(loaded, 80)
            for c in range(KC):
                act.activation(w_hi[:, c, :], w_raw[:, c, :], ACT.Copy, scale=neg_scale).then_inc(w_hi_ready, 1)
            act.activation(tanh_g[:], g_raw[:], ACT.Tanh).then_inc(w_hi_ready, 1)
            act.wait_ge(w_hi_ready, KC + 1)
            act.activation(half_g[:], tanh_g[:], ACT.Copy, scale=1.0 / TOP).then_inc(w_hi_ready, 1)
            act.wait_ge(made, 3)
            norm_a.scalar(act, 0, eps[:])
            norm_b.scalar(act, 0, eps[:])
            for b in range(B):
                for c in range(KC):
                    act.wait_ge(turned, KC * b + c + 1)
                    act.activation(t_hi[:, c, :], tp[c][:], ACT.Copy).then_inc(t_hi_ready, 1)
                if b + 1 < B:
                    norm_a.scalar(act, b + 1, eps[:])
                    norm_b.scalar(act, b + 1, eps[:])
                if b:
                    act.wait_ge(stored, 32 * b)
                    act.wait_ge(n_scored, b)
                for j in range(QC):
                    act.wait_ge(full, QC * b + j + 1)
                    act.activation(q_hi[:, j, :], bank[j][:], ACT.Copy).then_inc(q_hi_ready, 1)

        @block.vector
        def _(dve):
            steps = Steps(dve, own)
            dve.memset(nk[:], 0.0).then_inc(nk_ready, 1)
            dve.wait_ge(nk_ready, 1)
            dve.wait_ge(loaded, 80)
            for h in range(H1):
                rows = slice((h % 2) * D1, (h % 2 + 1) * D1)
                ins = dve.tensor_copy(nk[rows, h // 2, h:h + 1], nk_col[rows, :])
                steps.did(ins)
            steps.wait()
            dve.tensor_copy(nk_hi[:], nk[:]).then_inc(nk_ready, 1)
            dve.wait_ge(nk_ready, 2)
            dve.tensor_tensor(nk_lo[:], nk[:], nk_hi[:].bitcast(F32), ALU.subtract).then_inc(nk_ready, 2)
            for c in range(KC):
                dve.wait_ge(w_hi_ready, c + 1)
                dve.scalar_tensor_tensor(w_lo[:, c, :], w_raw[:, c, :], neg_scale, w_hi[:, c, :].bitcast(F32),
                                         ALU.mult, ALU.subtract).then_inc(w_ready, 1)
            dve.wait_ge(w_hi_ready, KC + 2)
            dve.wait_ge(x_loaded, 16)

            def normalise(b):
                dve.wait_ge(gathered[b], 16 * TOP * QT)
                steps.link(dve.tensor_tensor(tmp[:], yg[b][:, 0], yg[b][:, 1], ALU.add))
                dve.scalar_tensor_tensor(xin[:, b], tmp[:], half_g[:, 0:1], xin[:, b], ALU.mult, ALU.add
                                         ).then_inc(x2_ready, 1)
                dve.wait_ge(x2_ready, b + 1)
                if b:
                    dve.wait_ge(turned, KC * b)
                norm_a.vector(dve, steps, b, [xin[:, b, s, :] for s in range(QT)], [xn[:, s, :] for s in range(QT)])
                steps.wait()
                norm_b.vector(dve, steps, b, [xn[:, s, :] for s in range(QT)], [xn[:, s, :] for s in range(QT)],
                              gamma_row[:])
                dve.sem_inc(xn_ready, 1)

            def rest_of_rows(b):
                for c in range(KC):
                    dve.wait_ge(t_hi_ready, KC * b + c + 1)
                    dve.tensor_tensor(t_lo[:, c, :], tp[c][:], t_hi[:, c, :].bitcast(F32),
                                      ALU.subtract).then_inc(t_ready, 1)

            def null_scores(b):
                dve.wait_ge(n_scored, b + 1)
                if b:
                    dve.wait_ge(sn_stored, 16 * b)
                dve.tensor_copy(sn[:].rearrange("p h t -> p t h"), sn_ps[:]).then_inc(sn_ready, 1)
            normalise(0)
            rest_of_rows(0)
            for b in range(B):
                if b + 1 < B:
                    normalise(b + 1)
                if b:
                    null_scores(b - 1)
                for j in range(QC):
                    dve.wait_ge(q_hi_ready, QC * b + j + 1)
                    dve.tensor_tensor(q_lo[:, j, :], bank[j][:], q_hi[:, j, :].bitcast(F32), ALU.subtract
                                      ).then_inc(q_ready, 1)
                if b + 1 < B:
                    rest_of_rows(b + 1)
            null_scores(B - 1)


def stage_final(nc, x2s, o1s, wo, out_gamma, gates, gate2, wg, bg, we, be, out):
    with Space(nc, "f") as sp:
        OC = I1 // P
        EW = E * D
        WN = OC * D + KC * D + KC * EW
        w_raw = [sp.sb(f"w_raw{i}", [P, EW]) for i in range(2)]
        w_hi, w_lo = sp.sb("w_hi", [P, WN], F32R), sp.sb("w_lo", [P, WN], F32R)
        g_raw, tanh_g = sp.sb("g_raw", [P, 2]), sp.sb("tanh_g", [P, 2])
        gamma_row, bg_row, be_sb = sp.sb("gamma_row", [P, D]), sp.sb("bg_row", [P, D]), sp.sb("be_sb", [E, D])
        eps, ident, iota_e = sp.sb("eps", [P, 1]), sp.sb("ident", [P, P]), sp.sb("iota_e", [P, E])
        xin = sp.sb("xin", [P, B, QT, D])
        ot = [sp.sb(f"ot{i}", [P, OC, NT]) for i in range(2)]
        ot2 = [sp.sb(f"ot2_{i}", [P, OC, NT]) for i in range(2)]
        ot_hi, ot_lo = sp.sb("ot_hi", [P, OC, NT], F32R), sp.sb("ot_lo", [P, OC, NT], F32R)
        att, xn = sp.sb("att", [P, QT, D]), sp.sb("xn", [P, QT, D])
        t_hi = [sp.sb(f"t_hi{i}", [P, KC, NT], F32R) for i in range(2)]
        t_lo = [sp.sb(f"t_lo{i}", [P, KC, NT], F32R) for i in range(2)]
        logits, probs = sp.sb("logits", [P, QT, D]), sp.sb("probs", [P, QT, D])
        top, top_i = sp.sb("top", [P, QT, 8]), sp.sb("top_i", [P, QT, 8], U32)
        neg_max, total, weight = sp.sb("neg_max", [P, QT]), sp.sb("total", [P, QT]), sp.sb("weight", [P, QT])
        e_i, e_f, hot = sp.sb("e_i", [P, QT], U32), sp.sb("e_f", [P, QT]), sp.sb("hot", [P, QT, E])
        hot_t = sp.sb("hot_t", [E, QT, P])
        be_rows = sp.sb("be_rows", [P, QT, D])
        acc, res = sp.sb("acc", [P, QT, D]), sp.sb("res", [P, QT, D])
        ex = [sp.ps(f"ex{i}", [P, 2, D]) for i in range(4)]
        tp = [sp.ps(f"tp{i}", [P, NT]) for i in range(KC)]
        lg = [sp.ps(f"lg{i}", [P, 2, D]) for i in range(2)]
        norms = [Norm(sp, f"norm{i}") for i in range(2)]
        loaded, x_loaded, made = sp.sem("loaded"), [sp.sem(f"x_loaded{b}") for b in range(B)], sp.sem("made")
        w_loaded = [sp.sem(f"w_loaded{i}") for i in range(2)]
        o_loaded = [sp.sem(f"o_loaded{i}") for i in range(2)]
        w_hi_ready, w_ready, tanh_ready = sp.sem("w_hi_ready"), sp.sem("w_ready"), sp.sem("tanh_ready")
        o_whole = sp.sem("o_whole")
        o_hi_ready, o_ready, projected = (sp.sem(n) for n in ("o_hi_ready", "o_ready", "projected"))
        xn_ready, turned, t_hi_ready, t_ready = (sp.sem(n) for n in ("xn_ready", "turned", "t_hi_ready", "t_ready"))
        gated, max_ready, exped, hot_ready = (sp.sem(n) for n in ("gated", "max_ready", "exped", "hot_ready"))
        hot_turned, hot_moved, be_ready, be_moved = (sp.sem(n) for n in ("hot_turned", "hot_moved", "be_ready", "be_moved"))
        ex_full, ex_read, res_ready, stored, own = (sp.sem(n) for n in ("ex_full", "ex_read", "res_ready", "stored", "own"))
        WO, WG, WE = 0, OC * D, OC * D + KC * D
        pieces = [(WO, OC * D, wo.rearrange("(c p) n -> p c n", p=P), OC),
                  (WG, KC * D, wg.rearrange("(c p) n -> p c n", p=P), KC)]
        for c in range(KC):
            pieces.append((WE + c * EW, EW, we[:, c * P:(c + 1) * P, :].rearrange("e p n -> p e n"), E))
        block = sp.block()

        @block.gpsimd
        def _(pool):
            pool.memset(eps[:], EPS).then_inc(made, 1)
            pool.memset(ident[:], 0.0).then_inc(made, 1)
            pool.wait_ge(made, 2)
            pool.affine_select(out=ident[:], in_=ident[:], compare_op=ALU.not_equal, fill=1.0, base=0,
                               pattern=[[-1, P]], channel_multiplier=1).then_inc(made, 1)
            pool.iota(iota_e[:], [[1, E]], base=0, channel_multiplier=0,
                      allow_small_or_imprecise_dtypes=True).then_inc(made, 1)
            for b in range(B):
                pool.wait_ge(o_loaded[b % 2], 32 * (b // 2 + 1))
                pool.tensor_tensor(ot[b % 2][:], ot[b % 2][:], ot2[b % 2][:], ALU.add).then_inc(o_whole, 1)
                if b:
                    pool.wait_ge(o_hi_ready, b + 1)
                    pool.tensor_tensor(ot_lo[:], ot[b % 2][:], ot_hi[:].bitcast(F32), ALU.subtract
                                       ).then_inc(o_ready, 1)

        @block.sync
        def _(sync):
            def load_o(b):
                for part, to in enumerate((ot, ot2)):
                    sync.dma_start(to[b % 2][:], o1s[b, part].rearrange("(c p) t -> p c t", p=P)
                                   ).then_inc(o_loaded[b % 2], 16)
            for i, (at, n, src, c) in enumerate(pieces):
                if i >= 2:
                    sync.wait_ge(w_ready, i - 1)
                sync.dma_start(w_raw[i % 2][:, 0:n].rearrange("p (c n) -> p c n", c=c), src).then_inc(w_loaded[i % 2], 16)
                if i == 0:
                    load_o(0)
                    sync.dma_start(g_raw[:, 0:1], row_of(gates, 2)[:, 1:2]).then_inc(loaded, 16)
                    sync.dma_start(g_raw[:, 1:2], row_of(gate2, 2)[:, 1:2]).then_inc(loaded, 16)
                    sync.dma_start(gamma_row[:], row_of(out_gamma, D)).then_inc(loaded, 16)
                    sync.dma_start(bg_row[:], row_of(bg, D)).then_inc(loaded, 16)
                    sync.dma_start(be_sb[:], be).then_inc(loaded, 16)
                    sync.dma_start(xin[:, 0], x2s[0].rearrange("(s p) d -> p s d", p=P)).then_inc(x_loaded[0], 16)
            for b in range(1, B):
                if b >= 2:
                    sync.wait_ge(o_ready, b - 1)
                load_o(b)
                sync.dma_start(xin[:, b], x2s[b].rearrange("(s p) d -> p s d", p=P)).then_inc(x_loaded[b], 16)
            for b in range(B):
                sync.wait_ge(res_ready, b + 1)
                sync.dma_start(out[b].rearrange("(s p) d -> p s d", p=P), res[:]).then_inc(stored, 16)
            sync.wait_ge(stored, 16 * B)

        @block.tensor
        def _(pe):
            pe.wait_ge(made, 4)

            def project(b):
                if b == 0:
                    pe.wait_ge(w_ready, 1)
                pe.wait_ge(o_ready, b + 1)
                if b:
                    pe.wait_ge(t_ready, KC * b)
                for s in range(QT):
                    ins = product3(pe, tp[s // 2][:, (s % 2) * D:(s % 2 + 1) * D],
                                   [((ot_hi[:, c, s * P:(s + 1) * P], ot_lo[:, c, s * P:(s + 1) * P]),
                                     (w_hi[:, WO + c * D:WO + (c + 1) * D], w_lo[:, WO + c * D:WO + (c + 1) * D]))
                                    for c in range(OC)])
                ins.then_inc(projected, 1)

            def turn(b):
                pe.wait_ge(xn_ready, b + 1)
                for c in range(KC):
                    for s in range(QT):
                        ins = pe.transpose(tp[c][:, s * P:(s + 1) * P], xn[:, s, c * P:(c + 1) * P], ident[:])
                    ins.then_inc(turned, 1)

            def stat(b, s):
                return [(t_hi[b % 2][:, c, s * P:(s + 1) * P], t_lo[b % 2][:, c, s * P:(s + 1) * P]) for c in range(KC)]

            def gates(b):
                pe.wait_ge(t_ready, KC * (b + 1))
                if b:
                    pe.wait_ge(be_moved, 2 * b)
                else:
                    pe.wait_ge(w_ready, len(pieces))
                for s in range(QT):
                    ins = product3(pe, lg[s // 2][:, s % 2, :],
                                   [(stat(b, s)[c], (w_hi[:, WG + c * D:WG + (c + 1) * D],
                                                     w_lo[:, WG + c * D:WG + (c + 1) * D])) for c in range(KC)])
                ins.then_inc(gated, 1)

            def experts(b, s):
                for i in range(4):
                    if b or s:
                        pe.wait_ge(ex_read, 4 * E * b + E * (s - 1) + 2 * (i + 1))
                    cols = [slice(WE + c * EW + i * NT, WE + c * EW + (i + 1) * NT) for c in range(KC)]
                    product3(pe, ex[i][:].rearrange("p a n -> p (a n)"),
                             [(stat(b, s)[c], (w_hi[:, cols[c]], w_lo[:, cols[c]])) for c in range(KC)]
                             ).then_inc(ex_full, 1)

            project(0)
            turn(0)
            gates(0)
            for b in range(B):
                more = b + 1 < B
                experts(b, 0)
                if more:
                    project(b + 1)
                pe.wait_ge(hot_ready, b + 1)
                for s in range(QT):
                    ins = pe.transpose(lg[s // 2][0:E, s % 2, 0:P], hot[:, s, :], ident[:])
                ins.then_inc(hot_turned, 1)
                pe.wait_ge(hot_moved, b + 1)
                for s in range(QT):
                    ins = pe.matmul(lg[s // 2][:, s % 2, :], hot_t[:, s, :], be_sb[:], start=True, stop=True)
                ins.then_inc(be_ready, 1)
                experts(b, 1)
                experts(b, 2)
                if more:
                    turn(b + 1)
                experts(b, 3)
                if more:
                    gates(b + 1)

        @block.scalar
        def _(act):
            act.wait_ge(made, 4)
            for i, (at, n, src, c) in enumerate(pieces):
                act.wait_ge(w_loaded[i % 2], 16 * (i // 2 + 1))
                act.activation(w_hi[:, at:at + n], w_raw[i % 2][:, 0:n], ACT.Copy).then_inc(w_hi_ready, 1)
                if i == 0:
                    act.wait_ge(o_whole, 1)
                    act.activation(ot_hi[:], ot[0][:], ACT.Copy).then_inc(o_hi_ready, 1)
            act.wait_ge(loaded, 80)
            act.activation(tanh_g[:], g_raw[:], ACT.Tanh).then_inc(tanh_ready, 1)

            def rows_high(b):
                for norm in norms:
                    norm.scalar(act, b, eps[:])
                if b >= 2:
                    act.wait_ge(ex_full, 4 * QT * (b - 1))
                for c in range(KC):
                    act.wait_ge(turned, KC * b + c + 1)
                    act.activation(t_hi[b % 2][:, c, :], tp[c][:], ACT.Copy).then_inc(t_hi_ready, 1)
            rows_high(0)
            for b in range(B):
                if b + 1 < B:
                    act.wait_ge(o_whole, b + 2)
                    act.wait_ge(projected, b + 1)
                    act.activation(ot_hi[:], ot[(b + 1) % 2][:], ACT.Copy).then_inc(o_hi_ready, 1)
                act.wait_ge(max_ready, b + 1)
                for s in range(QT):
                    act.activation(probs[:, s, :], logits[:, s, :], ACT.Exp, bias=neg_max[:, s:s + 1],
                                   accum_out=total[:, s:s + 1]).then_inc(exped, 1)
                act.wait_ge(hot_turned, b + 1)
                for i in range(2):
                    ins = act.activation(hot_t[:, 2 * i:2 * i + 2, :], lg[i][0:E, :, 0:P], ACT.Copy)
                ins.then_inc(hot_moved, 1)
                act.wait_ge(be_ready, b + 1)
                for i in range(2):
                    act.activation(be_rows[:, 2 * i:2 * i + 2, :], lg[i][:], ACT.Copy).then_inc(be_moved, 1)
                if b + 1 < B:
                    rows_high(b + 1)

        @block.vector
        def _(dve):
            steps = Steps(dve, own)
            for i, (at, n, src, c) in enumerate(pieces):
                dve.wait_ge(w_hi_ready, i + 1)
                dve.tensor_tensor(w_lo[:, at:at + n], w_raw[i % 2][:, 0:n], w_hi[:, at:at + n].bitcast(F32),
                                  ALU.subtract).then_inc(w_ready, 1)
                if i == 0:
                    dve.wait_ge(o_hi_ready, 1)
                    dve.tensor_tensor(ot_lo[:], ot[0][:], ot_hi[:].bitcast(F32), ALU.subtract).then_inc(o_ready, 1)
            dve.wait_ge(tanh_ready, 1)
            tiles = range(QT)

            def residual(b):
                dve.wait_ge(projected, b + 1)
                norms[0].vector(dve, steps, b, [tp[s // 2][:, (s % 2) * D:(s % 2 + 1) * D] for s in tiles],
                                [att[:, s, :] for s in tiles], gamma_row[:])
                dve.wait_ge(x_loaded[b], 16)
                steps.link(dve.scalar_tensor_tensor(xin[:, b], att[:], tanh_g[:, 0:1], xin[:, b], ALU.mult, ALU.add))

            def normalise(b):
                norms[1].vector(dve, steps, b, [xin[:, b, s, :] for s in tiles], [xn[:, s, :] for s in tiles])
                dve.sem_inc(xn_ready, 1)

            def rows_low(b):
                for c in range(KC):
                    dve.wait_ge(t_hi_ready, KC * b + c + 1)
                    dve.tensor_tensor(t_lo[b % 2][:, c, :], tp[c][:], t_hi[b % 2][:, c, :].bitcast(F32),
                                      ALU.subtract).then_inc(t_ready, 1)
            residual(0)
            normalise(0)
            rows_low(0)
            for b in range(B):
                dve.wait_ge(gated, b + 1)
                for i in range(2):
                    ins = dve.tensor_tensor(logits[:, 2 * i:2 * i + 2, :], lg[i][:],
                                            bg_row[:].unsqueeze(1).broadcast_to([P, 2, D]), ALU.add)
                steps.link(ins)
                steps.link(dve.tensor_reduce(neg_max[:], logits[:], AX.X, ALU.max))
                dve.tensor_scalar(neg_max[:], neg_max[:], -1.0, None, ALU.mult).then_inc(max_ready, 1)
                for s in tiles:
                    dve.wait_ge(exped, QT * b + s + 1)
                    ins = dve.max(top[:, s, :], probs[:, s, :])
                steps.link(ins)
                for s in tiles:
                    ins = dve.max_index(top_i[:, s, :], top[:, s, :], probs[:, s, :])
                steps.link(ins)
                steps.link(dve.tensor_scalar(e_i[:], top_i[:, :, 0], E - 1, None, ALU.bitwise_and))
                steps.link(dve.tensor_copy(e_f[:], e_i[:]))
                dve.tensor_tensor(hot[:], iota_e[:].unsqueeze(1).broadcast_to([P, QT, E]),
                                  e_f[:].unsqueeze(2).broadcast_to([P, QT, E]), ALU.is_equal).then_inc(hot_ready, 1)
                steps.link(dve.reciprocal(weight[:], total[:]))
                steps.link(dve.tensor_scalar(weight[:], weight[:], tanh_g[:, 1:2], None, ALU.mult))
                dve.wait_ge(hot_ready, b + 1)
                if b:
                    dve.wait_ge(stored, 16 * b)
                for s in tiles:
                    for e in range(E):
                        dve.wait_ge(ex_full, 4 * (QT * b + s) + e // 2 + 1)
                        if e:
                            dve.wait_ge(ex_read, E * (QT * b + s) + e)
                            ins = dve.scalar_tensor_tensor(acc[:, s, :], ex[e // 2][:, e % 2, :], hot[:, s, e:e + 1],
                                                           acc[:, s, :], ALU.mult, ALU.add)
                        else:
                            ins = dve.tensor_scalar(acc[:, s, :], ex[0][:, 0, :], hot[:, s, 0:1], None, ALU.mult)
                        ins.then_inc(ex_read, 1)
                    dve.wait_ge(ex_read, E * (QT * b + s) + E)
                    dve.wait_ge(be_moved, 2 * b + s // 2 + 1)
                    steps.link(dve.tensor_tensor(acc[:, s, :], acc[:, s, :], be_rows[:, s, :], ALU.add))
                    steps.link(dve.tensor_scalar(acc[:, s, :], acc[:, s, :], 0.0, weight[:, s:s + 1], ALU.max, ALU.mult))
                    ins = dve.tensor_tensor(res[:, s, :], acc[:, s, :], xin[:, b, s, :], ALU.add)
                    if b + 1 < B and s < QT - 1:
                        (residual, normalise, rows_low)[s](b + 1)
                ins.then_inc(res_ready, 1)


INPUTS = ["x", "ctx_1024", "mask_Bx1xSxS2_ik1", "mask_BxS2_bf1", "g_xattn", "g_ffn",
          "L0_xattn_wq", "L0_xattn_bq", "L0_xattn_wk", "L0_xattn_bk", "L0_xattn_wv", "L0_xattn_bv", "L0_xattn_wo",
          "L0_xattn_bo", "L0_ffn_expert_tokens", "L0_ffn_W1", "L0_ffn_b1", "L0_ffn_W2", "L0_ffn_b2", "L0_ffn_W3",
          "L0_ffn_b3", "L1_xattn_gamma", "L1_xattn_w_q", "L1_xattn_w_kv", "L1_xattn_null_kv", "L1_xattn_w_out",
          "L1_xattn_out_gamma", "L1_ffn_Wg", "L1_ffn_bg", "L1_ffn_We", "L1_ffn_be"]


def build(nc, a, out):
    def scratch(name, shape, dt=F32):
        return nc.dram_tensor(name, shape, dt).ap()

    k0s, v0s = scratch("k0s", (2, B, D, CTX)), scratch("v0s", (B, CTX, D))
    k1s, v1s = scratch("k1s", (2, B, I1, CTX)), scratch("v1s", (B, CTX, I1))
    bias0, bias1 = scratch("bias0", (B, S, CTX), BF16), scratch("bias1", (B, CTX), BF16)
    q0s, q1s = scratch("q0s", (2, B, D, S)), scratch("q1s", (2, B, I1, S))
    o0s, o1s = scratch("o0s", (B, 2, D, S)), scratch("o1s", (B, 2, I1, S))
    x1s, x2s = scratch("x1s", (B, S, D)), scratch("x2s", (B, S, D))
    xgs, ys = scratch("xgs", (SLOTS, D)), scratch("ys", (SLOTS, D))
    pos_s, tile_s = scratch("pos_s", (P, TOP, NB), I32), scratch("tile_s", (1, J + 2), I32)
    bias_s, null_s = scratch("bias_s", (E, P, BW)), scratch("null_s", (B, P, H1, QT))

    stage_context(nc, a["ctx_1024"], a["L0_xattn_wk"], a["L0_xattn_bk"], a["L0_xattn_wv"], a["L0_xattn_bv"],
                  a["L1_xattn_w_kv"], a["mask_Bx1xSxS2_ik1"].rearrange("b a q k -> (b a) q k"), a["mask_BxS2_bf1"],
                  a["x"], a["L0_xattn_wq"], a["L0_xattn_bq"], k0s, v0s, k1s, v1s, bias0, bias1, q0s)
    stage_attention(nc, "a0", H0, D0, q0s, k0s, v0s, o0s, bias0, clear=xgs)
    stage_route(nc, a["x"], o0s, a["L0_xattn_wo"], a["L0_xattn_bo"], a["g_xattn"], a["L0_ffn_expert_tokens"],
                a["L0_ffn_b1"], a["L0_ffn_b2"], a["L0_ffn_b3"], x1s, xgs, pos_s, tile_s, bias_s)
    stage_experts(nc, xgs, tile_s, bias_s, a["L0_ffn_W1"], a["L0_ffn_W2"], a["L0_ffn_W3"], ys)
    stage_gather(nc, x1s, ys, pos_s, a["g_ffn"], a["L1_xattn_gamma"], a["L1_xattn_w_q"], a["L1_xattn_null_kv"],
                 x2s, q1s, null_s)
    stage_attention(nc, "a1", H1, D1, q1s, k1s, v1s, o1s, bias1, null_s, a["L1_xattn_null_kv"])
    stage_final(nc, x2s, o1s, a["L1_xattn_w_out"], a["L1_xattn_out_gamma"], a["g_xattn"], a["g_ffn"],
                a["L1_ffn_Wg"], a["L1_ffn_bg"], a["L1_ffn_We"], a["L1_ffn_be"], out)


def kernel(**inputs):
    import numpy as _np
    import concourse.bacc as _bacc
    from concourse import mybir as _mybir
    from concourse.bass_utils import run_bass_kernel_spmd as _run

    nc = _bacc.Bacc("TRN2", target_bir_lowering=False, num_devices=1)
    arrays, args = {}, {}
    for name in INPUTS:
        a = _np.ascontiguousarray(inputs[name])
        if a.dtype == bool:
            a = a.view(_np.uint8)
        arrays[f"in_{name}_dram"] = a
        args[name] = nc.dram_tensor(f"in_{name}_dram", a.shape, _mybir.dt.from_np(a.dtype), kind="ExternalInput").ap()
    out = nc.dram_tensor("out_0_dram", (B, S, D), F32, kind="ExternalOutput").ap()
    build(nc, args, out)
    r = _run(nc, [arrays], core_ids=[0])
    return r.results[0]["out_0_dram"]
```
